# Optimizing a Trainium2 kernel written in Bass

```python
import numpy as np
import jax
import jax.numpy as jnp

def _softmax(x, axis=-1):
    return jax.nn.softmax(x, axis=axis)

def _gelu(x):
    return jax.nn.gelu(x, approximate=True)

def _silu(x):
    return jax.nn.silu(x)

def _sigmoid(x):
    return jax.nn.sigmoid(x)

def _layernorm(x, axis=-1, eps=1e-05):
    m = jnp.mean(x, axis=axis, keepdims=True)
    v = jnp.var(x, axis=axis, keepdims=True)
    return (x - m) / jnp.sqrt(v + eps)

def _scatter_add(tgt, idx, src, axis=0):
    return tgt.at[idx].add(src)

def _segment_sum(src, seg, n):
    return jax.ops.segment_sum(src, seg, n)
kernel_name = 'mk_conv_attn_hybrid_d2_conv_nchw2048_r4_cdaf0f'

def setup_inputs(seed: int=0):
    np.random.seed(seed)
    _w = jnp.asarray

    def _rec_inputs():
        import jax
        import jax.numpy as jnp
        _gk = jax.random.key(seed)
        x = -7.109e-05 + 0.9999 * jax.random.normal(jax.random.fold_in(_gk, 1), (8, 512, 16, 16), jnp.float32)
        return x
    x = _rec_inputs()

    def _L0_conv_setup():
        import jax, jax.numpy as jnp
        import numpy as np
        BN_EPS = 1e-05
        key = jax.random.key(seed)
        k1, k2 = jax.random.split(key)
        B, C, H, W = (8, 512, 16, 16)
        x = jax.random.normal(k1, (B, C, H, W), dtype=jnp.float32)
        cfc_w = jax.random.normal(k2, (C, 3), dtype=jnp.float32) * 0.1
        bn_w = jnp.ones((C,), dtype=jnp.float32)
        bn_b = jnp.zeros((C,), dtype=jnp.float32)
        return {'x': x, 'cfc_w': cfc_w, 'bn_w': bn_w, 'bn_b': bn_b}
    _L0_conv_all = _L0_conv_setup()
    _L0_conv_in = {k: v for k, v in _L0_conv_all.items() if k in ('cfc_w', 'bn_w', 'bn_b')}
    del _L0_conv_all

    def _L1_attn_setup():
        import jax, jax.numpy as jnp
        import numpy as np
        H = 16
        D = 32
        SOFTCAP = 30.0
        WINDOW = 256
        SCALE = 1.0 / np.sqrt(D)

        def _attention(x, w_q, w_k, w_v, w_o):
            B, S, hid = x.shape
            q = (x @ w_q.T).reshape(B, S, H, D).transpose(0, 2, 1, 3)
            k = (x @ w_k.T).reshape(B, S, H, D).transpose(0, 2, 1, 3)
            v = (x @ w_v.T).reshape(B, S, H, D).transpose(0, 2, 1, 3)
            scores = jnp.einsum('bhsd,bhtd->bhst', q, k) * SCALE
            scores = SOFTCAP * jnp.tanh(scores / SOFTCAP)
            i = jnp.arange(S)[:, None]
            j = jnp.arange(S)[None, :]
            mask = (j <= i) & (i - j < WINDOW)
            scores = jnp.where(mask, scores, jnp.float32(-1e+30))
            probs = jax.nn.softmax(scores, axis=-1)
            attn = jnp.einsum('bhst,bhtd->bhsd', probs, v)
            attn = attn.transpose(0, 2, 1, 3).reshape(B, S, hid)
            return attn @ w_o.T
        key = jax.random.key(seed)
        ks = jax.random.split(key, 5)
        hid = H * D
        x = jax.random.normal(ks[0], (1, 512, hid), dtype=jnp.float32)
        s = 1.0 / np.sqrt(hid)
        w_q = jax.random.normal(ks[1], (hid, hid), dtype=jnp.float32) * s
        w_k = jax.random.normal(ks[2], (hid, hid), dtype=jnp.float32) * s
        w_v = jax.random.normal(ks[3], (hid, hid), dtype=jnp.float32) * s
        w_o = jax.random.normal(ks[4], (hid, hid), dtype=jnp.float32) * s
        return {'x': x, 'w_q': w_q, 'w_k': w_k, 'w_v': w_v, 'w_o': w_o}
    _L1_attn_all = _L1_attn_setup()
    _L1_attn_in = {k: v for k, v in _L1_attn_all.items() if k in ('w_q', 'w_k', 'w_v', 'w_o')}
    del _L1_attn_all

    def _L1_ffn_setup():
        import jax, jax.numpy as jnp
        import numpy as np
        B, S, H = (1, 512, 512)
        E, K, I = (8, 2, 256)
        IS = 2 * I
        key = jax.random.key(seed)
        ks = jax.random.split(key, 8)
        w = 0.02
        return {'x': jax.random.normal(ks[0], (B, S, H), jnp.float32), 'gate_w': jax.random.normal(ks[1], (E, H), jnp.float32) * w, 'wg': jax.random.normal(ks[2], (E, H, I), jnp.float32) * w, 'wu': jax.random.normal(ks[3], (E, H, I), jnp.float32) * w, 'wd': jax.random.normal(ks[4], (E, I, H), jnp.float32) * w, 'sg': jax.random.normal(ks[5], (H, IS), jnp.float32) * w, 'su': jax.random.normal(ks[6], (H, IS), jnp.float32) * w, 'sd': jax.random.normal(ks[7], (IS, H), jnp.float32) * w}
    _L1_ffn_all = _L1_ffn_setup()
    _L1_ffn_in = {k: v for k, v in _L1_ffn_all.items() if k in ('gate_w', 'wg', 'wu', 'wd', 'sg', 'su', 'sd')}
    del _L1_ffn_all
    return {'x': x, 'L0_conv_cfc_w': _L0_conv_in['cfc_w'], 'L0_conv_bn_w': _L0_conv_in['bn_w'], 'L0_conv_bn_b': _L0_conv_in['bn_b'], 'L1_attn_w_q': _L1_attn_in['w_q'], 'L1_attn_w_k': _L1_attn_in['w_k'], 'L1_attn_w_v': _L1_attn_in['w_v'], 'L1_attn_w_o': _L1_attn_in['w_o'], 'L1_ffn_gate_w': _L1_ffn_in['gate_w'], 'L1_ffn_wg': _L1_ffn_in['wg'], 'L1_ffn_wu': _L1_ffn_in['wu'], 'L1_ffn_wd': _L1_ffn_in['wd'], 'L1_ffn_sg': _L1_ffn_in['sg'], 'L1_ffn_su': _L1_ffn_in['su'], 'L1_ffn_sd': _L1_ffn_in['sd']}

def reference(x, L0_conv_cfc_w, L0_conv_bn_w, L0_conv_bn_b, L1_attn_w_q, L1_attn_w_k, L1_attn_w_v, L1_attn_w_o, L1_ffn_gate_w, L1_ffn_wg, L1_ffn_wu, L1_ffn_wd, L1_ffn_sg, L1_ffn_su, L1_ffn_sd):
    import jax
    import jax.numpy as jnp

    def _L0_conv_ref(x, cfc_w, bn_w, bn_b):
        import jax, jax.numpy as jnp
        import numpy as np
        BN_EPS = 1e-05
        b, c, h, w = x.shape
        xf = x.reshape(b, c, h * w)
        mean = jnp.mean(xf, axis=-1)
        mx = jnp.max(xf, axis=-1)
        std = jnp.std(xf, axis=-1, ddof=1)
        u = jnp.stack([mean, mx, std], axis=-1)
        med = jnp.median(u.reshape(b, -1), axis=-1)[:, None, None]
        u = jax.lax.stop_gradient((u - med) ** 3)
        z = jnp.einsum('bck,ck->bc', u, cfc_w)
        z = z / jnp.sqrt(jnp.float32(1.0) + BN_EPS) * bn_w + bn_b
        g = jax.nn.sigmoid(z)
        return x * g[:, :, None, None]

    def _L1_attn_ref(x, w_q, w_k, w_v, w_o):
        import jax, jax.numpy as jnp
        import numpy as np
        H = 16
        D = 32
        SOFTCAP = 30.0
        WINDOW = 256
        SCALE = 1.0 / np.sqrt(D)

        def _attention(x, w_q, w_k, w_v, w_o):
            B, S, hid = x.shape
            q = (x @ w_q.T).reshape(B, S, H, D).transpose(0, 2, 1, 3)
            k = (x @ w_k.T).reshape(B, S, H, D).transpose(0, 2, 1, 3)
            v = (x @ w_v.T).reshape(B, S, H, D).transpose(0, 2, 1, 3)
            scores = jnp.einsum('bhsd,bhtd->bhst', q, k) * SCALE
            scores = SOFTCAP * jnp.tanh(scores / SOFTCAP)
            i = jnp.arange(S)[:, None]
            j = jnp.arange(S)[None, :]
            mask = (j <= i) & (i - j < WINDOW)
            scores = jnp.where(mask, scores, jnp.float32(-1e+30))
            probs = jax.nn.softmax(scores, axis=-1)
            attn = jnp.einsum('bhst,bhtd->bhsd', probs, v)
            attn = attn.transpose(0, 2, 1, 3).reshape(B, S, hid)
            return attn @ w_o.T
        return _attention(x, w_q, w_k, w_v, w_o)

    def _L1_ffn_ref(x, gate_w, wg, wu, wd, sg, su, sd):
        import jax, jax.numpy as jnp
        import numpy as np
        B, S, H = (1, 512, 512)
        E, K, I = (8, 2, 256)
        IS = 2 * I
        b, s, h = x.shape
        xf = x.reshape(-1, h)
        T = xf.shape[0]
        scores = jax.nn.softmax(jnp.einsum('th,eh->te', xf, gate_w), axis=-1)
        topk_w, topk_i = jax.lax.top_k(scores, K)
        topk_w = topk_w / jnp.sum(topk_w, axis=-1, keepdims=True)
        cw = jnp.zeros_like(scores).at[jnp.arange(T)[:, None], topk_i].add(topk_w)
        g = jnp.einsum('th,ehi->eti', xf, wg)
        u = jnp.einsum('th,ehi->eti', xf, wu)
        hgated = jax.nn.silu(g) * u
        eo = jnp.einsum('eti,eih->eth', hgated, wd)
        y = jnp.einsum('te,eth->th', cw, eo)
        shared = jax.nn.silu(xf @ sg) * (xf @ su) @ sd
        return (y + shared).reshape(b, s, h)

    def _gn(v, G=32, eps=1e-05):
        B_, C_, H_, W_ = v.shape
        g = v.reshape(B_, G, C_ // G, H_, W_)
        m = jnp.mean(g, axis=(2, 3, 4), keepdims=True)
        s = jnp.var(g, axis=(2, 3, 4), keepdims=True)
        return ((g - m) / jnp.sqrt(s + eps)).reshape(v.shape)

    def _ln_c(v, eps=1e-06):
        m = jnp.mean(v, axis=1, keepdims=True)
        s = jnp.var(v, axis=1, keepdims=True)
        return (v - m) / jnp.sqrt(s + eps)

    def _ln_t(v, eps=1e-05):
        m = jnp.mean(v, axis=-1, keepdims=True)
        s = jnp.var(v, axis=-1, keepdims=True)
        return (v - m) / jnp.sqrt(s + eps)

    def _to_tokens(v):
        B_, C_, H_, W_ = v.shape
        return v.reshape(B_, C_, H_ * W_).transpose(0, 2, 1)

    def _from_tokens(t, like):
        B_, C_, H_, W_ = like.shape
        return t.transpose(0, 2, 1).reshape(B_, C_, H_, W_)
    x = x + _L0_conv_ref(_gn(x), L0_conv_cfc_w, L0_conv_bn_w, L0_conv_bn_b)
    t = _to_tokens(x)
    t = t + _L1_attn_ref(_ln_t(t), L1_attn_w_q, L1_attn_w_k, L1_attn_w_v, L1_attn_w_o)
    t = t + _L1_ffn_ref(_ln_t(t), L1_ffn_gate_w, L1_ffn_wg, L1_ffn_wu, L1_ffn_wd, L1_ffn_sg, L1_ffn_su, L1_ffn_sd)
    x = _from_tokens(t, x)
    return x

_drawn_inputs = setup_inputs


def setup_inputs(seed=0):
    import zlib

    import numpy as np

    out = dict(_drawn_inputs(seed))
    spreads = {'L0_conv_bn_w': (1.0, 0.6), 'L0_conv_bn_b': (0.0, 0.522)}
    factors = {'L1_ffn_gate_w': 4.033, 'L1_ffn_wg': 3.517, 'L1_ffn_wu': 3.45, 'L1_ffn_wd': 3.45}
    for name, (base, spread) in spreads.items():
        noise = np.random.default_rng([zlib.crc32(name.encode()), seed]).standard_normal(out[name].shape)
        drawn = base * np.exp(spread * noise) if base else spread * noise
        out[name] = jnp.asarray(drawn.astype(out[name].dtype))
    for name, factor in factors.items():
        out[name] = (out[name] * factor).astype(out[name].dtype)
    return out
```

```python
from contextlib import ExitStack

import numpy as np
import concourse.bass as bass
from concourse import mybir

B, C, S = 8, 512, 256
NH, D = 16, 32
E, I = 8, 256
IS = 512
P = 128
CB = C // P
TT = S // P
NT = B * TT
GN_CH = C // 32
UK = 3
UP = CB * UK
MED_N = C * UK
ROUNDS = 17
RANGE = 256.0
NPAIR = NH // 2
HC = P // D
NTILES = (2 * B * S + E * (P - 1)) // P
BIG = 1e9
SOFTCAP = 30.0
EPS = 1e-5

fp32 = mybir.dt.float32
fp32r = mybir.dt.float32r
fp16 = mybir.dt.float16
i32 = mybir.dt.int32
u32 = mybir.dt.uint32
ALU = mybir.AluOpType
ACT = mybir.ActivationFunctionType
AX = mybir.AxisListType

FRONT_ONLY = ["YT0", "YT1", "XN0", "XN1", "Q0", "K0", "Q1", "K1", "V0", "V1"]
STEP_FIRST = ["YT0", "YT1", "XN0", "XN1", "Q0", "K0", "Q1", "K1", "V0", "V1", "OP0", "OP1"]
STEP_MID = ["YT0", "YT1", "X2T0", "X2T1", "GT", "XN0", "XN1", "Q0", "K0", "Q1", "K1", "V0", "V1", "OP0", "OP1"]
STEP_LAST = ["X2T0", "X2T1", "GT", "OP0", "OP1"]
TAIL = ["X2T0", "X2T1", "GT"]
RING = 3


def ring(part, item, b):
    order, first, per = {
        "front": (FRONT_ONLY, 0, 0),
        "first": (STEP_FIRST, len(FRONT_ONLY), 0),
        "mid": (STEP_MID, len(FRONT_ONLY) + len(STEP_FIRST), len(STEP_MID) // RING),
        "last": (STEP_LAST, len(FRONT_ONLY) + len(STEP_FIRST) + (B - 2) * len(STEP_MID), 0),
        "tail": (TAIL, len(FRONT_ONLY) + len(STEP_FIRST) + (B - 2) * len(STEP_MID) + len(STEP_LAST), 0),
    }[part]
    n = first + order.index(item)
    return n % RING, n // RING + ((b - 1) * per if per else 0)


class Steps:

    def __init__(self):
        self.n = 0
        self.base = 0

    def up(self):
        self.n += 1
        return self.value()

    def value(self):
        return self.n + self.base

    def enter(self, turn, per):
        self.start, self.per = self.n, per
        self.base = turn * per

    def leave(self, turns):
        assert self.n - self.start == self.per, (self.n - self.start, self.per)
        self.n += (turns - 1) * self.per
        self.base = 0



def layer_kernel(nc, x, params, wqkvo, gate, ws, wgu, wd, out):
    ctx = ExitStack()
    with ctx:
        def sb(name, shape, dt=fp32, scope=ctx):
            return scope.enter_context(nc.sbuf_tensor(name, shape, dt))

        x2_rows = nc.dram_tensor("x2_rows", [B * S, C], fp32, kind="Internal").ap()
        x2_cols = nc.dram_tensor("x2_cols", [B * P, CB * S], fp32, kind="Internal").ap()
        y_slots = nc.dram_tensor("y_slots", [NTILES * P, C], fp32, kind="Internal").ap()

        T = sb("T", [P, B, CB * S])
        ident = sb("ident", [P, P])
        ones = sb("ones", [P, P])
        before = sb("before", [P, P])
        iota_f = sb("iota_f", [P, P])
        token_f = sb("token_f", [P, 2 * NT])
        maxes = sb("maxes", [P, NT, 8])
        topi = sb("topi", [P, NT, 8])
        w12 = sb("w12", [P, 2, NT])
        slots = sb("slots", [P, 2 * NT], u32)
        ids = sb("ids", [P, NTILES], u32)
        tile_expert = sb("tile_expert", [1, NTILES], u32)

        a_scope = ExitStack()
        sw_h = sb("sw_h", [P, 3, CB * C], fp32r, a_scope)
        sw_l = sb("sw_l", [P, 3, CB * C], fp32r, a_scope)
        w_h = sb("w_h", [P, 4, CB * C], fp32r, a_scope)
        w_l = sb("w_l", [P, 4, CB * C], fp32r, a_scope)
        front = sb("front", [P, CB * S], fp32, a_scope)
        x2 = sb("x2", [P, TT * C], fp32, a_scope)
        xt_h = sb("xt_h", [P, CB, S], fp32r, a_scope)
        xt_l = sb("xt_l", [P, CB, S], fp32r, a_scope)
        qT = sb("qT", [P, CB, S], fp32, a_scope)
        kT = sb("kT", [P, CB, S], fp32, a_scope)
        v = sb("v", [P, TT, C], fp32, a_scope)
        probs = sb("probs", [P, 4, 2 * 384], fp32, a_scope)
        rden = sb("rden", [P, S], fp32, a_scope)
        att = sb("att", [P, S], fp32, a_scope)
        att_h = sb("att_h", [P, CB, S], fp32r, a_scope)
        att_l = sb("att_l", [P, CB, S], fp32r, a_scope)
        x2T = sb("x2T", [P, CB * S], fp32, a_scope)
        gate_sb = sb("gate_sb", [P, CB, E], fp32, a_scope)
        lg = sb("lg", [P, TT * E], fp32, a_scope)
        top8 = sb("top8", [P, TT, 8], fp32, a_scope)
        idx8 = sb("idx8", [P, TT, 8], u32, a_scope)
        mean_var = sb("mean_var", [P, TT, 2], fp32, a_scope)
        bn6 = sb("bn6", [P, TT, 6], fp32, a_scope)
        var_eps = sb("var_eps", [P, TT], fp32, a_scope)
        rstd = sb("rstd", [P, TT], fp32, a_scope)
        powers = sb("powers", [P, 2 * B * CB], fp32, a_scope)
        prm = sb("prm", [P, CB * UK + 2 * CB], fp32, a_scope)
        coefA = sb("coefA", [P, B * CB], fp32, a_scope)
        coefB = sb("coefB", [P, B * CB], fp32, a_scope)
        col = sb("col", [B * UP, 12], fp32, a_scope)
        row = sb("row", [1, 8, B * UP], fp32, a_scope)
        g_avg = sb("g_avg", [P, P], fp32, a_scope)
        g_med = sb("g_med", [B * UP, B * UP], fp32, a_scope)

        qf = qT[:, :, :].rearrange("p c s -> p (c s)")
        kf = kT[:, :, :].rearrange("p c s -> p (c s)")
        vf = v[:, :, :].rearrange("p t c -> p (t c)")
        n32 = B * CB
        bst = qf[:, 0:6 * n32].rearrange("p (n k) -> p n k", k=6)
        chmax = qf[:, 6 * n32:7 * n32]
        small = kf[:, 0:16 * n32].rearrange("p (k n) -> p k n", n=n32)
        pw_in = kf[:, 16 * n32:18 * n32]
        pw_out = kf[:, 18 * n32:20 * n32]
        u = vf[:, 0:B * UP]
        uw = vf[:, B * UP:4 * B * UP].rearrange("p (k n) -> p k n", k=3)
        uT = vf[0:B * UP, 4 * B * UP:4 * B * UP + P]
        junk = vf[0:B * UP, 4 * B * UP + P:4 * B * UP + 4 * P].rearrange("p (k n) -> p k n", k=3)
        iota_i = qf[:, 512:512 + P].bitcast(i32)
        token_i = qf[:, 768:768 + 2 * NT].bitcast(i32)
        stage = probs[:, :, :].rearrange("p a n -> p (a n)").rearrange("p (k n) -> p k n", n=1024)
        a_scope.close()

        wd_sb = sb("wd_sb", [P, E, (I // P) * C])
        xgT = sb("xgT", [P, C])
        es = sb("es", [P, I])
        eh = sb("eh", [P, I])
        ehT = sb("ehT", [P, I])
        yo = sb("yo", [P, 3, C])
        sw_words = 2 * 3 * CB * C
        sb("gap", [P, sw_words - (E * (I // P) * C + C + 3 * I + 3 * C)])
        wgu_sb = sb("wgu_sb", [P, E, CB * 2 * I])
        xg = sb("xg", [P, 3, C])
        b_scope = ExitStack()
        xc = sb("xc", [P, CB * S], fp32, b_scope)
        xb_h = sb("xb_h", [P, CB, S], fp32r, b_scope)
        xb_l = sb("xb_l", [P, CB, S], fp32r, b_scope)
        sg = sb("sg", [P, 2, S], fp32, b_scope)
        hf = sb("hf", [P, 2, S], fp32, b_scope)
        hh = sb("hh", [P, CB, S], fp32r, b_scope)
        hl = sb("hl", [P, CB, S], fp32r, b_scope)
        picked = sb("picked", [P, 2, NT, E], fp32, b_scope)
        chosen = sb("chosen", [P, NT, E], fp32, b_scope)
        r4 = sb("r4", [P, 4, NT, E], fp32, b_scope)
        masked = sb("masked", [P, 2 * NT, E], fp32, b_scope)
        cmp = sb("cmp", [P, E, NT], fp32, b_scope)
        cmp8 = sb("cmp8", [P, 2, E, E], fp32, b_scope)
        s8 = sb("s8", [P, 4, E], fp32, b_scope)
        te = sb("te", [1, NTILES, E], fp32, b_scope)
        te_f = sb("te_f", [1, NTILES], fp32, b_scope)
        ex = sb("ex", [P, 4, NT], fp32, b_scope)
        slot_f = sb("slot_f", [P, 3, 2 * NT], fp32, b_scope)
        slot_i = sb("slot_i", [P, 3, 2 * NT], i32, b_scope)
        oh_lo = sb("oh_lo", [P, 2 * NT, P], fp16, b_scope)
        oh_hi = sb("oh_hi", [P, 2 * NT, 40], fp16, b_scope)
        b_scope.close()
        y12 = sb("y12", [P, 4, 2, C])
        fin = sb("fin", [P, 4, 2, C])

        scores = ctx.enter_context(nc.psum_tensor("scores", [P, 4, 512], fp32))
        PS = [scores[:, i, :] for i in range(4)]
        PS += [ctx.enter_context(nc.psum_tensor(f"PS{i}", [P, 512], fp32))[:, :] for i in range(4, 8)]
        score_bank, od_bank, ring_bank = PS[0:4], PS[4], PS[5:8]
        gu_bank, dn_bank = PS[0:2], PS[2:4]
        route_bank, ids_bank = PS[4], PS[5]
        egu_bank, ey_bank, xT_bank, hT_bank = PS[0], PS[2], PS[6], PS[7]

        def sem(name):
            return ctx.enter_context(nc.semaphore(name))

        wait_carrier = sem("wait_carrier")
        x_loaded = [sem(f"x_loaded{b}") for b in range(B)]
        prm_loaded, gate_loaded = sem("prm_loaded"), sem("gate_loaded")
        stage_loaded = [sem(f"stage_loaded{k}") for k in range(3)]
        whi_done, wlo_done = sem("whi_done"), sem("wlo_done")
        fills_done, consts_done = sem("fills_done"), sem("consts_done")
        dve_step, pool_step, act_step = sem("dve_step"), sem("pool_step"), sem("act_step")
        chmean_ready, grpmean_ready, chvar_ready, grpvar_ready = (
            sem("chmean_ready"), sem("grpmean_ready"), sem("chvar_ready"), sem("grpvar_ready"))
        powin_ready, pow_ready = sem("powin_ready"), sem("pow_ready")
        u_ready, uT_full = sem("u_ready"), sem("uT_full")
        counts_ready, counts_summed = sem("counts_ready"), sem("counts_summed")
        med_in, med_out = sem("med_in"), sem("med_out")
        z_ready, ez_ready = sem("z_ready"), sem("ez_ready")
        y_ready, t_ready = sem("y_ready"), sem("t_ready")
        var1_ready, rstd1_ready, var2_ready, rstd2_ready = (
            sem("var1_ready"), sem("rstd1_ready"), sem("var2_ready"), sem("rstd2_ready"))
        xn_ready, xt_h_done, x2_ready = sem("xn_ready"), sem("xt_h_done"), sem("x2_ready")
        ring_full = [sem(f"ring_full{k}") for k in range(RING)]
        ring_free = [sem(f"ring_free{k}") for k in range(RING)]
        scores_full, tanh_done, exp_done, mask_done = (
            sem("scores_full"), sem("tanh_done"), sem("exp_done"), sem("mask_done"))
        pv_done, att_ready, att_h_done, att_l_done = (
            sem("pv_done"), sem("att_ready"), sem("att_h_done"), sem("att_l_done"))
        x2_stored, x2T_stored = sem("x2_stored"), sem("x2T_stored")
        attention_over = sem("attention_over")
        wgu_loaded, wd_loaded = sem("wgu_loaded"), sem("wd_loaded")
        xc_loaded, xb_h_done, xb_l_done = sem("xc_loaded"), sem("xb_h_done"), sem("xb_l_done")
        gu_full, silu_done, h_done, hh_done, hl_done = (
            sem("gu_full"), sem("silu_done"), sem("h_done"), sem("hh_done"), sem("hl_done"))
        dn_full, dn_free = sem("dn_full"), sem("dn_free")
        chosen_ready, prefix_full, gap_exp = (
            sem("chosen_ready"), sem("prefix_full"), sem("gap_exp"))
        onehot_ready, ids_full, ids_ready, experts_ready = (
            sem("onehot_ready"), sem("ids_full"), sem("ids_ready"), sem("experts_ready"))
        xg_loaded = [sem(f"xg_loaded{k}") for k in range(3)]
        xT_full, xT_ready, egu_full, esilu_done, eh_ready = (
            sem("xT_full"), sem("xT_ready"), sem("egu_full"), sem("esilu_done"), sem("eh_ready"))
        hT_full, hT_ready, ey_full, yo_ready = (
            sem("hT_full"), sem("hT_ready"), sem("ey_full"), sem("yo_ready"))
        yo_stored = [sem(f"yo_stored{k}") for k in range(3)]
        y12_loaded = [sem(f"y12_loaded{k}") for k in range(4)]
        fin_ready = sem("fin_ready")
        out_stored = [sem(f"out_stored{k}") for k in range(4)]

        def at(t, b):
            return t[:, bass.ds(b, 1), :].rearrange("p a n -> p (a n)")

        def stand_alone(eng):
            eng.sem_inc(wait_carrier, 1)

        def tile_at(b, tt):
            return at(T, b)[:, tt * C:(tt + 1) * C]

        def filled(part, item, s):
            k, used = ring(part, item, s)
            return ring_full[k], used + 1

        def emptied(part, item, s):
            k, used = ring(part, item, s)
            return ring_free[k], used + 1

        NFILLS = 11
        NCONSTS = 8
        NW = 14

        def chunk_of(k, attn, shared):
            t, j = (attn, k) if k < 8 else (shared, k - 8)
            return t[:, j // 2, 1024 * (j % 2):1024 * (j % 2 + 1)]

        block = ctx.enter_context(nc.Block())

        @block.sync
        def _(sp):
            for b in range(B):
                sp.dma_start(at(T, b).rearrange("p (k s) -> p k s", k=CB),
                             x[b].rearrange("(k p) s -> p k s", p=P)).then_inc(x_loaded[b], 16)
            for k in range(NW):
                if k >= 3:
                    sp.wait_ge(wlo_done, k - 2)
                sp.dma_start(stage[:, k % 3, :], chunk_of(k, wqkvo, ws)).then_inc(stage_loaded[k % 3], 16)

            def store_x2(b):
                sp.wait_ge(x2_ready, b + 1)
                sp.dma_start(x2_rows[bass.ds(b * S, S), :].rearrange("(t p) c -> p t c", p=P),
                             x2[:, :].rearrange("p (t c) -> p t c", t=TT)).then_inc(x2_stored, 16)

            def store_x2T(part, b, s):
                sp.wait_ge(*emptied(part, "X2T0", s))
                sp.wait_ge(*emptied(part, "X2T1", s))
                sp.dma_start(x2_cols[bass.ds(b * P, P), :], x2T[:, :]).then_inc(x2T_stored, 16)

            store_x2(0)
            with sp.Fori(1, B - 1) as b:
                store_x2T("mid", b - 1, b)
                store_x2(b)
            store_x2T("last", B - 2, B - 1)
            store_x2(B - 1)
            store_x2T("tail", B - 1, B)

            sp.wait_ge(attention_over, 1)
            sp.wait_ge(x2T_stored, 16 * B)
            sp.wait_ge(x2_stored, 16 * B)
            sp.dma_start(xc[:, :], x2_cols[0:P, :]).then_inc(xc_loaded, 16)
            for e in range(E):
                sp.dma_start(at(wgu_sb, e), at(wgu, e)).then_inc(wgu_loaded, 16)
            with sp.Fori(1, B) as b:
                sp.wait_ge(xc_loaded, 16 * b)
                sp.wait_ge(xb_l_done, b)
                sp.dma_start(xc[:, :], x2_cols[bass.ds(b * P, P), :]).then_inc(xc_loaded, 16)
            sp.wait_ge(dn_full, B)
            for e in range(E):
                sp.dma_start(at(wd_sb, e), at(wd, e)).then_inc(wd_loaded, 16)

            with sp.Fori(0, NTILES // 3) as i:
                for k in range(3):
                    sp.wait_ge(yo_ready, 3 * i + k + 1)
                    sp.dma_start(y_slots[bass.ds((3 * i + k) * P, P), :], yo[:, k, :]).then_inc(yo_stored[k], 16)
            with sp.Fori(0, NT // 4) as i:
                for k in range(4):
                    sp.wait_ge(fin_ready, 4 * i + k + 1)
                    sp.dma_start(out[bass.ds((4 * i + k) * P, P), :], fin[:, k, 1, :]).then_inc(out_stored[k], 16)
            for k in range(4):
                sp.wait_ge(out_stored[k], 16 * (NT // 4))

        @block.gpsimd
        def _(pool):
            pool.wait_ge(fills_done, NFILLS)
            for t, base, pattern, mult, fill, op in (
                (ident[:, :], 0, [[-1, P]], 1, 1.0, ALU.not_equal),
                (before[:, :], -1, [[1, P]], -1, 0.0, ALU.is_ge),
                (g_avg[:, :].rearrange("p (a c) -> p a c", c=GN_CH), 0, [[-GN_CH, 8], [0, GN_CH]], 1, 0.0, ALU.is_ge),
                (g_med[:, :].rearrange("p (a c) -> p a c", c=UP), 0, [[-UP, B], [0, UP]], 1, 0.0, ALU.is_ge),
            ):
                pool.affine_select(out=t, in_=t, compare_op=op, fill=fill, base=base, pattern=pattern,
                                   channel_multiplier=mult).then_inc(consts_done, 1)
            pool.wait_ge(consts_done, 4)
            for t, base, pattern in (
                (g_avg[:, :].rearrange("p (a c) -> p a c", c=GN_CH), GN_CH - 1, [[GN_CH, 8], [0, GN_CH]]),
                (g_med[:, :].rearrange("p (a c) -> p a c", c=UP), UP - 1, [[UP, B], [0, UP]]),
            ):
                pool.affine_select(out=t, in_=t, compare_op=ALU.is_ge, fill=0.0, base=base, pattern=pattern,
                                   channel_multiplier=-1).then_inc(consts_done, 1)
            pool.iota(iota_i, pattern=[[1, P]], base=0, channel_multiplier=0).then_inc(consts_done, 1)
            pool.iota(token_i.rearrange("p (a t) -> p a t", a=2), pattern=[[0, 2], [P, NT]], base=0,
                      channel_multiplier=1).then_inc(consts_done, 1)

            for k in range(NW):
                pool.wait_ge(whi_done, k + 1)
                pool.tensor_tensor(chunk_of(k, w_l, sw_l), stage[:, k % 3, :],
                                   chunk_of(k, w_h, sw_h).bitcast(fp32), ALU.subtract).then_inc(wlo_done, 1)
                if k == 5:
                    pool.wait_ge(powin_ready, 1)
                    pool.tensor_tensor(pw_out, pw_in, powers[:, :], ALU.pow).then_inc(pow_ready, 1)

            def rstd_of(var_ready, rstd_ready, b):
                pool.wait_ge(var_ready, b + 1)
                pool.tensor_tensor(rstd[:, :], var_eps[:, :], powers[:, 0:TT], ALU.pow).then_inc(rstd_ready, 1)

            def mask(b, p):
                pool.wait_ge(exp_done, 8 * b + p + 1)
                stand_alone(pool)
                for a in range(2):
                    t = probs[:, p % 4, :].rearrange("p (h q) -> p h q", h=2)[:, :, 256 * a:256 * a + P]
                    ins = pool.affine_select(out=t, in_=t, compare_op=ALU.is_ge, fill=0.0, base=0,
                                             pattern=[[0, 2], [1, P]], channel_multiplier=-1)
                ins.then_inc(mask_done, 1)

            def att_low(b, c):
                pool.wait_ge(att_h_done, 4 * b + c + 1)
                pool.tensor_tensor(att_l[:, c, :], att[:, :], att_h[:, c, :].bitcast(fp32),
                                   ALU.subtract).then_inc(att_l_done, 1)

            def step(b, has_front):
                if has_front:
                    rstd_of(var1_ready, rstd1_ready, b + 1)
                for p in range(5):
                    mask(b, p)
                att_low(b, 0)
                mask(b, 5)
                mask(b, 6)
                att_low(b, 1)
                mask(b, 7)
                att_low(b, 2)
                att_low(b, 3)
                rstd_of(var2_ready, rstd2_ready, b)

            rstd_of(var1_ready, rstd1_ready, 0)
            step(0, True)
            with pool.Fori(1, B - 1) as b:
                step(b, True)
            step(B - 1, False)

            def hidden_low_of(b):
                for j in range(CB):
                    pool.wait_ge(hh_done, CB * b + j + 1)
                    pool.tensor_tensor(hl[:, j, :], hf[:, j % 2, :], hh[:, j, :].bitcast(fp32),
                                       ALU.subtract).then_inc(hl_done, 1)

            with pool.Fori(0, B) as b:
                hidden_low_of(b)

            pool.wait_ge(ids_ready, 1)
            for t in range(NTILES):
                if t >= 3:
                    pool.wait_ge(xT_full, t - 2)
                pool.indirect_dma_start(xg[:, t % 3, :], None, x2_rows[:, :],
                                        bass.IndirectOffsetOnAxis(ids[:, t:t + 1], 0)).then_inc(xg_loaded[t % 3], 16)
            for k in range(3):
                pool.wait_ge(yo_stored[k], 16 * (NTILES // 3))
            for t in range(NT):
                if t >= 4:
                    pool.wait_ge(fin_ready, t - 3)
                for j in range(2):
                    c = j * NT + t
                    pool.indirect_dma_start(y12[:, t % 4, j, :], None, y_slots[:, :],
                                            bass.IndirectOffsetOnAxis(slots[:, c:c + 1], 0)).then_inc(y12_loaded[t % 4], 16)

        @block.scalar
        def _(act):
            act.dma_start(prm[:, :], params).then_inc(prm_loaded, 16)
            act.dma_start(gate_sb[:, :, :], gate).then_inc(gate_loaded, 16)
            for k in range(NW):
                act.wait_ge(stage_loaded[k % 3], 16 * (k // 3 + 1))
                act.activation(chunk_of(k, w_h, sw_h), stage[:, k % 3, :], ACT.Copy).then_inc(whi_done, 1)
            act.wait_ge(z_ready, 1)
            act.activation(small[:, 15, :], small[:, 14, :], ACT.Exp, scale=-1.0).then_inc(ez_ready, 1)

            def tokens(part, b, s):
                for tt in range(TT):
                    act.wait_ge(*filled(part, f"YT{tt}", s))
                    k, _ = ring(part, f"YT{tt}", s)
                    act.activation(tile_at(b, tt), ring_bank[k], ACT.Copy).then_inc(ring_free[k], 1)

            def xt_high(part, s):
                for h in range(2):
                    act.wait_ge(*filled(part, f"XN{h}", s))
                    k, _ = ring(part, f"XN{h}", s)
                    act.activation(xt_h[:, 2 * h:2 * h + 2, :].rearrange("p c s -> p (c s)"), ring_bank[k],
                                   ACT.Copy).then_inc(xt_h_done, 1)

            def values(part, s):
                for tt in range(TT):
                    act.wait_ge(*filled(part, f"V{tt}", s))
                    k, _ = ring(part, f"V{tt}", s)
                    act.activation(v[:, tt, :], ring_bank[k], ACT.Copy).then_inc(ring_free[k], 1)

            def soft(b, p, first=False):
                act.wait_ge(scores_full, 8 * b + p + 1)
                if not (first and p < 4):
                    act.wait_ge(pv_done, 4 * b + p // 2 - 1)
                act.activation(probs[:, p % 4, :].rearrange("p (h q) -> p h q", h=2),
                               scores[:, 2 * (p % 2):2 * (p % 2) + 2, 0:384], ACT.Tanh,
                               scale=1.0 / (np.sqrt(D) * SOFTCAP)).then_inc(tanh_done, 1)
                act.wait_ge(tanh_done, 8 * b + p + 1)
                act.activation(probs[:, p % 4, :], probs[:, p % 4, :], ACT.Exp, scale=SOFTCAP).then_inc(exp_done, 1)

            def att_high(b, c):
                act.wait_ge(att_ready, 4 * b + c + 1)
                act.activation(att_h[:, c, :], att[:, :], ACT.Copy).then_inc(att_h_done, 1)

            def x2_transposed(part, s):
                for h in range(2):
                    act.wait_ge(*filled(part, f"X2T{h}", s))
                    k, _ = ring(part, f"X2T{h}", s)
                    act.activation(x2T[:, 512 * h:512 * (h + 1)], ring_bank[k], ACT.Copy).then_inc(ring_free[k], 1)

            def step(part, b, has_front, has_back):
                first = isinstance(b, int) and b == 0
                soft(b, 0, first)
                if has_front:
                    tokens(part, b + 1, b)
                soft(b, 1, first)
                if has_back:
                    x2_transposed(part, b)
                soft(b, 2, first)
                soft(b, 3, first)
                if has_front:
                    xt_high(part, b)
                soft(b, 4, first)
                att_high(b, 0)
                soft(b, 5, first)
                soft(b, 6, first)
                att_high(b, 1)
                soft(b, 7, first)
                att_high(b, 2)
                att_high(b, 3)
                if has_front:
                    values(part, b)
                if has_back:
                    act.wait_ge(x2T_stored, 16 * b)

            tokens("front", 0, 0)
            xt_high("front", 0)
            values("front", 0)
            act.wait_ge(wlo_done, NW)
            step("first", 0, True, False)
            with act.Fori(1, B - 1) as b:
                step("mid", b, True, True)
            step("last", B - 1, False, True)
            x2_transposed("tail", B)

            act.wait_ge(attention_over, 1)
            act.activation(ex[:, 1, :], ex[:, 0, :], ACT.Exp).then_inc(gap_exp, 1)

            def shared(b, first=False):
                act.wait_ge(xc_loaded, 16 * (b + 1))
                if not first:
                    act.wait_ge(gu_full, CB * b)
                act.activation(xb_h[:, :, :].rearrange("p c s -> p (c s)"), xc[:, :], ACT.Copy).then_inc(xb_h_done, 1)
                for j in range(CB):
                    act.wait_ge(gu_full, CB * b + j + 1)
                    act.activation(sg[:, j % 2, :], gu_bank[j % 2][:, 0:S], ACT.Silu).then_inc(silu_done, 1)
                    act.wait_ge(h_done, CB * b + j + 1)
                    act.activation(hh[:, j, :], hf[:, j % 2, :], ACT.Copy).then_inc(hh_done, 1)

            shared(0, True)
            with act.Fori(1, B) as b:
                shared(b)

            def x_transposed(t):
                act.wait_ge(xT_full, t + 1)
                act.activation(xgT[:, :], xT_bank, ACT.Copy).then_inc(xT_ready, 1)

            def gated(t):
                act.wait_ge(egu_full, t + 1)
                act.activation(es[:, :], egu_bank[:, 0:I], ACT.Silu).then_inc(esilu_done, 1)

            act.wait_ge(dn_full, B)
            x_transposed(0)
            with act.Fori(0, NTILES - 1) as t:
                gated(t)
                x_transposed(t + 1)
            gated(NTILES - 1)

        @block.vector
        def _(dve):
            n = Steps()

            def fill(t, value):
                dve.memset(t, value).then_inc(fills_done, 1)

            fill(ident[:, :], 0.0)
            fill(before[:, :], 1.0)
            fill(g_avg[:, :], 1.0 / GN_CH)
            fill(g_med[:, :], 1.0)
            fill(ones[:, :], 1.0)
            fill(powers[:, 0:n32], -0.5)
            fill(powers[:, n32:2 * n32], 0.5)
            lo, below = col[:, 0:1], col[:, 1:2]
            thr, jw, cnt = col[:, 2:5], col[:, 5:8], col[:, 8:11]
            fill(lo, -RANGE / 2)
            for j in range(3):
                fill(jw[:, j:j + 1], (j + 1) * RANGE / 4)
            dve.wait_ge(fills_done, NFILLS)

            for b in range(B):
                dve.wait_ge(x_loaded[b], 16)
                xb = at(T, b).rearrange("p (k s) -> p k s", k=CB)
                for k in range(CB):
                    dve.bn_stats(bst[:, CB * b + k, :], xb[:, k, :])
                ins = dve.reduce_max(chmax[:, CB * b:CB * (b + 1)], xb, AX.X)
            ins.then_inc(dve_step, 1)
            dve.wait_ge(dve_step, n.up())

            def step_of(ins):
                ins.then_inc(dve_step, 1)
                return n.up()

            def K(k):
                return small[:, k, :]

            step_of(dve.tensor_tensor(K(0), bst[:, :, 1], bst[:, :, 4], ALU.add))
            step_of(dve.tensor_tensor(K(1), bst[:, :, 1], bst[:, :, 4], ALU.subtract))
            dve.wait_ge(dve_step, step_of(dve.tensor_tensor(K(2), bst[:, :, 2], bst[:, :, 5], ALU.add)))
            dve.tensor_scalar(K(3), K(0), 0.5, None, ALU.mult).then_inc(chmean_ready, 1)
            dve.wait_ge(dve_step, step_of(dve.tensor_tensor(K(4), K(1), K(1), ALU.mult)))
            dve.wait_ge(dve_step, step_of(dve.scalar_tensor_tensor(
                K(5), K(4), S / 4.0, K(2), ALU.mult, ALU.add)))
            dve.wait_ge(grpmean_ready, 1)
            grp_mean = K(6)
            dve.wait_ge(dve_step, step_of(dve.tensor_copy(grp_mean, PS[0][:, 0:n32])))
            dve.wait_ge(dve_step, step_of(dve.tensor_tensor(K(7), K(3), grp_mean, ALU.subtract)))
            dve.wait_ge(dve_step, step_of(dve.tensor_tensor(K(8), K(7), K(7), ALU.mult)))
            dve.scalar_tensor_tensor(K(9), K(5), 1.0 / S, K(8), ALU.mult, ALU.add).then_inc(chvar_ready, 1)
            step_of(dve.tensor_scalar(pw_in[:, n32:2 * n32], K(5), 1.0 / (S - 1), 1e-30, ALU.mult, ALU.max))
            dve.wait_ge(grpvar_ready, 1)
            dve.tensor_scalar(pw_in[:, 0:n32], PS[1][:, 0:n32], EPS, None, ALU.add).then_inc(powin_ready, 1)
            dve.wait_ge(pow_ready, 1)
            r = pw_out[:, 0:n32]
            u3 = u.rearrange("p (n k) -> p n k", k=UK)
            dve.wait_ge(dve_step, step_of(dve.tensor_tensor(K(10), chmax, grp_mean, ALU.subtract)))
            dve.tensor_tensor(u3[:, :, 0], K(7), r, ALU.mult)
            dve.tensor_tensor(u3[:, :, 1], K(10), r, ALU.mult)
            dve.tensor_tensor(u3[:, :, 2], pw_out[:, n32:2 * n32], r, ALU.mult).then_inc(u_ready, 1)

            dve.wait_ge(uT_full, 1)
            dve.wait_ge(dve_step, step_of(dve.tensor_copy(uT, PS[2][0:B * UP, 0:P])))
            with dve.Fori(0, ROUNDS) as i:
                n.enter(i, 6)
                dve.wait_ge(dve_step, step_of(dve.tensor_scalar(thr, jw, lo, None, ALU.add)))
                for j in range(3):
                    ins = dve.tensor_scalar(junk[:, j, :], uT, thr[:, j:j + 1], 0.0, ALU.is_le, ALU.add,
                                            accum_out=cnt[:, j:j + 1])
                    if j < 2:
                        step_of(ins)
                ins.then_inc(counts_ready, 1)
                dve.wait_ge(counts_summed, i + 1)
                dve.wait_ge(dve_step, step_of(dve.tensor_scalar(
                    thr, PS[3][0:B * UP, 0:3], MED_N / 2 - 0.5, 0.0, ALU.is_lt, ALU.add, accum_out=below)))
                dve.wait_ge(dve_step, step_of(dve.scalar_tensor_tensor(
                    lo, below, jw[:, 0:1], lo, ALU.mult, ALU.add)))
                dve.wait_ge(dve_step, step_of(dve.tensor_scalar(jw, jw, 0.25, None, ALU.mult)))
                n.leave(ROUNDS)

            def least(dst, bound):
                dve.wait_ge(dve_step, step_of(dve.tensor_scalar(junk[:, 0, :], uT, bound, BIG, ALU.is_le, ALU.mult)))
                dve.wait_ge(dve_step, step_of(dve.tensor_tensor(junk[:, 1, :], junk[:, 0, :], uT, ALU.add)))
                return dve.tensor_reduce(dst, junk[:, 1, :], AX.X, ALU.min)

            def of_batch(k):
                return row[0:1, k, :].rearrange("p (b n) -> p b n", b=B)

            least(cnt[:, 0:1], lo).then_inc(med_in, 1)
            dve.wait_ge(med_out, 1)
            dve.wait_ge(dve_step, step_of(dve.tensor_reduce(
                row[0:1, 1, 0:B], PS[4][0:1, 0:B * UP].rearrange("p (b n) -> p b n", b=B), AX.X, ALU.min)))
            dve.tensor_copy(of_batch(2), row[0:1, 1, 0:B].unsqueeze(2).to_broadcast([1, B, UP])).then_inc(med_in, 1)
            dve.wait_ge(med_out, 2)
            dve.wait_ge(dve_step, step_of(dve.tensor_copy(thr[:, 0:1], PS[4][0:B * UP, 128:129])))
            dve.tensor_scalar(junk[:, 2, :], uT, thr[:, 0:1], 0.0, ALU.is_le, ALU.add,
                              accum_out=cnt[:, 1:2]).then_inc(med_in, 1)
            least(cnt[:, 2:3], thr[:, 0:1]).then_inc(med_in, 1)
            dve.wait_ge(med_out, 3)
            step_of(dve.tensor_reduce(row[0:1, 3, 0:B], PS[5][0:1, 0:B * UP].rearrange("p (b n) -> p b n", b=B),
                                      AX.X, ALU.add))
            dve.wait_ge(dve_step, step_of(dve.tensor_reduce(
                row[0:1, 4, 0:B], PS[5][0:1, 128:128 + B * UP].rearrange("p (b n) -> p b n", b=B), AX.X, ALU.min)))
            dve.wait_ge(dve_step, step_of(dve.tensor_scalar(
                row[0:1, 5, 0:B], row[0:1, 3, 0:B], MED_N / 2 + 0.5, BIG, ALU.is_lt, ALU.mult)))
            dve.wait_ge(dve_step, step_of(dve.tensor_tensor(
                row[0:1, 5, 0:B], row[0:1, 5, 0:B], row[0:1, 1, 0:B], ALU.add)))
            dve.wait_ge(dve_step, step_of(dve.tensor_tensor(
                row[0:1, 6, 0:B], row[0:1, 5, 0:B], row[0:1, 4, 0:B], ALU.min)))
            dve.wait_ge(dve_step, step_of(dve.tensor_tensor(
                row[0:1, 6, 0:B], row[0:1, 6, 0:B], row[0:1, 1, 0:B], ALU.add)))
            dve.tensor_scalar(row[0:1, 7, 0:B], row[0:1, 6, 0:B], 0.5, None, ALU.mult).then_inc(med_in, 1)

            dve.wait_ge(med_out, 4)
            dve.wait_ge(prm_loaded, 16)
            by_b = "p (b n) -> p b n"
            dve.wait_ge(dve_step, step_of(dve.tensor_tensor(
                uw[:, 0, :].rearrange(by_b, b=B), u.rearrange(by_b, b=B),
                PS[6][:, 0:B].unsqueeze(2).to_broadcast([P, B, UP]), ALU.subtract)))
            dve.wait_ge(dve_step, step_of(dve.tensor_tensor(uw[:, 1, :], uw[:, 0, :], uw[:, 0, :], ALU.mult)))
            dve.wait_ge(dve_step, step_of(dve.tensor_tensor(uw[:, 2, :], uw[:, 1, :], uw[:, 0, :], ALU.mult)))
            dve.wait_ge(dve_step, step_of(dve.tensor_tensor(
                uw[:, 0, :].rearrange(by_b, b=B), uw[:, 2, :].rearrange(by_b, b=B),
                prm[:, 0:UP].unsqueeze(1).to_broadcast([P, B, UP]), ALU.mult)))
            dve.wait_ge(dve_step, step_of(dve.tensor_reduce(
                K(11), uw[:, 0, :].rearrange("p (n k) -> p n k", k=UK), AX.X, ALU.add)))
            bn_scale = float(1.0 / np.sqrt(np.float32(1.0) + np.float32(EPS)))
            dve.wait_ge(dve_step, step_of(dve.scalar_tensor_tensor(
                K(12).rearrange(by_b, b=B), K(11).rearrange(by_b, b=B), bn_scale,
                prm[:, UP:UP + CB].unsqueeze(1).to_broadcast([P, B, CB]), ALU.mult, ALU.mult)))
            dve.tensor_tensor(K(14).rearrange(by_b, b=B), K(12).rearrange(by_b, b=B),
                              prm[:, UP + CB:UP + 2 * CB].unsqueeze(1).to_broadcast([P, B, CB]),
                              ALU.add).then_inc(z_ready, 1)
            dve.wait_ge(ez_ready, 1)
            dve.wait_ge(dve_step, step_of(dve.tensor_scalar(K(0), K(15), 1.0, None, ALU.add)))
            dve.wait_ge(dve_step, step_of(dve.reciprocal(K(1), K(0))))
            dve.wait_ge(dve_step, step_of(dve.tensor_tensor(K(2), K(1), r, ALU.mult)))
            step_of(dve.tensor_scalar(coefA[:, :], K(2), 1.0, None, ALU.add))
            dve.wait_ge(dve_step, step_of(dve.scalar_tensor_tensor(
                coefB[:, :], grp_mean, -1.0, K(2), ALU.mult, ALU.mult)))
            dve.wait_ge(consts_done, NCONSTS)
            step_of(dve.tensor_copy(iota_f[:, :], iota_i))
            dve.wait_ge(dve_step, step_of(dve.tensor_copy(token_f[:, :], token_i)))

            def affine(b):
                xb = at(T, b).rearrange("p (k s) -> p k s", k=CB)
                ab, bb = coefA[:, bass.ds(b * CB, CB)], coefB[:, bass.ds(b * CB, CB)]
                for k in range(CB):
                    ins = dve.tensor_scalar(front[:, k * S:(k + 1) * S], xb[:, k, :], ab[:, k:k + 1], bb[:, k:k + 1],
                                            ALU.mult, ALU.add)
                ins.then_inc(y_ready, 1)

            def layernorm(dst, b, var_ready, rstd_ready):
                stand_alone(dve)
                for tt in range(TT):
                    step_of(dve.bn_stats(bn6[:, tt, :], tile_at(b, tt)))
                dve.wait_ge(dve_step, n.value())
                stand_alone(dve)
                for tt in range(TT):
                    step_of(dve.bn_aggr(mean_var[:, tt, :], bn6[:, tt, :]))
                dve.wait_ge(dve_step, n.value())
                dve.tensor_scalar(var_eps[:, :], mean_var[:, :, 1], EPS, None, ALU.add).then_inc(var_ready, 1)
                dve.wait_ge(rstd_ready, b + 1)
                for tt in range(TT):
                    ins = dve.tensor_scalar(dst[:, tt * C:(tt + 1) * C], tile_at(b, tt), mean_var[:, tt, 0:1],
                                            rstd[:, tt:tt + 1], ALU.subtract, ALU.mult)
                return ins

            def first_norm(part, b, s):
                for tt in range(TT):
                    dve.wait_ge(*emptied(part, f"YT{tt}", s))
                layernorm(front, b, var1_ready, rstd1_ready).then_inc(xn_ready, 1)

            def xt_low(part, b, s):
                for h in range(2):
                    dve.wait_ge(xt_h_done, 2 * b + h + 1)
                    k, _ = ring(part, f"XN{h}", s)
                    dve.tensor_tensor(xt_l[:, 2 * h:2 * h + 2, :].rearrange("p c s -> p (c s)"), ring_bank[k],
                                      xt_h[:, 2 * h:2 * h + 2, :].rearrange("p c s -> p (c s)").bitcast(fp32),
                                      ALU.subtract).then_inc(ring_free[k], 1)

            def project_out(part, item, s):
                dve.wait_ge(*filled(part, item, s))
                k, _ = ring(part, item, s)
                h = int(item[1])
                dst = (qT if item[0] == "Q" else kT)[:, 2 * h:2 * h + 2, :].rearrange("p c s -> p (c s)")
                dve.tensor_copy(dst, ring_bank[k]).then_inc(ring_free[k], 1)

            def normalise(b, c, first=False):
                dve.wait_ge(pv_done, 4 * b + c + 1)
                dve.wait_ge(dve_step, step_of(dve.reciprocal(rden[:, :], od_bank[:, S:2 * S])))
                if not first:
                    dve.wait_ge(att_l_done, 4 * b + c)
                dve.tensor_tensor(att[:, :], od_bank[:, 0:S], rden[:, :], ALU.mult).then_inc(att_ready, 1)

            def gate_top(part, b, s):
                dve.wait_ge(*filled(part, "GT", s))
                k, _ = ring(part, "GT", s)
                dve.tensor_copy(lg[:, :], ring_bank[k][:, 0:TT * E]).then_inc(ring_free[k], 1)
                dve.wait_ge(*emptied(part, "GT", s))
                stand_alone(dve)
                for tt in range(TT):
                    step_of(dve.max(top8[:, tt, :], lg[:, tt * E:(tt + 1) * E]))
                dve.wait_ge(dve_step, n.value())
                stand_alone(dve)
                for tt in range(TT):
                    step_of(dve.max_index(idx8[:, tt, :], top8[:, tt, :], lg[:, tt * E:(tt + 1) * E]))
                dve.wait_ge(dve_step, n.value())
                step_of(dve.tensor_copy(maxes[:, bass.ds(b * TT, TT), :], top8[:, :, :]))
                dve.wait_ge(dve_step, step_of(dve.tensor_copy(topi[:, bass.ds(b * TT, TT), :], idx8[:, :, :])))

            def second(part, b, s, first=False):
                for tt in range(TT):
                    dve.wait_ge(*filled(part, f"OP{tt}", s))
                    k, _ = ring(part, f"OP{tt}", s)
                    dve.tensor_tensor(tile_at(b, tt), ring_bank[k], tile_at(b, tt),
                                      ALU.add).then_inc(ring_free[k], 1)
                for tt in range(TT):
                    dve.wait_ge(*emptied(part, f"OP{tt}", s))
                if not first:
                    dve.wait_ge(x2_stored, 16 * b)
                layernorm(x2, b, var2_ready, rstd2_ready).then_inc(x2_ready, 1)

            def step(part, b, has_front, has_back):
                first = isinstance(b, int) and b == 0
                if has_front:
                    affine(b + 1)
                    first_norm(part, b + 1, b)
                if has_back:
                    gate_top(part, b - 1, b)
                if has_front:
                    xt_low(part, b + 1, b)
                normalise(b, 0, first)
                if has_front:
                    project_out(part, "Q0", b)
                    project_out(part, "K0", b)
                normalise(b, 1)
                if has_front:
                    project_out(part, "Q1", b)
                    project_out(part, "K1", b)
                normalise(b, 2)
                normalise(b, 3)
                second(part, b, b, first)

            affine(0)
            first_norm("front", 0, 0)
            xt_low("front", 0, 0)
            for item in ("Q0", "K0", "Q1", "K1"):
                project_out("front", item, 0)
            step("first", 0, True, False)
            with dve.Fori(1, B - 1) as b:
                n.enter(b - 1, 18)
                step("mid", b, True, True)
                n.leave(B - 2)
            step("last", B - 1, False, True)
            gate_top("tail", B - 1, B)
            dve.wait_ge(x2_stored, 16 * B)
            dve.wait_ge(x2T_stored, 16 * B)
            dve.tensor_tensor(ex[:, 0, :], maxes[:, :, 1], maxes[:, :, 0], ALU.subtract).then_inc(attention_over, 1)

            def first_part():
                for j in range(2):
                    step_of(dve.tensor_tensor(
                        picked[:, j, :, :], iota_f[:, 0:E].unsqueeze(1).to_broadcast([P, NT, E]),
                        topi[:, :, j:j + 1].to_broadcast([P, NT, E]), ALU.is_equal))
                dve.wait_ge(dve_step, n.value())
                dve.tensor_tensor(chosen[:, :, :], picked[:, 0, :, :], picked[:, 1, :, :],
                                  ALU.add).then_inc(chosen_ready, 1)
                dve.wait_ge(gap_exp, 1)
                dve.wait_ge(dve_step, step_of(dve.tensor_scalar(ex[:, 2, :], ex[:, 1, :], 1.0, None, ALU.add)))
                dve.wait_ge(dve_step, step_of(dve.reciprocal(w12[:, 0, :], ex[:, 2, :])))
                step_of(dve.tensor_tensor(w12[:, 1, :], w12[:, 0, :], ex[:, 1, :], ALU.mult))

            def second_part():
                R = [r4[:, k, :, :] for k in range(4)]
                prefix = route_bank[:, 0:P].rearrange("p (t e) -> p t e", e=E)
                dve.wait_ge(prefix_full, 1)
                total = R[3]
                step_of(dve.tensor_copy(total, route_bank[:, P:2 * P].rearrange("p (t e) -> p t e", e=E)))
                dve.wait_ge(dve_step, n.value())
                src = total
                for k, d in enumerate((1, 2, 4, 8)):
                    dst = R[k % 2]
                    step_of(dve.tensor_copy(dst[:, 0:d, :], src[:, 0:d, :]))
                    step_of(dve.tensor_tensor(dst[:, d:NT, :], src[:, d:NT, :], src[:, 0:NT - d, :], ALU.add))
                    dve.wait_ge(dve_step, n.value())
                    src = dst
                running = src
                dve.wait_ge(dve_step, step_of(dve.tensor_tensor(R[0], running, total, ALU.subtract)))
                dve.wait_ge(dve_step, step_of(dve.tensor_tensor(R[2], prefix, R[0], ALU.add)))
                dve.wait_ge(dve_step, step_of(dve.tensor_scalar(s8[:, 0, :], running[:, NT - 1, :], 1.0 / P, None, ALU.mult)))
                dve.wait_ge(dve_step, step_of(dve.tensor_tensor(
                    cmp[:, :, :], s8[:, 0, :].unsqueeze(2).to_broadcast([P, E, NT]),
                    iota_f[:, 0:NT].unsqueeze(1).to_broadcast([P, E, NT]), ALU.is_gt)))
                step_of(dve.tensor_reduce(s8[:, 1, :], cmp[:, :, :], AX.X, ALU.add))
                dve.wait_ge(dve_step, step_of(dve.tensor_tensor(
                    cmp8[:, 0, :, :], iota_f[:, 0:E].unsqueeze(1).to_broadcast([P, E, E]),
                    iota_f[:, 0:E].unsqueeze(2).to_broadcast([P, E, E]), ALU.is_lt)))
                dve.wait_ge(dve_step, step_of(dve.tensor_tensor(
                    cmp8[:, 1, :, :], cmp8[:, 0, :, :], s8[:, 1, :].unsqueeze(1).to_broadcast([P, E, E]), ALU.mult)))
                dve.wait_ge(dve_step, step_of(dve.tensor_reduce(s8[:, 2, :], cmp8[:, 1, :, :], AX.X, ALU.add)))
                dve.wait_ge(dve_step, step_of(dve.tensor_scalar(s8[:, 3, :], s8[:, 2, :], float(P), None, ALU.mult)))
                dve.wait_ge(dve_step, step_of(dve.tensor_tensor(
                    R[0], R[2], s8[:, 3, :].unsqueeze(1).to_broadcast([P, NT, E]), ALU.add)))
                for j in range(2):
                    step_of(dve.tensor_tensor(masked[:, j * NT:(j + 1) * NT, :], picked[:, j, :, :], R[0], ALU.mult))
                dve.wait_ge(dve_step, n.value())
                dve.wait_ge(dve_step, step_of(dve.tensor_reduce(slot_f[:, 0, :], masked[:, :, :], AX.X, ALU.add)))
                step_of(dve.tensor_copy(slots[:, :], slot_f[:, 0, :]))
                dve.wait_ge(dve_step, step_of(dve.tensor_copy(slot_i[:, 0, :], slot_f[:, 0, :])))
                step_of(dve.tensor_scalar(slot_i[:, 1, :], slot_i[:, 0, :], 7, None, ALU.logical_shift_right))
                dve.wait_ge(dve_step, step_of(dve.tensor_scalar(slot_i[:, 2, :], slot_i[:, 0, :], P - 1, None,
                                                                ALU.bitwise_and)))
                dve.wait_ge(dve_step, step_of(dve.tensor_copy(slot_f[:, 1:3, :], slot_i[:, 1:3, :])))
                dve.wait_ge(dve_step, step_of(dve.tensor_tensor(
                    te[:, :, :], iota_f[0:1, 0:NTILES].unsqueeze(2).to_broadcast([1, NTILES, E]),
                    s8[0:1, 2, :].unsqueeze(1).to_broadcast([1, NTILES, E]), ALU.is_ge)))
                dve.wait_ge(dve_step, step_of(dve.tensor_reduce(te_f[:, :], te[:, :, :], AX.X, ALU.add)))
                dve.tensor_scalar(tile_expert[:, :], te_f[:, :], -1.0, None, ALU.add).then_inc(experts_ready, 1)
                for c in range(2 * NT):
                    dve.tensor_scalar(oh_lo[:, c, :], iota_f[:, :], slot_f[:, 2, c:c + 1], None, ALU.is_equal)
                    ins = dve.tensor_scalar(oh_hi[:, c, 0:NTILES], iota_f[:, 0:NTILES], slot_f[:, 1, c:c + 1],
                                            token_f[:, c:c + 1], ALU.is_equal, ALU.mult)
                ins.then_inc(onehot_ready, 1)

            def shared(b, first=False):
                dve.wait_ge(xb_h_done, b + 1)
                dve.tensor_tensor(xb_l[:, :, :].rearrange("p c s -> p (c s)"), xc[:, :],
                                  xb_h[:, :, :].rearrange("p c s -> p (c s)").bitcast(fp32),
                                  ALU.subtract).then_inc(xb_l_done, 1)
                for j in range(CB):
                    dve.wait_ge(silu_done, CB * b + j + 1)
                    if not (first and j < 2):
                        dve.wait_ge(hl_done, CB * b + j - 1)
                    dve.tensor_tensor(hf[:, j % 2, :], gu_bank[j % 2][:, S:2 * S], sg[:, j % 2, :],
                                      ALU.mult).then_inc(h_done, 1)
                dve.wait_ge(dn_full, b + 1)
                for tt in range(TT):
                    ins = dve.tensor_tensor(tile_at(b, tt), dn_bank[tt], tile_at(b, tt), ALU.add)
                ins.then_inc(dn_free, 1)

            first_part()
            shared(0, True)
            second_part()
            shared(1)
            dve.wait_ge(ids_full, 1)
            dve.tensor_copy(ids[:, :], ids_bank[:, 0:NTILES]).then_inc(ids_ready, 1)
            with dve.Fori(2, B) as b:
                shared(b)

            def hidden(t):
                dve.wait_ge(esilu_done, t + 1)
                dve.tensor_tensor(eh[:, :], egu_bank[:, I:2 * I], es[:, :], ALU.mult).then_inc(eh_ready, 1)

            def hidden_T(t):
                dve.wait_ge(hT_full, t + 1)
                dve.tensor_copy(ehT[:, :], hT_bank[:, 0:I]).then_inc(hT_ready, 1)

            def expert_out(t, k, uses):
                dve.wait_ge(ey_full, t + 1)
                if not (isinstance(uses, int) and uses == 0):
                    dve.wait_ge(yo_stored[k], 16 * uses)
                dve.tensor_copy(yo[:, k, :], ey_bank).then_inc(yo_ready, 1)

            def three_tiles(i, start=False):
                for k in range(3):
                    hidden(3 * i + k)
                    if k == 0 and not start:
                        expert_out(3 * i - 1, 2, i - 1)
                    elif k:
                        expert_out(3 * i + k - 1, k - 1, i)
                    hidden_T(3 * i + k)

            dve.wait_ge(dn_free, B)
            three_tiles(0, start=True)
            three_tiles(1)
            with dve.Fori(2, NTILES // 3) as i:
                three_tiles(i)
            expert_out(NTILES - 1, 2, NTILES // 3 - 1)

            def combine(i, k):
                t = 4 * i + k
                dve.wait_ge(y12_loaded[k], 32 * (i + 1))
                tile = T[:, :, :].rearrange("p b n -> p (b n)")[:, bass.ds(t * C, C)]
                return t, tile

            for i in range(NT // 4):
                for k in range(4):
                    t, tile = combine(i, k)
                    if i:
                        dve.wait_ge(out_stored[k], 16 * i)
                    dve.wait_ge(dve_step, step_of(dve.scalar_tensor_tensor(
                        fin[:, k, 0, :], y12[:, k, 0, :], w12[:, 0, t:t + 1], tile, ALU.mult, ALU.add)))
                    dve.scalar_tensor_tensor(fin[:, k, 1, :], y12[:, k, 1, :], w12[:, 1, t:t + 1], fin[:, k, 0, :],
                                             ALU.mult, ALU.add).then_inc(fin_ready, 1)

        @block.tensor
        def _(pe):
            def triple(out, parts, lhs, rhs):
                products = [(k, a, b) for k in parts for a, b in ((0, 0), (0, 1), (1, 0))]
                for m, (k, a, b) in enumerate(products):
                    ins = pe.matmul(out, lhs(k, a), rhs(k, b), start=m == 0, stop=m == len(products) - 1)
                return ins

            pe.wait_ge(chmean_ready, 1)
            pe.wait_ge(consts_done, NCONSTS)
            pe.matmul(PS[0][:, 0:n32], g_avg[:, :], small[:, 3, :], start=True, stop=True).then_inc(grpmean_ready, 1)
            pe.wait_ge(chvar_ready, 1)
            pe.matmul(PS[1][:, 0:n32], g_avg[:, :], small[:, 9, :], start=True, stop=True).then_inc(grpvar_ready, 1)
            pe.wait_ge(u_ready, 1)
            pe.transpose(PS[2][0:B * UP, 0:P], u, ident[:, :]).then_inc(uT_full, 1)
            UPS = B * UP
            with pe.Fori(0, ROUNDS) as i:
                pe.wait_ge(counts_ready, i + 1)
                pe.matmul(PS[3][0:UPS, 0:3], g_med[:, :], col[:, 8:11], start=True, stop=True).then_inc(counts_summed, 1)
            pe.wait_ge(med_in, 1)
            pe.transpose(PS[4][0:1, 0:UPS], col[:, 8:9], ident[0:UPS, 0:UPS]).then_inc(med_out, 1)
            pe.wait_ge(med_in, 2)
            pe.matmul(PS[4][0:UPS, 128:129], row[0:1, 2, :], ones[0:1, 0:1], start=True, stop=True).then_inc(med_out, 1)
            pe.wait_ge(med_in, 4)
            pe.transpose(PS[5][0:1, 0:UPS], col[:, 9:10], ident[0:UPS, 0:UPS])
            pe.transpose(PS[5][0:1, 128:128 + UPS], col[:, 10:11], ident[0:UPS, 0:UPS]).then_inc(med_out, 1)
            pe.wait_ge(med_in, 5)
            pe.matmul(PS[6][:, 0:B], ones[0:1, :], row[0:1, 7, 0:B], start=True, stop=True).then_inc(med_out, 1)

            def begin(part, item, s):
                k, used = ring(part, item, s)
                if not (isinstance(used, int) and used == 0):
                    pe.wait_ge(ring_free[k], used)
                return ring_bank[k], ring_full[k]

            def y_transposes(part, b, s):
                pe.wait_ge(y_ready, b + 1)
                for tt in range(TT):
                    bank, full = begin(part, f"YT{tt}", s)
                    for k in range(CB):
                        ins = pe.transpose(bank[:, k * P:(k + 1) * P], front[:, k * S + tt * P:k * S + (tt + 1) * P],
                                           ident[:, :])
                    ins.then_inc(full, 1)

            def transposes(part, name, src, s):
                for h in range(2):
                    bank, full = begin(part, f"{name}{h}", s)
                    for k in range(2):
                        for tt in range(TT):
                            at_c = tt * C + (2 * h + k) * P
                            ins = pe.transpose(bank[:, k * S + tt * P:k * S + (tt + 1) * P], src[:, at_c:at_c + P],
                                               ident[:, :])
                    ins.then_inc(full, 1)

            def wslice(t, j, k, lo_, hi_):
                return t[:, j, k * C + lo_:k * C + hi_]

            def heads_projection(part, item, s):
                j = "QK".index(item[0])
                bank, full = begin(part, item, s)
                for m in range(2):
                    lo_ = (2 * int(item[1]) + m) * P
                    ins = triple(bank[:, m * S:(m + 1) * S], range(CB),
                                 lambda k, a: wslice((w_h, w_l)[a], j, k, lo_, lo_ + P),
                                 lambda k, a: (xt_h, xt_l)[a][:, k, :])
                ins.then_inc(full, 1)

            def values_projection(part, s, tt):
                bank, full = begin(part, f"V{tt}", s)
                triple(bank, range(CB), lambda k, a: (xt_h, xt_l)[a][:, k, tt * P:(tt + 1) * P],
                       lambda k, a: wslice((w_h, w_l)[a], 2, k, 0, C)).then_inc(full, 1)

            def head_scores(b, p, first):
                if not (first and p < 2):
                    pe.wait_ge(tanh_done, 8 * b + p - 1)
                for h in (2 * p, 2 * p + 1):
                    bank, c, r = score_bank[2 * (p % 2) + h % 2], h // HC, D * (h % HC)
                    pe.matmul(bank[:, 0:S], kT[r:r + D, c, 0:P], qT[r:r + D, c, :], start=True, stop=True)
                    ins = pe.matmul(bank[:, S:S + P], kT[r:r + D, c, P:S], qT[r:r + D, c, P:S], start=True, stop=True)
                ins.then_inc(scores_full, 1)

            def head_values(b, c, first):
                pe.wait_ge(mask_done, 8 * b + 2 * c + 2)
                if not (first and c == 0):
                    pe.wait_ge(att_ready, 4 * b + c)
                for off, lhs in ((0, lambda h, tt: v[:, tt, h * D:(h + 1) * D]), (S, lambda h, tt: ones[:, 0:D])):
                    for tt in range(TT):
                        for j in range(HC):
                            h = HC * c + j
                            pr = probs[:, (h // 2) % 4, 384 * (h % 2):384 * (h % 2 + 1)]
                            ins = pe.matmul(od_bank[j * D:(j + 1) * D, off + tt * P:off + S], lhs(h, tt),
                                            pr[:, 0:S] if tt == 0 else pr[:, S:S + P], start=tt == 0, stop=tt == TT - 1,
                                            skip_group_check=True)
                ins.then_inc(pv_done, 1)

            def out_projection(part, b):
                pe.wait_ge(att_l_done, 4 * b + 4)
                for tt in range(TT):
                    bank, full = begin(part, f"OP{tt}", b)
                    triple(bank, range(CB), lambda k, a: (att_h, att_l)[a][:, k, tt * P:(tt + 1) * P],
                           lambda k, a: wslice((w_h, w_l)[a], 3, k, 0, C)).then_inc(full, 1)

            def gate_logits(part, b, s):
                pe.wait_ge(x2_ready, b + 1)
                transposes(part, "X2T", x2, s)
                bank, full = begin(part, "GT", s)
                pe.wait_ge(*emptied(part, "X2T0", s))
                pe.wait_ge(*emptied(part, "X2T1", s))
                for tt in range(TT):
                    for k in range(CB):
                        ins = pe.matmul(bank[:, tt * E:(tt + 1) * E], x2T[:, k * S + tt * P:k * S + (tt + 1) * P],
                                        gate_sb[:, k, :], start=k == 0, stop=k == CB - 1)
                ins.then_inc(full, 1)

            def front_transposes(part, b, s):
                pe.wait_ge(xn_ready, b + 1)
                transposes(part, "XN", front, s)
                pe.wait_ge(*emptied(part, "XN0", s))
                pe.wait_ge(*emptied(part, "XN1", s))

            def step(part, b, has_front, has_back):
                first = isinstance(b, int) and b == 0
                head_scores(b, 0, first)
                head_scores(b, 1, first)
                if has_front:
                    y_transposes(part, b + 1, b)
                if has_back:
                    gate_logits(part, b - 1, b)
                head_scores(b, 2, first)
                head_scores(b, 3, first)
                if has_front:
                    pe.wait_ge(xn_ready, b + 2)
                    transposes(part, "XN", front, b)
                head_values(b, 0, first)
                head_scores(b, 4, first)
                if has_front:
                    pe.wait_ge(*emptied(part, "XN0", b))
                    pe.wait_ge(*emptied(part, "XN1", b))
                    heads_projection(part, "Q0", b)
                head_scores(b, 5, first)
                if has_front:
                    heads_projection(part, "K0", b)
                head_values(b, 1, first)
                head_scores(b, 6, first)
                head_scores(b, 7, first)
                if has_front:
                    heads_projection(part, "Q1", b)
                    heads_projection(part, "K1", b)
                head_values(b, 2, first)
                head_values(b, 3, first)
                if has_front:
                    values_projection(part, b, 0)
                    values_projection(part, b, 1)
                out_projection(part, b)

            y_transposes("front", 0, 0)
            front_transposes("front", 0, 0)
            pe.wait_ge(wlo_done, NW)
            for item in ("Q0", "K0", "Q1", "K1"):
                heads_projection("front", item, 0)
            values_projection("front", 0, 0)
            values_projection("front", 0, 1)
            for item in ("Q1", "K1", "V0", "V1", "Q0", "K0"):
                pe.wait_ge(*emptied("front", item, 0))
            pe.wait_ge(gate_loaded, 16)
            step("first", 0, True, False)
            with pe.Fori(1, B - 1) as b:
                step("mid", b, True, True)
            step("last", B - 1, False, True)
            gate_logits("tail", B - 1, B)

            pe.wait_ge(*emptied("tail", "GT", B))
            pe.wait_ge(chosen_ready, 1)
            rhs = chosen[:, :, :].rearrange("p t e -> p (t e)")
            pe.matmul(route_bank[:, 0:P], before[:, :], rhs, start=True, stop=True)
            pe.matmul(route_bank[:, P:2 * P], ones[:, :], rhs, start=True, stop=True).then_inc(prefix_full, 1)

            def hidden_chunk(b, j, first):
                if not (first and j < 2):
                    pe.wait_ge(h_done, CB * b + j - 1)
                bank = gu_bank[j % 2]
                for g in range(2):
                    ins = triple(bank[:, g * S:(g + 1) * S], range(CB),
                                 lambda k, a: wslice((sw_h, sw_l)[a], g, k, j * P, (j + 1) * P),
                                 lambda k, a: (xb_h, xb_l)[a][:, k, :])
                ins.then_inc(gu_full, 1)

            def down_chunk(b, j, first):
                pe.wait_ge(hl_done, CB * b + j + 1)
                if j == 0 and not first:
                    pe.wait_ge(dn_free, b)
                for tt in range(TT):
                    for m, (a, c) in enumerate(((0, 0), (0, 1), (1, 0))):
                        ins = pe.matmul(dn_bank[tt], (hh, hl)[a][:, j, tt * P:(tt + 1) * P],
                                        wslice((sw_h, sw_l)[c], 2, j, 0, C), start=j == 0 and m == 0,
                                        stop=j == CB - 1 and m == 2)
                if j == CB - 1:
                    ins.then_inc(dn_full, 1)

            def shared(b, first=False):
                pe.wait_ge(xb_l_done, b + 1)
                hidden_chunk(b, 0, first)
                for j in range(1, CB):
                    hidden_chunk(b, j, first)
                    down_chunk(b, j - 1, first)
                down_chunk(b, CB - 1, first)

            shared(0, True)
            shared(1)
            pe.wait_ge(onehot_ready, 1)
            for c in range(2 * NT):
                ins = pe.matmul(ids_bank[:, 0:NTILES], oh_lo[:, c, :], oh_hi[:, c, 0:NTILES], start=c == 0,
                                stop=c == 2 * NT - 1)
            ins.then_inc(ids_full, 1)
            with pe.Fori(2, B) as b:
                shared(b)

            def gather_T(t, k, turn):
                pe.wait_ge(xg_loaded[k], 16 * (turn + 1))
                for c in range(CB):
                    ins = pe.transpose(xT_bank[:, c * P:(c + 1) * P], xg[:, k, c * P:(c + 1) * P], ident[:, :])
                ins.then_inc(xT_full, 1)

            def expert_hidden(t, e):
                pe.wait_ge(xT_ready, t + 1)
                w = at(wgu_sb, e)
                for k in range(CB):
                    ins = pe.matmul(egu_bank, xgT[:, k * P:(k + 1) * P], w[:, k * 2 * I:(k + 1) * 2 * I],
                                    start=k == 0, stop=k == CB - 1)
                ins.then_inc(egu_full, 1)

            def hidden_T(t):
                pe.wait_ge(eh_ready, t + 1)
                for c in range(I // P):
                    ins = pe.transpose(hT_bank[:, c * P:(c + 1) * P], eh[:, c * P:(c + 1) * P], ident[:, :])
                ins.then_inc(hT_full, 1)

            def expert_down(t, e):
                pe.wait_ge(hT_ready, t + 1)
                if not (isinstance(t, int) and t == 0):
                    pe.wait_ge(yo_ready, t)
                w = at(wd_sb, e)
                for k in range(I // P):
                    ins = pe.matmul(ey_bank, ehT[:, k * P:(k + 1) * P], w[:, k * C:(k + 1) * C],
                                    start=k == 0, stop=k == I // P - 1)
                ins.then_inc(ey_full, 1)

            def expert_of(t):
                return pe.value_load(tile_expert[0:1, bass.ds(t, 1)], min_val=0, max_val=E - 1)

            def three_tiles(i, start=False, end=False):
                for k in range(3):
                    t = 3 * i + k
                    expert_hidden(t, expert_of(t))
                    if not (end and k == 2):
                        gather_T(t + 1, (k + 1) % 3, i + (k + 1) // 3)
                    if not (start and k == 0):
                        if start and k == 1:
                            pe.wait_ge(wd_loaded, 16 * E)
                        expert_down(t - 1, expert_of(t - 1))
                    hidden_T(t)

            pe.wait_ge(experts_ready, 1)
            pe.wait_ge(wgu_loaded, 16 * E)
            pe.wait_ge(dn_free, B)
            gather_T(0, 0, 0)
            three_tiles(0, start=True)
            with pe.Fori(1, NTILES // 3 - 1) as i:
                three_tiles(i)
            three_tiles(NTILES // 3 - 1, end=True)
            expert_down(NTILES - 1, expert_of(NTILES - 1))


def kernel(**inputs):
    import concourse.bacc as _bacc
    from concourse.bass_utils import run_bass_kernel_spmd as _run

    a = {k: np.asarray(v_) for k, v_ in inputs.items()}

    def by_rows(w):
        return w.reshape(-1, P, w.shape[-1]).transpose(1, 0, 2).reshape(P, -1)

    def channels(w):
        return w.reshape(CB, P, -1).transpose(1, 0, 2).reshape(P, -1)

    attn = [a[f"L1_attn_w_{n}"].T for n in "qkvo"]
    wgu = np.concatenate([a["L1_ffn_wg"], a["L1_ffn_wu"]], axis=2)
    arrays = {
        "x": a["x"].reshape(B, C, S),
        "params": np.concatenate([channels(a["L0_conv_cfc_w"]), channels(a["L0_conv_bn_w"]),
                                  channels(a["L0_conv_bn_b"])], axis=1),
        "wqkvo": np.stack([by_rows(w) for w in attn], axis=1),
        "gate": channels(a["L1_ffn_gate_w"].T).reshape(P, CB, E),
        "ws": np.stack([by_rows(a[f"L1_ffn_s{n}"]) for n in "gud"], axis=1),
        "wgu": np.stack([by_rows(w) for w in wgu], axis=1),
        "wd": np.stack([by_rows(w) for w in a["L1_ffn_wd"]], axis=1),
    }
    nc = _bacc.Bacc("TRN2", target_bir_lowering=False, num_devices=1)
    ins, args = {}, []
    for name, array in arrays.items():
        array = np.ascontiguousarray(array)
        ins[f"in_{name}"] = array
        args.append(nc.dram_tensor(f"in_{name}", array.shape, mybir.dt.from_np(array.dtype), kind="ExternalInput").ap())
    args.append(nc.dram_tensor("out_tokens", (B * S, C), fp32, kind="ExternalOutput").ap())
    layer_kernel(nc, *args)
    r = _run(nc, [ins], core_ids=[0])
    tokens = r.results[0]["out_tokens"]
    return np.ascontiguousarray(tokens.reshape(B, S, C).transpose(0, 2, 1)).reshape(B, C, 16, 16)
```

```python
from contextlib import ExitStack

import numpy as np
import concourse.bass as bass
from concourse import mybir

B, C, S = 8, 512, 256
NH, D = 16, 32
E, I = 8, 256
IS = 512
P = 128
CB = C // P
TT = S // P
NT = B * TT
GN_CH = C // 32
UK = 3
UP = CB * UK
MED_N = C * UK
ROUNDS = 17
RANGE = 256.0
NPAIR = NH // 2
HC = P // D
NTILES = (2 * B * S + E * (P - 1)) // P
BIG = 1e9
SOFTCAP = 30.0
EPS = 1e-5

fp32 = mybir.dt.float32
fp32r = mybir.dt.float32r
fp16 = mybir.dt.float16
i32 = mybir.dt.int32
u32 = mybir.dt.uint32
ALU = mybir.AluOpType
ACT = mybir.ActivationFunctionType
AX = mybir.AxisListType

RING = 3
STEP = ["XN0", "XN1", "X2T0", "X2T1", "GT", "Q0", "K0", "Q1", "K1", "V0", "V1", "YT0", "YT1", "OP0", "OP1"]
GATE_ITEMS = ["X2T0", "X2T1", "GT"]
PARTS = {
    "lead": (1, ["YT0", "YT1"]),
    "front": (1, [i for i in STEP[:13] if i not in GATE_ITEMS]),
    "first": (1, [i for i in STEP if i not in GATE_ITEMS]),
    "mid": (B - 3, STEP),
    "late": (1, [i for i in STEP if i[:2] != "YT"]),
    "last": (1, GATE_ITEMS + ["OP0", "OP1"]),
    "tail": (1, GATE_ITEMS),
}


def ring(part, item, b):
    n = 0
    for name, (steps, items) in PARTS.items():
        if name == part:
            break
        n += steps * len(items)
    n += items.index(item)
    return n % RING, n // RING + ((b - 1) * (len(items) // RING) if part == "mid" else 0)


class Steps:

    def __init__(self):
        self.n = 0
        self.base = 0

    def up(self):
        self.n += 1
        return self.value()

    def value(self):
        return self.n + self.base

    def enter(self, turn, per):
        self.start, self.per = self.n, per
        self.base = turn * per

    def leave(self, turns):
        assert self.n - self.start == self.per, (self.n - self.start, self.per)
        self.n += (turns - 1) * self.per
        self.base = 0



def layer_kernel(nc, x, params, wqkvo, gate, ws, wgu, wd, out):
    ctx = ExitStack()
    with ctx:
        def sb(name, shape, dt=fp32, scope=ctx):
            return scope.enter_context(nc.sbuf_tensor(name, shape, dt))

        x2_rows = nc.dram_tensor("x2_rows", [B * S, C], fp32, kind="Internal").ap()
        x2_cols = nc.dram_tensor("x2_cols", [B * P, CB * S], fp32, kind="Internal").ap()
        y_slots = nc.dram_tensor("y_slots", [NTILES * P, C], fp32, kind="Internal").ap()

        T = sb("T", [P, B, CB * S])
        ident = sb("ident", [P, P])
        ones = sb("ones", [P, P])
        before = sb("before", [P, P])
        iota_f = sb("iota_f", [P, P])
        token_f = sb("token_f", [P, 2 * NT])
        maxes = sb("maxes", [P, NT, 8])
        topi = sb("topi", [P, NT, 8])
        w12 = sb("w12", [P, 2, NT])
        slots = sb("slots", [P, 2 * NT], u32)
        ids = sb("ids", [P, NTILES], u32)
        tile_expert = sb("tile_expert", [1, NTILES], u32)

        a_scope = ExitStack()
        sw_h = sb("sw_h", [P, 3, CB * C], fp32r, a_scope)
        sw_l = sb("sw_l", [P, 3, CB * C], fp32r, a_scope)
        w_h = sb("w_h", [P, 4, CB * C], fp32r, a_scope)
        w_l = sb("w_l", [P, 4, CB * C], fp32r, a_scope)
        front = sb("front", [P, CB * S], fp32, a_scope)
        xt_h = sb("xt_h", [P, CB, S], fp32r, a_scope)
        xt_l = sb("xt_l", [P, CB, S], fp32r, a_scope)
        qT = sb("qT", [P, CB, S], fp32, a_scope)
        kT = sb("kT", [P, CB, S], fp32, a_scope)
        v = sb("v", [P, TT, C], fp32, a_scope)
        probs = sb("probs", [P, 4, 2 * 384], fp32, a_scope)
        rden = sb("rden", [P, S], fp32, a_scope)
        att = sb("att", [P, S], fp32, a_scope)
        att_h = sb("att_h", [P, CB, S], fp32r, a_scope)
        att_l = sb("att_l", [P, CB, S], fp32r, a_scope)
        x2T = sb("x2T", [P, CB * S], fp32, a_scope)
        x2 = sb("x2", [P, TT * C], fp32, a_scope)
        gate_sb = sb("gate_sb", [P, CB, E], fp32, a_scope)
        lg = sb("lg", [P, TT * E], fp32, a_scope)
        top8 = sb("top8", [P, TT, 8], fp32, a_scope)
        idx8 = sb("idx8", [P, TT, 8], u32, a_scope)
        mean_var = sb("mean_var", [P, TT, 2], fp32, a_scope)
        bn6 = sb("bn6", [P, TT, 6], fp32, a_scope)
        var_eps = sb("var_eps", [P, TT], fp32, a_scope)
        rstd = sb("rstd", [P, TT], fp32, a_scope)
        powers = sb("powers", [P, 2 * B * CB], fp32, a_scope)
        prm = sb("prm", [P, CB * UK + 2 * CB], fp32, a_scope)
        coefA = sb("coefA", [P, B * CB], fp32, a_scope)
        coefB = sb("coefB", [P, B * CB], fp32, a_scope)
        col = sb("col", [B * UP, 12], fp32, a_scope)
        row = sb("row", [1, 8, B * UP], fp32, a_scope)
        g_avg = sb("g_avg", [P, P], fp32, a_scope)
        g_med = sb("g_med", [B * UP, B * UP], fp32, a_scope)

        qf = qT[:, :, :].rearrange("p c s -> p (c s)")
        kf = kT[:, :, :].rearrange("p c s -> p (c s)")
        vf = v[:, :, :].rearrange("p t c -> p (t c)")
        n32 = B * CB
        bst = qf[:, 0:6 * n32].rearrange("p (n k) -> p n k", k=6)
        chmax = qf[:, 6 * n32:7 * n32]
        small = kf[:, 0:16 * n32].rearrange("p (k n) -> p k n", n=n32)
        pw_in = kf[:, 16 * n32:18 * n32]
        pw_out = kf[:, 18 * n32:20 * n32]
        u = vf[:, 0:B * UP]
        uw = vf[:, B * UP:4 * B * UP].rearrange("p (k n) -> p k n", k=3)
        uT = vf[0:B * UP, 4 * B * UP:4 * B * UP + P]
        junk = vf[0:B * UP, 4 * B * UP + P:4 * B * UP + 4 * P].rearrange("p (k n) -> p k n", k=3)
        iota_i = qf[:, 512:512 + P].bitcast(i32)
        token_i = qf[:, 768:768 + 2 * NT].bitcast(i32)
        stage = probs[:, :, :].rearrange("p a n -> p (a n)").rearrange("p (k n) -> p k n", n=1024)
        a_scope.close()

        wd_sb = sb("wd_sb", [P, E, (I // P) * C])
        xgT = sb("xgT", [P, C])
        es = sb("es", [P, I])
        eh = sb("eh", [P, I])
        ehT = sb("ehT", [P, I])
        yo = sb("yo", [P, 3, C])
        sw_words = 2 * 3 * CB * C
        sb("gap", [P, sw_words - (E * (I // P) * C + C + 3 * I + 3 * C)])
        wgu_sb = sb("wgu_sb", [P, E, CB * 2 * I])
        b_scope = ExitStack()
        xc = sb("xc", [P, CB * S], fp32, b_scope)
        xb_h = sb("xb_h", [P, CB, S], fp32r, b_scope)
        xb_l = sb("xb_l", [P, CB, S], fp32r, b_scope)
        hh = sb("hh", [P, CB, S], fp32r, b_scope)
        hl = sb("hl", [P, CB, S], fp32r, b_scope)
        sg = sb("sg", [P, 2, S], fp32, b_scope)
        hf = sb("hf", [P, 2, S], fp32, b_scope)
        xg = sb("xg", [P, 3, C], fp32, b_scope)
        picked = sb("picked", [P, 2, NT, E], fp32, b_scope)
        chosen = sb("chosen", [P, NT, E], fp32, b_scope)
        r4 = sb("r4", [P, 4, NT, E], fp32, b_scope)
        masked = sb("masked", [P, 2 * NT, E], fp32, b_scope)
        cmp = sb("cmp", [P, E, NT], fp32, b_scope)
        cmp8 = sb("cmp8", [P, 2, E, E], fp32, b_scope)
        s8 = sb("s8", [P, 4, E], fp32, b_scope)
        te = sb("te", [1, NTILES, E], fp32, b_scope)
        te_f = sb("te_f", [1, NTILES], fp32, b_scope)
        ex = sb("ex", [P, 4, NT], fp32, b_scope)
        slot_f = sb("slot_f", [P, 3, 2 * NT], fp32, b_scope)
        slot_i = sb("slot_i", [P, 3, 2 * NT], i32, b_scope)
        oh_lo = sb("oh_lo", [P, 2 * NT, P], fp16, b_scope)
        oh_hi = sb("oh_hi", [P, 2 * NT, 40], fp16, b_scope)
        b_scope.close()
        y12 = sb("y12", [P, 4, 2, C])
        fin = sb("fin", [P, 4, 2, C])

        scores = ctx.enter_context(nc.psum_tensor("scores", [P, 4, 512], fp32))
        PS = [scores[:, i, :] for i in range(4)]
        PS += [ctx.enter_context(nc.psum_tensor(f"PS{i}", [P, 512], fp32))[:, :] for i in range(4, 8)]
        score_bank, od_bank, ring_bank = PS[0:4], PS[4], PS[5:8]
        gu_bank, dn_bank = PS[0:2], PS[2:4]
        route_bank, ids_bank = PS[4], PS[5]
        egu_bank, ey_bank, xT_bank, hT_bank = PS[0], PS[2], PS[6], PS[7]

        def sem(name):
            return ctx.enter_context(nc.semaphore(name))

        wait_carrier = sem("wait_carrier")
        x_loaded = [sem(f"x_loaded{b}") for b in range(B)]
        prm_loaded, gate_loaded = sem("prm_loaded"), sem("gate_loaded")
        stage_loaded = [sem(f"stage_loaded{k}") for k in range(3)]
        whi_done, wlo_done = sem("whi_done"), sem("wlo_done")
        fills_done, consts_done = sem("fills_done"), sem("consts_done")
        dve_step, pool_step, act_step = sem("dve_step"), sem("pool_step"), sem("act_step")
        chmean_ready, grpmean_ready, chvar_ready, grpvar_ready = (
            sem("chmean_ready"), sem("grpmean_ready"), sem("chvar_ready"), sem("grpvar_ready"))
        powin_ready, pow_ready = sem("powin_ready"), sem("pow_ready")
        u_ready, uT_full = sem("u_ready"), sem("uT_full")
        counts_ready, counts_summed = sem("counts_ready"), sem("counts_summed")
        med_in, med_out = sem("med_in"), sem("med_out")
        z_ready, ez_ready = sem("z_ready"), sem("ez_ready")
        y_ready, t_ready = sem("y_ready"), sem("t_ready")
        var1_ready, rstd1_ready, var2_ready, rstd2_ready = (
            sem("var1_ready"), sem("rstd1_ready"), sem("var2_ready"), sem("rstd2_ready"))
        xn_ready, xt_h_done, x2_ready = sem("xn_ready"), sem("xt_h_done"), sem("x2_ready")
        ring_full = [sem(f"ring_full{k}") for k in range(RING)]
        ring_free = [sem(f"ring_free{k}") for k in range(RING)]
        scores_full, tanh_done, exp_done, mask_done = (
            sem("scores_full"), sem("tanh_done"), sem("exp_done"), sem("mask_done"))
        pv_done, att_ready, att_h_done, att_l_done = (
            sem("pv_done"), sem("att_ready"), sem("att_h_done"), sem("att_l_done"))
        x2_stored, x2T_stored = sem("x2_stored"), sem("x2T_stored")
        attention_over = sem("attention_over")
        wgu_loaded, wd_loaded = sem("wgu_loaded"), sem("wd_loaded")
        xc_loaded, xb_h_done, xb_l_done = sem("xc_loaded"), sem("xb_h_done"), sem("xb_l_done")
        gu_full, silu_done, h_done, hh_done, hl_done = (
            sem("gu_full"), sem("silu_done"), sem("h_done"), sem("hh_done"), sem("hl_done"))
        dn_full, dn_free = sem("dn_full"), sem("dn_free")
        chosen_ready, prefix_full, gap_exp = (
            sem("chosen_ready"), sem("prefix_full"), sem("gap_exp"))
        onehot_ready, ids_full, ids_ready, experts_ready = (
            sem("onehot_ready"), sem("ids_full"), sem("ids_ready"), sem("experts_ready"))
        xg_loaded = [sem(f"xg_loaded{k}") for k in range(3)]
        xT_full, xT_ready, egu_full, esilu_done, eh_ready = (
            sem("xT_full"), sem("xT_ready"), sem("egu_full"), sem("esilu_done"), sem("eh_ready"))
        hT_full, hT_ready, ey_full, yo_ready = (
            sem("hT_full"), sem("hT_ready"), sem("ey_full"), sem("yo_ready"))
        yo_stored = [sem(f"yo_stored{k}") for k in range(3)]
        y12_loaded = [sem(f"y12_loaded{k}") for k in range(4)]
        fin_ready = sem("fin_ready")
        out_stored = [sem(f"out_stored{k}") for k in range(4)]

        def at(t, b):
            return t[:, bass.ds(b, 1), :].rearrange("p a n -> p (a n)")

        def stand_alone(eng):
            eng.sem_inc(wait_carrier, 1)

        def tile_at(b, tt):
            return at(T, b)[:, tt * C:(tt + 1) * C]

        def filled(part, item, s):
            k, used = ring(part, item, s)
            return ring_full[k], used + 1

        def emptied(part, item, s):
            k, used = ring(part, item, s)
            return ring_free[k], used + 1

        NFILLS = 11
        NCONSTS = 8
        NW = 14

        def chunk_of(k, attn, shared):
            t, j = (attn, k) if k < 8 else (shared, k - 8)
            return t[:, j // 2, 1024 * (j % 2):1024 * (j % 2 + 1)]

        block = ctx.enter_context(nc.Block())

        @block.sync
        def _(sp):
            for b in range(B):
                sp.dma_start(at(T, b).rearrange("p (k s) -> p k s", k=CB),
                             x[b].rearrange("(k p) s -> p k s", p=P)).then_inc(x_loaded[b], 16)
            for k in range(NW):
                if k >= 3:
                    sp.wait_ge(wlo_done, k - 2)
                sp.dma_start(stage[:, k % 3, :], chunk_of(k, wqkvo, ws)).then_inc(stage_loaded[k % 3], 16)

            def store_x2(b):
                sp.wait_ge(x2_ready, b + 1)
                sp.dma_start(x2_rows[bass.ds(b * S, S), :].rearrange("(t p) c -> p t c", p=P),
                             x2[:, :].rearrange("p (t c) -> p t c", t=TT)).then_inc(x2_stored, 16)

            def store_x2T(part, b, s):
                sp.wait_ge(*emptied(part, "X2T0", s))
                stand_alone(sp)
                sp.wait_ge(*emptied(part, "X2T1", s))
                sp.dma_start(x2_cols[bass.ds(b * P, P), :], x2T[:, :]).then_inc(x2T_stored, 16)

            store_x2(0)
            with sp.Fori(1, B - 2) as b:
                store_x2T("mid", b - 1, b)
                store_x2(b)
            store_x2T("late", B - 3, B - 2)
            store_x2(B - 2)
            sp.wait_ge(*filled("late", "XN1", B - 2))
            sp.wait_ge(x2T_stored, 16)
            sp.dma_start(xc[:, :], x2_cols[0:P, :]).then_inc(xc_loaded, 16)
            store_x2T("last", B - 2, B - 1)
            store_x2(B - 1)
            store_x2T("tail", B - 1, B)

            sp.wait_ge(gu_full, 1)
            sp.wait_ge(x2T_stored, 16 * B)
            sp.dma_start(at(wgu_sb, 0), at(wgu, 0)).then_inc(wgu_loaded, 16)
            with sp.Fori(1, B) as b:
                sp.wait_ge(xc_loaded, 16 * b)
                sp.wait_ge(xb_l_done, b)
                sp.dma_start(xc[:, :], x2_cols[bass.ds(b * P, P), :]).then_inc(xc_loaded, 16)
                sp.dma_start(at(wgu_sb, b), at(wgu, b)).then_inc(wgu_loaded, 16)
            sp.wait_ge(dn_full, B)
            for e in range(E):
                sp.dma_start(at(wd_sb, e), at(wd, e)).then_inc(wd_loaded, 16)

            with sp.Fori(0, NTILES // 3) as i:
                for k in range(3):
                    sp.wait_ge(yo_ready, 3 * i + k + 1)
                    sp.dma_start(y_slots[bass.ds((3 * i + k) * P, P), :], yo[:, k, :]).then_inc(yo_stored[k], 16)
            with sp.Fori(0, NT // 4) as i:
                for k in range(4):
                    sp.wait_ge(fin_ready, 4 * i + k + 1)
                    sp.dma_start(out[bass.ds((4 * i + k) * P, P), :], fin[:, k, 1, :]).then_inc(out_stored[k], 16)
            for k in range(4):
                sp.wait_ge(out_stored[k], 16 * (NT // 4))

        @block.gpsimd
        def _(pool):
            pool.wait_ge(fills_done, NFILLS)
            for t, base, pattern, mult, fill, op in (
                (ident[:, :], 0, [[-1, P]], 1, 1.0, ALU.not_equal),
                (before[:, :], -1, [[1, P]], -1, 0.0, ALU.is_ge),
                (g_avg[:, :].rearrange("p (a c) -> p a c", c=GN_CH), 0, [[-GN_CH, 8], [0, GN_CH]], 1, 0.0, ALU.is_ge),
                (g_med[:, :].rearrange("p (a c) -> p a c", c=UP), 0, [[-UP, B], [0, UP]], 1, 0.0, ALU.is_ge),
            ):
                pool.affine_select(out=t, in_=t, compare_op=op, fill=fill, base=base, pattern=pattern,
                                   channel_multiplier=mult).then_inc(consts_done, 1)
            pool.wait_ge(consts_done, 4)
            for t, base, pattern in (
                (g_avg[:, :].rearrange("p (a c) -> p a c", c=GN_CH), GN_CH - 1, [[GN_CH, 8], [0, GN_CH]]),
                (g_med[:, :].rearrange("p (a c) -> p a c", c=UP), UP - 1, [[UP, B], [0, UP]]),
            ):
                pool.affine_select(out=t, in_=t, compare_op=ALU.is_ge, fill=0.0, base=base, pattern=pattern,
                                   channel_multiplier=-1).then_inc(consts_done, 1)
            pool.iota(iota_i, pattern=[[1, P]], base=0, channel_multiplier=0).then_inc(consts_done, 1)
            pool.iota(token_i.rearrange("p (a t) -> p a t", a=2), pattern=[[0, 2], [P, NT]], base=0,
                      channel_multiplier=1).then_inc(consts_done, 1)

            for k in range(NW):
                pool.wait_ge(whi_done, k + 1)
                pool.tensor_tensor(chunk_of(k, w_l, sw_l), stage[:, k % 3, :],
                                   chunk_of(k, w_h, sw_h).bitcast(fp32), ALU.subtract).then_inc(wlo_done, 1)
                if k == 5:
                    pool.wait_ge(powin_ready, 1)
                    pool.tensor_tensor(pw_out, pw_in, powers[:, :], ALU.pow).then_inc(pow_ready, 1)

            def rstd_of(var_ready, rstd_ready, b):
                pool.wait_ge(var_ready, b + 1)
                pool.tensor_tensor(rstd[:, :], var_eps[:, :], powers[:, 0:TT], ALU.pow).then_inc(rstd_ready, 1)

            def mask(b, p):
                pool.wait_ge(exp_done, 8 * b + p + 1)
                stand_alone(pool)
                for a in range(2):
                    t = probs[:, p % 4, :].rearrange("p (h q) -> p h q", h=2)[:, :, 256 * a:256 * a + P]
                    ins = pool.affine_select(out=t, in_=t, compare_op=ALU.is_ge, fill=0.0, base=0,
                                             pattern=[[0, 2], [1, P]], channel_multiplier=-1)
                ins.then_inc(mask_done, 1)

            def att_low(b, c):
                pool.wait_ge(att_h_done, 4 * b + c + 1)
                pool.tensor_tensor(att_l[:, c, :], att[:, :], att_h[:, c, :].bitcast(fp32),
                                   ALU.subtract).then_inc(att_l_done, 1)

            def step(b, has_next):
                for p in range(5):
                    mask(b, p)
                att_low(b, 0)
                mask(b, 5)
                mask(b, 6)
                att_low(b, 1)
                mask(b, 7)
                att_low(b, 2)
                att_low(b, 3)
                if has_next:
                    rstd_of(var1_ready, rstd1_ready, b + 2)
                rstd_of(var2_ready, rstd2_ready, b)

            rstd_of(var1_ready, rstd1_ready, 0)
            rstd_of(var1_ready, rstd1_ready, 1)
            step(0, True)
            with pool.Fori(1, B - 2) as b:
                step(b, True)
            step(B - 2, False)
            step(B - 1, False)

            def hidden_low_of(b):
                for j in range(CB):
                    pool.wait_ge(hh_done, CB * b + j + 1)
                    pool.tensor_tensor(hl[:, j, :], hf[:, j % 2, :], hh[:, j, :].bitcast(fp32),
                                       ALU.subtract).then_inc(hl_done, 1)

            with pool.Fori(0, B) as b:
                hidden_low_of(b)

            pool.wait_ge(ids_ready, 1)
            for t in range(NTILES):
                if t >= 3:
                    pool.wait_ge(xT_full, t - 2)
                pool.indirect_dma_start(xg[:, t % 3, :], None, x2_rows[:, :],
                                        bass.IndirectOffsetOnAxis(ids[:, t:t + 1], 0)).then_inc(xg_loaded[t % 3], 16)
            for k in range(3):
                pool.wait_ge(yo_stored[k], 16 * (NTILES // 3))
            for t in range(NT):
                if t >= 4:
                    pool.wait_ge(fin_ready, t - 3)
                for j in range(2):
                    c = j * NT + t
                    pool.indirect_dma_start(y12[:, t % 4, j, :], None, y_slots[:, :],
                                            bass.IndirectOffsetOnAxis(slots[:, c:c + 1], 0)).then_inc(y12_loaded[t % 4], 16)

        @block.scalar
        def _(act):
            act.dma_start(prm[:, :], params).then_inc(prm_loaded, 16)
            act.dma_start(gate_sb[:, :, :], gate).then_inc(gate_loaded, 16)
            for k in range(NW):
                act.wait_ge(stage_loaded[k % 3], 16 * (k // 3 + 1))
                act.activation(chunk_of(k, w_h, sw_h), stage[:, k % 3, :], ACT.Copy).then_inc(whi_done, 1)
            act.wait_ge(z_ready, 1)
            act.activation(small[:, 15, :], small[:, 14, :], ACT.Exp, scale=-1.0).then_inc(ez_ready, 1)

            def tokens(part, b, s):
                for tt in range(TT):
                    act.wait_ge(*filled(part, f"YT{tt}", s))
                    k, _ = ring(part, f"YT{tt}", s)
                    act.activation(tile_at(b, tt), ring_bank[k], ACT.Copy).then_inc(ring_free[k], 1)

            def xt_high(part, s):
                for h in range(2):
                    act.wait_ge(*filled(part, f"XN{h}", s))
                    k, _ = ring(part, f"XN{h}", s)
                    act.activation(xt_h[:, 2 * h:2 * h + 2, :].rearrange("p c s -> p (c s)"), ring_bank[k],
                                   ACT.Copy).then_inc(xt_h_done, 1)

            def values(part, s):
                for tt in range(TT):
                    act.wait_ge(*filled(part, f"V{tt}", s))
                    k, _ = ring(part, f"V{tt}", s)
                    act.activation(v[:, tt, :], ring_bank[k], ACT.Copy).then_inc(ring_free[k], 1)

            def soft(b, p, first=False):
                act.wait_ge(scores_full, 8 * b + p + 1)
                if not (first and p < 4):
                    act.wait_ge(pv_done, 4 * b + p // 2 - 1)
                act.activation(probs[:, p % 4, :].rearrange("p (h q) -> p h q", h=2),
                               scores[:, 2 * (p % 2):2 * (p % 2) + 2, 0:384], ACT.Tanh,
                               scale=1.0 / (np.sqrt(D) * SOFTCAP)).then_inc(tanh_done, 1)
                act.wait_ge(tanh_done, 8 * b + p + 1)
                act.activation(probs[:, p % 4, :], probs[:, p % 4, :], ACT.Exp, scale=SOFTCAP).then_inc(exp_done, 1)

            def att_high(b, c):
                act.wait_ge(att_ready, 4 * b + c + 1)
                act.activation(att_h[:, c, :], att[:, :], ACT.Copy).then_inc(att_h_done, 1)

            def x2_transposed(part, s):
                for h in range(2):
                    act.wait_ge(*filled(part, f"X2T{h}", s))
                    k, _ = ring(part, f"X2T{h}", s)
                    act.activation(x2T[:, 512 * h:512 * (h + 1)], ring_bank[k], ACT.Copy).then_inc(ring_free[k], 1)

            def step(part, b, has_front, has_back, has_next):
                first = isinstance(b, int) and b == 0
                soft(b, 0, first)
                soft(b, 1, first)
                if has_front:
                    xt_high(part, b)
                soft(b, 2, first)
                soft(b, 3, first)
                if has_back:
                    x2_transposed(part, b)
                soft(b, 4, first)
                att_high(b, 0)
                soft(b, 5, first)
                att_high(b, 1)
                soft(b, 6, first)
                soft(b, 7, first)
                att_high(b, 2)
                att_high(b, 3)
                if has_front:
                    values(part, b)
                if has_next:
                    tokens(part, b + 2, b)
                if has_back:
                    act.wait_ge(x2T_stored, 16 * b)

            def split_high(b):
                act.wait_ge(xc_loaded, 16 * (b + 1))
                act.activation(xb_h[:, :, :].rearrange("p c s -> p (c s)"), xc[:, :], ACT.Copy).then_inc(xb_h_done, 1)

            tokens("lead", 0, 0)
            xt_high("front", 0)
            values("front", 0)
            tokens("front", 1, 0)
            act.wait_ge(wlo_done, NW)
            step("first", 0, True, False, True)
            with act.Fori(1, B - 2) as b:
                step("mid", b, True, True, True)
            step("late", B - 2, True, True, False)
            split_high(0)
            step("last", B - 1, False, True, False)

            def gated_shared(b, j):
                act.wait_ge(gu_full, CB * b + j + 1)
                act.activation(sg[:, j % 2, :], gu_bank[j % 2][:, 0:S], ACT.Silu).then_inc(silu_done, 1)
                act.wait_ge(h_done, CB * b + j + 1)
                act.activation(hh[:, j, :], hf[:, j % 2, :], ACT.Copy).then_inc(hh_done, 1)

            gated_shared(0, 0)
            gated_shared(0, 1)
            x2_transposed("tail", B)
            gated_shared(0, 2)
            gated_shared(0, 3)
            split_high(1)
            act.wait_ge(attention_over, 1)
            act.activation(ex[:, 1, :], ex[:, 0, :], ACT.Exp).then_inc(gap_exp, 1)
            with act.Fori(1, B - 1) as b:
                for j in range(CB):
                    gated_shared(b, j)
                split_high(b + 1)
            for j in range(CB):
                gated_shared(B - 1, j)

            def x_transposed(t):
                act.wait_ge(xT_full, t + 1)
                act.activation(xgT[:, :], xT_bank, ACT.Copy).then_inc(xT_ready, 1)

            def gated(t):
                act.wait_ge(egu_full, t + 1)
                act.activation(es[:, :], egu_bank[:, 0:I], ACT.Silu).then_inc(esilu_done, 1)

            act.wait_ge(dn_full, B)
            x_transposed(0)
            with act.Fori(0, NTILES - 1) as t:
                gated(t)
                x_transposed(t + 1)
            gated(NTILES - 1)

        @block.vector
        def _(dve):
            n = Steps()

            def fill(t, value):
                dve.memset(t, value).then_inc(fills_done, 1)

            fill(ident[:, :], 0.0)
            fill(before[:, :], 1.0)
            fill(g_avg[:, :], 1.0 / GN_CH)
            fill(g_med[:, :], 1.0)
            fill(ones[:, :], 1.0)
            fill(powers[:, 0:n32], -0.5)
            fill(powers[:, n32:2 * n32], 0.5)
            lo, below = col[:, 0:1], col[:, 1:2]
            thr, jw, cnt = col[:, 2:5], col[:, 5:8], col[:, 8:11]
            fill(lo, -RANGE / 2)
            for j in range(3):
                fill(jw[:, j:j + 1], (j + 1) * RANGE / 4)
            dve.wait_ge(fills_done, NFILLS)

            for b in range(B):
                dve.wait_ge(x_loaded[b], 16)
                xb = at(T, b).rearrange("p (k s) -> p k s", k=CB)
                for k in range(CB):
                    dve.bn_stats(bst[:, CB * b + k, :], xb[:, k, :])
                ins = dve.reduce_max(chmax[:, CB * b:CB * (b + 1)], xb, AX.X)
            ins.then_inc(dve_step, 1)
            dve.wait_ge(dve_step, n.up())

            def step_of(ins):
                ins.then_inc(dve_step, 1)
                return n.up()

            def K(k):
                return small[:, k, :]

            step_of(dve.tensor_tensor(K(0), bst[:, :, 1], bst[:, :, 4], ALU.add))
            step_of(dve.tensor_tensor(K(1), bst[:, :, 1], bst[:, :, 4], ALU.subtract))
            dve.wait_ge(dve_step, step_of(dve.tensor_tensor(K(2), bst[:, :, 2], bst[:, :, 5], ALU.add)))
            dve.tensor_scalar(K(3), K(0), 0.5, None, ALU.mult).then_inc(chmean_ready, 1)
            dve.wait_ge(dve_step, step_of(dve.tensor_tensor(K(4), K(1), K(1), ALU.mult)))
            dve.wait_ge(dve_step, step_of(dve.scalar_tensor_tensor(
                K(5), K(4), S / 4.0, K(2), ALU.mult, ALU.add)))
            dve.wait_ge(grpmean_ready, 1)
            grp_mean = K(6)
            dve.wait_ge(dve_step, step_of(dve.tensor_copy(grp_mean, PS[0][:, 0:n32])))
            dve.wait_ge(dve_step, step_of(dve.tensor_tensor(K(7), K(3), grp_mean, ALU.subtract)))
            dve.wait_ge(dve_step, step_of(dve.tensor_tensor(K(8), K(7), K(7), ALU.mult)))
            dve.scalar_tensor_tensor(K(9), K(5), 1.0 / S, K(8), ALU.mult, ALU.add).then_inc(chvar_ready, 1)
            step_of(dve.tensor_scalar(pw_in[:, n32:2 * n32], K(5), 1.0 / (S - 1), 1e-30, ALU.mult, ALU.max))
            dve.wait_ge(grpvar_ready, 1)
            dve.tensor_scalar(pw_in[:, 0:n32], PS[1][:, 0:n32], EPS, None, ALU.add).then_inc(powin_ready, 1)
            dve.wait_ge(pow_ready, 1)
            r = pw_out[:, 0:n32]
            u3 = u.rearrange("p (n k) -> p n k", k=UK)
            dve.wait_ge(dve_step, step_of(dve.tensor_tensor(K(10), chmax, grp_mean, ALU.subtract)))
            dve.tensor_tensor(u3[:, :, 0], K(7), r, ALU.mult)
            dve.tensor_tensor(u3[:, :, 1], K(10), r, ALU.mult)
            dve.tensor_tensor(u3[:, :, 2], pw_out[:, n32:2 * n32], r, ALU.mult).then_inc(u_ready, 1)

            dve.wait_ge(uT_full, 1)
            dve.wait_ge(dve_step, step_of(dve.tensor_copy(uT, PS[2][0:B * UP, 0:P])))
            with dve.Fori(0, ROUNDS) as i:
                n.enter(i, 6)
                dve.wait_ge(dve_step, step_of(dve.tensor_scalar(thr, jw, lo, None, ALU.add)))
                for j in range(3):
                    ins = dve.tensor_scalar(junk[:, j, :], uT, thr[:, j:j + 1], 0.0, ALU.is_le, ALU.add,
                                            accum_out=cnt[:, j:j + 1])
                    if j < 2:
                        step_of(ins)
                ins.then_inc(counts_ready, 1)
                dve.wait_ge(counts_summed, i + 1)
                dve.wait_ge(dve_step, step_of(dve.tensor_scalar(
                    thr, PS[3][0:B * UP, 0:3], MED_N / 2 - 0.5, 0.0, ALU.is_lt, ALU.add, accum_out=below)))
                dve.wait_ge(dve_step, step_of(dve.scalar_tensor_tensor(
                    lo, below, jw[:, 0:1], lo, ALU.mult, ALU.add)))
                dve.wait_ge(dve_step, step_of(dve.tensor_scalar(jw, jw, 0.25, None, ALU.mult)))
                n.leave(ROUNDS)

            def least(dst, bound):
                dve.wait_ge(dve_step, step_of(dve.tensor_scalar(junk[:, 0, :], uT, bound, BIG, ALU.is_le, ALU.mult)))
                dve.wait_ge(dve_step, step_of(dve.tensor_tensor(junk[:, 1, :], junk[:, 0, :], uT, ALU.add)))
                return dve.tensor_reduce(dst, junk[:, 1, :], AX.X, ALU.min)

            def of_batch(k):
                return row[0:1, k, :].rearrange("p (b n) -> p b n", b=B)

            least(cnt[:, 0:1], lo).then_inc(med_in, 1)
            dve.wait_ge(med_out, 1)
            dve.wait_ge(dve_step, step_of(dve.tensor_reduce(
                row[0:1, 1, 0:B], PS[4][0:1, 0:B * UP].rearrange("p (b n) -> p b n", b=B), AX.X, ALU.min)))
            dve.tensor_copy(of_batch(2), row[0:1, 1, 0:B].unsqueeze(2).to_broadcast([1, B, UP])).then_inc(med_in, 1)
            dve.wait_ge(med_out, 2)
            dve.wait_ge(dve_step, step_of(dve.tensor_copy(thr[:, 0:1], PS[4][0:B * UP, 128:129])))
            dve.tensor_scalar(junk[:, 2, :], uT, thr[:, 0:1], 0.0, ALU.is_le, ALU.add,
                              accum_out=cnt[:, 1:2]).then_inc(med_in, 1)
            least(cnt[:, 2:3], thr[:, 0:1]).then_inc(med_in, 1)
            dve.wait_ge(med_out, 3)
            step_of(dve.tensor_reduce(row[0:1, 3, 0:B], PS[5][0:1, 0:B * UP].rearrange("p (b n) -> p b n", b=B),
                                      AX.X, ALU.add))
            dve.wait_ge(dve_step, step_of(dve.tensor_reduce(
                row[0:1, 4, 0:B], PS[5][0:1, 128:128 + B * UP].rearrange("p (b n) -> p b n", b=B), AX.X, ALU.min)))
            dve.wait_ge(dve_step, step_of(dve.tensor_scalar(
                row[0:1, 5, 0:B], row[0:1, 3, 0:B], MED_N / 2 + 0.5, BIG, ALU.is_lt, ALU.mult)))
            dve.wait_ge(dve_step, step_of(dve.tensor_tensor(
                row[0:1, 5, 0:B], row[0:1, 5, 0:B], row[0:1, 1, 0:B], ALU.add)))
            dve.wait_ge(dve_step, step_of(dve.tensor_tensor(
                row[0:1, 6, 0:B], row[0:1, 5, 0:B], row[0:1, 4, 0:B], ALU.min)))
            dve.wait_ge(dve_step, step_of(dve.tensor_tensor(
                row[0:1, 6, 0:B], row[0:1, 6, 0:B], row[0:1, 1, 0:B], ALU.add)))
            dve.tensor_scalar(row[0:1, 7, 0:B], row[0:1, 6, 0:B], 0.5, None, ALU.mult).then_inc(med_in, 1)

            dve.wait_ge(med_out, 4)
            dve.wait_ge(prm_loaded, 16)
            by_b = "p (b n) -> p b n"
            dve.wait_ge(dve_step, step_of(dve.tensor_tensor(
                uw[:, 0, :].rearrange(by_b, b=B), u.rearrange(by_b, b=B),
                PS[6][:, 0:B].unsqueeze(2).to_broadcast([P, B, UP]), ALU.subtract)))
            dve.wait_ge(dve_step, step_of(dve.tensor_tensor(uw[:, 1, :], uw[:, 0, :], uw[:, 0, :], ALU.mult)))
            dve.wait_ge(dve_step, step_of(dve.tensor_tensor(uw[:, 2, :], uw[:, 1, :], uw[:, 0, :], ALU.mult)))
            dve.wait_ge(dve_step, step_of(dve.tensor_tensor(
                uw[:, 0, :].rearrange(by_b, b=B), uw[:, 2, :].rearrange(by_b, b=B),
                prm[:, 0:UP].unsqueeze(1).to_broadcast([P, B, UP]), ALU.mult)))
            dve.wait_ge(dve_step, step_of(dve.tensor_reduce(
                K(11), uw[:, 0, :].rearrange("p (n k) -> p n k", k=UK), AX.X, ALU.add)))
            bn_scale = float(1.0 / np.sqrt(np.float32(1.0) + np.float32(EPS)))
            dve.wait_ge(dve_step, step_of(dve.scalar_tensor_tensor(
                K(12).rearrange(by_b, b=B), K(11).rearrange(by_b, b=B), bn_scale,
                prm[:, UP:UP + CB].unsqueeze(1).to_broadcast([P, B, CB]), ALU.mult, ALU.mult)))
            dve.tensor_tensor(K(14).rearrange(by_b, b=B), K(12).rearrange(by_b, b=B),
                              prm[:, UP + CB:UP + 2 * CB].unsqueeze(1).to_broadcast([P, B, CB]),
                              ALU.add).then_inc(z_ready, 1)
            dve.wait_ge(ez_ready, 1)
            dve.wait_ge(dve_step, step_of(dve.tensor_scalar(K(0), K(15), 1.0, None, ALU.add)))
            dve.wait_ge(dve_step, step_of(dve.reciprocal(K(1), K(0))))
            dve.wait_ge(dve_step, step_of(dve.tensor_tensor(K(2), K(1), r, ALU.mult)))
            step_of(dve.tensor_scalar(coefA[:, :], K(2), 1.0, None, ALU.add))
            dve.wait_ge(dve_step, step_of(dve.scalar_tensor_tensor(
                coefB[:, :], grp_mean, -1.0, K(2), ALU.mult, ALU.mult)))
            dve.wait_ge(consts_done, NCONSTS)
            step_of(dve.tensor_copy(iota_f[:, :], iota_i))
            dve.wait_ge(dve_step, step_of(dve.tensor_copy(token_f[:, :], token_i)))

            def affine(b):
                xb = at(T, b).rearrange("p (k s) -> p k s", k=CB)
                ab, bb = coefA[:, bass.ds(b * CB, CB)], coefB[:, bass.ds(b * CB, CB)]
                for k in range(CB):
                    ins = dve.tensor_scalar(front[:, k * S:(k + 1) * S], xb[:, k, :], ab[:, k:k + 1], bb[:, k:k + 1],
                                            ALU.mult, ALU.add)
                ins.then_inc(y_ready, 1)

            def layernorm(dst, b, var_ready, rstd_ready):
                stand_alone(dve)
                for tt in range(TT):
                    step_of(dve.bn_stats(bn6[:, tt, :], tile_at(b, tt)))
                dve.wait_ge(dve_step, n.value())
                stand_alone(dve)
                for tt in range(TT):
                    step_of(dve.bn_aggr(mean_var[:, tt, :], bn6[:, tt, :]))
                dve.wait_ge(dve_step, n.value())
                dve.tensor_scalar(var_eps[:, :], mean_var[:, :, 1], EPS, None, ALU.add).then_inc(var_ready, 1)
                dve.wait_ge(rstd_ready, b + 1)
                for tt in range(TT):
                    ins = dve.tensor_scalar(dst[:, tt * C:(tt + 1) * C], tile_at(b, tt), mean_var[:, tt, 0:1],
                                            rstd[:, tt:tt + 1], ALU.subtract, ALU.mult)
                return ins

            def first_norm(part, b, s):
                for tt in range(TT):
                    dve.wait_ge(*emptied(part, f"YT{tt}", s))
                layernorm(front, b, var1_ready, rstd1_ready).then_inc(xn_ready, 1)

            def xt_low(part, b, s):
                for h in range(2):
                    dve.wait_ge(xt_h_done, 2 * b + h + 1)
                    k, _ = ring(part, f"XN{h}", s)
                    dve.tensor_tensor(xt_l[:, 2 * h:2 * h + 2, :].rearrange("p c s -> p (c s)"), ring_bank[k],
                                      xt_h[:, 2 * h:2 * h + 2, :].rearrange("p c s -> p (c s)").bitcast(fp32),
                                      ALU.subtract).then_inc(ring_free[k], 1)

            def project_out(part, item, s):
                dve.wait_ge(*filled(part, item, s))
                k, _ = ring(part, item, s)
                h = int(item[1])
                dst = (qT if item[0] == "Q" else kT)[:, 2 * h:2 * h + 2, :].rearrange("p c s -> p (c s)")
                dve.tensor_copy(dst, ring_bank[k]).then_inc(ring_free[k], 1)

            def normalise(b, c, first=False):
                dve.wait_ge(pv_done, 4 * b + c + 1)
                dve.wait_ge(dve_step, step_of(dve.reciprocal(rden[:, :], od_bank[:, S:2 * S])))
                if not first:
                    dve.wait_ge(att_l_done, 4 * b + c)
                dve.tensor_tensor(att[:, :], od_bank[:, 0:S], rden[:, :], ALU.mult).then_inc(att_ready, 1)

            def gate_top(part, b, s):
                dve.wait_ge(*filled(part, "GT", s))
                k, _ = ring(part, "GT", s)
                dve.tensor_copy(lg[:, :], ring_bank[k][:, 0:TT * E]).then_inc(ring_free[k], 1)
                dve.wait_ge(*emptied(part, "GT", s))
                stand_alone(dve)
                for tt in range(TT):
                    step_of(dve.max(top8[:, tt, :], lg[:, tt * E:(tt + 1) * E]))
                dve.wait_ge(dve_step, n.value())
                stand_alone(dve)
                for tt in range(TT):
                    step_of(dve.max_index(idx8[:, tt, :], top8[:, tt, :], lg[:, tt * E:(tt + 1) * E]))
                dve.wait_ge(dve_step, n.value())
                step_of(dve.tensor_copy(maxes[:, bass.ds(b * TT, TT), :], top8[:, :, :]))
                dve.wait_ge(dve_step, step_of(dve.tensor_copy(topi[:, bass.ds(b * TT, TT), :], idx8[:, :, :])))

            def second(part, b, s, first=False):
                for tt in range(TT):
                    dve.wait_ge(*filled(part, f"OP{tt}", s))
                    k, _ = ring(part, f"OP{tt}", s)
                    dve.tensor_tensor(tile_at(b, tt), ring_bank[k], tile_at(b, tt),
                                      ALU.add).then_inc(ring_free[k], 1)
                for tt in range(TT):
                    dve.wait_ge(*emptied(part, f"OP{tt}", s))
                if not first:
                    dve.wait_ge(x2_stored, 16 * b)
                layernorm(x2, b, var2_ready, rstd2_ready).then_inc(x2_ready, 1)

            def split_low(b):
                dve.wait_ge(xb_h_done, b + 1)
                dve.tensor_tensor(xb_l[:, :, :].rearrange("p c s -> p (c s)"), xc[:, :],
                                  xb_h[:, :, :].rearrange("p c s -> p (c s)").bitcast(fp32),
                                  ALU.subtract).then_inc(xb_l_done, 1)

            def step(part, b, has_front, has_back, has_next):
                first = isinstance(b, int) and b == 0
                if has_front:
                    xt_low(part, b + 1, b)
                normalise(b, 0, first)
                if has_back:
                    gate_top(part, b - 1, b)
                if has_front:
                    project_out(part, "Q0", b)
                normalise(b, 1)
                if has_front:
                    project_out(part, "K0", b)
                if has_next:
                    affine(b + 2)
                normalise(b, 2)
                if has_front:
                    project_out(part, "Q1", b)
                normalise(b, 3)
                if has_front:
                    project_out(part, "K1", b)
                if has_next:
                    first_norm(part, b + 2, b)
                if not (has_front or has_next):
                    split_low(0)
                second(part, b, b, first)

            affine(0)
            first_norm("lead", 0, 0)
            xt_low("front", 0, 0)
            affine(1)
            for item in ("Q0", "K0", "Q1", "K1"):
                project_out("front", item, 0)
            first_norm("front", 1, 0)
            step("first", 0, True, False, True)
            with dve.Fori(1, B - 2) as b:
                n.enter(b - 1, 18)
                step("mid", b, True, True, True)
                n.leave(B - 3)
            step("late", B - 2, True, True, False)
            step("last", B - 1, False, True, False)

            def hidden_shared(b, j, first=False):
                dve.wait_ge(silu_done, CB * b + j + 1)
                if not (first and j < 2):
                    dve.wait_ge(hl_done, CB * b + j - 1)
                dve.tensor_tensor(hf[:, j % 2, :], gu_bank[j % 2][:, S:2 * S], sg[:, j % 2, :],
                                  ALU.mult).then_inc(h_done, 1)

            def add_shared(b):
                dve.wait_ge(dn_full, b + 1)
                for tt in range(TT):
                    ins = dve.tensor_tensor(tile_at(b, tt), dn_bank[tt], tile_at(b, tt), ALU.add)
                ins.then_inc(dn_free, 1)

            hidden_shared(0, 0, True)
            hidden_shared(0, 1, True)
            gate_top("tail", B - 1, B)
            hidden_shared(0, 2)
            hidden_shared(0, 3)
            dve.wait_ge(x2_stored, 16 * B)
            dve.wait_ge(x2T_stored, 16 * B)
            dve.tensor_tensor(ex[:, 0, :], maxes[:, :, 1], maxes[:, :, 0], ALU.subtract).then_inc(attention_over, 1)

            for j in range(2):
                step_of(dve.tensor_tensor(
                    picked[:, j, :, :], iota_f[:, 0:E].unsqueeze(1).to_broadcast([P, NT, E]),
                    topi[:, :, j:j + 1].to_broadcast([P, NT, E]), ALU.is_equal))
            dve.wait_ge(dve_step, n.value())
            dve.tensor_tensor(chosen[:, :, :], picked[:, 0, :, :], picked[:, 1, :, :],
                              ALU.add).then_inc(chosen_ready, 1)
            split_low(1)
            dve.wait_ge(gap_exp, 1)
            dve.wait_ge(dve_step, step_of(dve.tensor_scalar(ex[:, 2, :], ex[:, 1, :], 1.0, None, ALU.add)))
            dve.wait_ge(dve_step, step_of(dve.reciprocal(w12[:, 0, :], ex[:, 2, :])))
            step_of(dve.tensor_tensor(w12[:, 1, :], w12[:, 0, :], ex[:, 1, :], ALU.mult))

            R = [r4[:, k, :, :] for k in range(4)]
            prefix = route_bank[:, 0:P].rearrange("p (t e) -> p t e", e=E)
            total, running = R[3], R[1]

            def running_sums():
                dve.wait_ge(prefix_full, 1)
                step_of(dve.tensor_copy(total, route_bank[:, P:2 * P].rearrange("p (t e) -> p t e", e=E)))
                dve.wait_ge(dve_step, n.value())
                src = total
                for k, d in enumerate((1, 2, 4, 8)):
                    dst = R[k % 2]
                    step_of(dve.tensor_copy(dst[:, 0:d, :], src[:, 0:d, :]))
                    step_of(dve.tensor_tensor(dst[:, d:NT, :], src[:, d:NT, :], src[:, 0:NT - d, :], ALU.add))
                    dve.wait_ge(dve_step, n.value())
                    src = dst

            def expert_starts():
                dve.wait_ge(dve_step, step_of(dve.tensor_tensor(R[0], running, total, ALU.subtract)))
                dve.wait_ge(dve_step, step_of(dve.tensor_tensor(R[2], prefix, R[0], ALU.add)))
                dve.wait_ge(dve_step, step_of(dve.tensor_scalar(s8[:, 0, :], running[:, NT - 1, :], 1.0 / P, None, ALU.mult)))
                dve.wait_ge(dve_step, step_of(dve.tensor_tensor(
                    cmp[:, :, :], s8[:, 0, :].unsqueeze(2).to_broadcast([P, E, NT]),
                    iota_f[:, 0:NT].unsqueeze(1).to_broadcast([P, E, NT]), ALU.is_gt)))
                step_of(dve.tensor_reduce(s8[:, 1, :], cmp[:, :, :], AX.X, ALU.add))
                dve.wait_ge(dve_step, step_of(dve.tensor_tensor(
                    cmp8[:, 0, :, :], iota_f[:, 0:E].unsqueeze(1).to_broadcast([P, E, E]),
                    iota_f[:, 0:E].unsqueeze(2).to_broadcast([P, E, E]), ALU.is_lt)))
                dve.wait_ge(dve_step, step_of(dve.tensor_tensor(
                    cmp8[:, 1, :, :], cmp8[:, 0, :, :], s8[:, 1, :].unsqueeze(1).to_broadcast([P, E, E]), ALU.mult)))
                dve.wait_ge(dve_step, step_of(dve.tensor_reduce(s8[:, 2, :], cmp8[:, 1, :, :], AX.X, ALU.add)))
                dve.wait_ge(dve_step, step_of(dve.tensor_scalar(s8[:, 3, :], s8[:, 2, :], float(P), None, ALU.mult)))

            def pair_slots():
                dve.wait_ge(dve_step, step_of(dve.tensor_tensor(
                    R[0], R[2], s8[:, 3, :].unsqueeze(1).to_broadcast([P, NT, E]), ALU.add)))
                for j in range(2):
                    step_of(dve.tensor_tensor(masked[:, j * NT:(j + 1) * NT, :], picked[:, j, :, :], R[0], ALU.mult))
                dve.wait_ge(dve_step, n.value())
                dve.wait_ge(dve_step, step_of(dve.tensor_reduce(slot_f[:, 0, :], masked[:, :, :], AX.X, ALU.add)))
                step_of(dve.tensor_copy(slots[:, :], slot_f[:, 0, :]))
                dve.wait_ge(dve_step, step_of(dve.tensor_copy(slot_i[:, 0, :], slot_f[:, 0, :])))
                step_of(dve.tensor_scalar(slot_i[:, 1, :], slot_i[:, 0, :], 7, None, ALU.logical_shift_right))
                dve.wait_ge(dve_step, step_of(dve.tensor_scalar(slot_i[:, 2, :], slot_i[:, 0, :], P - 1, None,
                                                                ALU.bitwise_and)))
                dve.wait_ge(dve_step, step_of(dve.tensor_copy(slot_f[:, 1:3, :], slot_i[:, 1:3, :])))

            def tile_experts():
                dve.wait_ge(dve_step, step_of(dve.tensor_tensor(
                    te[:, :, :], iota_f[0:1, 0:NTILES].unsqueeze(2).to_broadcast([1, NTILES, E]),
                    s8[0:1, 2, :].unsqueeze(1).to_broadcast([1, NTILES, E]), ALU.is_ge)))
                dve.wait_ge(dve_step, step_of(dve.tensor_reduce(te_f[:, :], te[:, :, :], AX.X, ALU.add)))
                dve.tensor_scalar(tile_expert[:, :], te_f[:, :], -1.0, None, ALU.add).then_inc(experts_ready, 1)

            def one_hots(part):
                for c in range(part * NT // 4, (part + 1) * NT // 4):
                    dve.tensor_scalar(oh_lo[:, c, :], iota_f[:, :], slot_f[:, 2, c:c + 1], None, ALU.is_equal)
                    ins = dve.tensor_scalar(oh_hi[:, c, 0:NTILES], iota_f[:, 0:NTILES], slot_f[:, 1, c:c + 1],
                                            token_f[:, c:c + 1], ALU.is_equal, ALU.mult)
                ins.then_inc(onehot_ready, 1)

            hidden_shared(1, 0)
            add_shared(0)
            running_sums()
            hidden_shared(1, 1)
            expert_starts()
            hidden_shared(1, 2)
            pair_slots()
            hidden_shared(1, 3)
            split_low(2)
            tile_experts()
            for b in (2, 3):
                for j in range(CB):
                    hidden_shared(b, j)
                    if j == 0:
                        add_shared(b - 1)
                    if j == CB - 1:
                        split_low(b + 1)
                    one_hots(CB * (b - 2) + j)
            with dve.Fori(4, B - 1) as b:
                for j in range(CB):
                    hidden_shared(b, j)
                    if j == 0:
                        add_shared(b - 1)
                split_low(b + 1)
            for j in range(CB):
                hidden_shared(B - 1, j)
                if j == 0:
                    add_shared(B - 2)
                    dve.wait_ge(ids_full, 1)
                    dve.tensor_copy(ids[:, :], ids_bank[:, 0:NTILES]).then_inc(ids_ready, 1)
            add_shared(B - 1)

            def hidden(t):
                dve.wait_ge(esilu_done, t + 1)
                dve.tensor_tensor(eh[:, :], egu_bank[:, I:2 * I], es[:, :], ALU.mult).then_inc(eh_ready, 1)

            def hidden_T(t):
                dve.wait_ge(hT_full, t + 1)
                dve.tensor_copy(ehT[:, :], hT_bank[:, 0:I]).then_inc(hT_ready, 1)

            def expert_out(t, k, uses):
                dve.wait_ge(ey_full, t + 1)
                if not (isinstance(uses, int) and uses == 0):
                    dve.wait_ge(yo_stored[k], 16 * uses)
                dve.tensor_copy(yo[:, k, :], ey_bank).then_inc(yo_ready, 1)

            def three_tiles(i, start=False):
                for k in range(3):
                    hidden(3 * i + k)
                    if k == 0 and not start:
                        expert_out(3 * i - 1, 2, i - 1)
                    elif k:
                        expert_out(3 * i + k - 1, k - 1, i)
                    hidden_T(3 * i + k)

            dve.wait_ge(dn_free, B)
            three_tiles(0, start=True)
            three_tiles(1)
            with dve.Fori(2, NTILES // 3) as i:
                three_tiles(i)
            expert_out(NTILES - 1, 2, NTILES // 3 - 1)

            def combine(i, k):
                t = 4 * i + k
                dve.wait_ge(y12_loaded[k], 32 * (i + 1))
                tile = T[:, :, :].rearrange("p b n -> p (b n)")[:, bass.ds(t * C, C)]
                return t, tile

            for i in range(NT // 4):
                for k in range(4):
                    t, tile = combine(i, k)
                    if i:
                        dve.wait_ge(out_stored[k], 16 * i)
                    dve.wait_ge(dve_step, step_of(dve.scalar_tensor_tensor(
                        fin[:, k, 0, :], y12[:, k, 0, :], w12[:, 0, t:t + 1], tile, ALU.mult, ALU.add)))
                    dve.scalar_tensor_tensor(fin[:, k, 1, :], y12[:, k, 1, :], w12[:, 1, t:t + 1], fin[:, k, 0, :],
                                             ALU.mult, ALU.add).then_inc(fin_ready, 1)

        @block.tensor
        def _(pe):
            def triple(out, parts, lhs, rhs):
                products = [(k, a, b) for k in parts for a, b in ((0, 0), (0, 1), (1, 0))]
                for m, (k, a, b) in enumerate(products):
                    ins = pe.matmul(out, lhs(k, a), rhs(k, b), start=m == 0, stop=m == len(products) - 1)
                return ins

            pe.wait_ge(chmean_ready, 1)
            pe.wait_ge(consts_done, NCONSTS)
            pe.matmul(PS[0][:, 0:n32], g_avg[:, :], small[:, 3, :], start=True, stop=True).then_inc(grpmean_ready, 1)
            pe.wait_ge(chvar_ready, 1)
            pe.matmul(PS[1][:, 0:n32], g_avg[:, :], small[:, 9, :], start=True, stop=True).then_inc(grpvar_ready, 1)
            pe.wait_ge(u_ready, 1)
            pe.transpose(PS[2][0:B * UP, 0:P], u, ident[:, :]).then_inc(uT_full, 1)
            UPS = B * UP
            with pe.Fori(0, ROUNDS) as i:
                pe.wait_ge(counts_ready, i + 1)
                pe.matmul(PS[3][0:UPS, 0:3], g_med[:, :], col[:, 8:11], start=True, stop=True).then_inc(counts_summed, 1)
            pe.wait_ge(med_in, 1)
            pe.transpose(PS[4][0:1, 0:UPS], col[:, 8:9], ident[0:UPS, 0:UPS]).then_inc(med_out, 1)
            pe.wait_ge(med_in, 2)
            pe.matmul(PS[4][0:UPS, 128:129], row[0:1, 2, :], ones[0:1, 0:1], start=True, stop=True).then_inc(med_out, 1)
            pe.wait_ge(med_in, 4)
            pe.transpose(PS[5][0:1, 0:UPS], col[:, 9:10], ident[0:UPS, 0:UPS])
            pe.transpose(PS[5][0:1, 128:128 + UPS], col[:, 10:11], ident[0:UPS, 0:UPS]).then_inc(med_out, 1)
            pe.wait_ge(med_in, 5)
            pe.matmul(PS[6][:, 0:B], ones[0:1, :], row[0:1, 7, 0:B], start=True, stop=True).then_inc(med_out, 1)

            def begin(part, item, s):
                k, used = ring(part, item, s)
                if not (isinstance(used, int) and used == 0):
                    pe.wait_ge(ring_free[k], used)
                return ring_bank[k], ring_full[k]

            def y_transposes(part, b, s):
                pe.wait_ge(y_ready, b + 1)
                for tt in range(TT):
                    bank, full = begin(part, f"YT{tt}", s)
                    for k in range(CB):
                        ins = pe.transpose(bank[:, k * P:(k + 1) * P], front[:, k * S + tt * P:k * S + (tt + 1) * P],
                                           ident[:, :])
                    ins.then_inc(full, 1)

            def transposes(part, name, src, s):
                for h in range(2):
                    bank, full = begin(part, f"{name}{h}", s)
                    for k in range(2):
                        for tt in range(TT):
                            at_c = tt * C + (2 * h + k) * P
                            ins = pe.transpose(bank[:, k * S + tt * P:k * S + (tt + 1) * P], src[:, at_c:at_c + P],
                                               ident[:, :])
                    ins.then_inc(full, 1)

            def wslice(t, j, k, lo_, hi_):
                return t[:, j, k * C + lo_:k * C + hi_]

            def heads_projection(part, item, s):
                j = "QK".index(item[0])
                bank, full = begin(part, item, s)
                for m in range(2):
                    lo_ = (2 * int(item[1]) + m) * P
                    ins = triple(bank[:, m * S:(m + 1) * S], range(CB),
                                 lambda k, a: wslice((w_h, w_l)[a], j, k, lo_, lo_ + P),
                                 lambda k, a: (xt_h, xt_l)[a][:, k, :])
                ins.then_inc(full, 1)

            def values_projection(part, s, tt):
                bank, full = begin(part, f"V{tt}", s)
                triple(bank, range(CB), lambda k, a: (xt_h, xt_l)[a][:, k, tt * P:(tt + 1) * P],
                       lambda k, a: wslice((w_h, w_l)[a], 2, k, 0, C)).then_inc(full, 1)

            def head_scores(b, p, first):
                if not (first and p < 2):
                    pe.wait_ge(tanh_done, 8 * b + p - 1)
                for h in (2 * p, 2 * p + 1):
                    bank, c, r = score_bank[2 * (p % 2) + h % 2], h // HC, D * (h % HC)
                    pe.matmul(bank[:, 0:S], kT[r:r + D, c, 0:P], qT[r:r + D, c, :], start=True, stop=True)
                    ins = pe.matmul(bank[:, S:S + P], kT[r:r + D, c, P:S], qT[r:r + D, c, P:S], start=True, stop=True)
                ins.then_inc(scores_full, 1)

            def head_values(b, c, first):
                pe.wait_ge(mask_done, 8 * b + 2 * c + 2)
                if not (first and c == 0):
                    pe.wait_ge(att_ready, 4 * b + c)
                for off, lhs in ((0, lambda h, tt: v[:, tt, h * D:(h + 1) * D]), (S, lambda h, tt: ones[:, 0:D])):
                    for tt in range(TT):
                        for j in range(HC):
                            h = HC * c + j
                            pr = probs[:, (h // 2) % 4, 384 * (h % 2):384 * (h % 2 + 1)]
                            ins = pe.matmul(od_bank[j * D:(j + 1) * D, off + tt * P:off + S], lhs(h, tt),
                                            pr[:, 0:S] if tt == 0 else pr[:, S:S + P], start=tt == 0, stop=tt == TT - 1,
                                            skip_group_check=True)
                ins.then_inc(pv_done, 1)

            def out_projection(part, b):
                pe.wait_ge(att_l_done, 4 * b + 4)
                for tt in range(TT):
                    bank, full = begin(part, f"OP{tt}", b)
                    triple(bank, range(CB), lambda k, a: (att_h, att_l)[a][:, k, tt * P:(tt + 1) * P],
                           lambda k, a: wslice((w_h, w_l)[a], 3, k, 0, C)).then_inc(full, 1)

            def gate_transposes(part, b, s):
                pe.wait_ge(x2_ready, b + 1)
                transposes(part, "X2T", x2, s)

            def gate_logits(part, s):
                bank, full = begin(part, "GT", s)
                pe.wait_ge(*emptied(part, "X2T0", s))
                pe.wait_ge(*emptied(part, "X2T1", s))
                for tt in range(TT):
                    for k in range(CB):
                        ins = pe.matmul(bank[:, tt * E:(tt + 1) * E], x2T[:, k * S + tt * P:k * S + (tt + 1) * P],
                                        gate_sb[:, k, :], start=k == 0, stop=k == CB - 1)
                ins.then_inc(full, 1)

            def front_transposes(part, b, s):
                pe.wait_ge(xn_ready, b + 1)
                transposes(part, "XN", front, s)

            def front_split(part, s):
                pe.wait_ge(*emptied(part, "XN0", s))
                pe.wait_ge(*emptied(part, "XN1", s))

            def step(part, b, has_front, has_back, has_next):
                first = isinstance(b, int) and b == 0
                head_scores(b, 0, first)
                head_scores(b, 1, first)
                if has_front:
                    front_transposes(part, b + 1, b)
                head_scores(b, 2, first)
                head_scores(b, 3, first)
                head_values(b, 0, first)
                if has_back:
                    gate_transposes(part, b - 1, b)
                head_scores(b, 4, first)
                if has_back:
                    gate_logits(part, b)
                if has_front:
                    front_split(part, b)
                    heads_projection(part, "Q0", b)
                head_scores(b, 5, first)
                head_values(b, 1, first)
                if has_front:
                    heads_projection(part, "K0", b)
                head_scores(b, 6, first)
                head_scores(b, 7, first)
                head_values(b, 2, first)
                if has_front:
                    heads_projection(part, "Q1", b)
                head_values(b, 3, first)
                if has_front:
                    heads_projection(part, "K1", b)
                    values_projection(part, b, 0)
                    values_projection(part, b, 1)
                if has_next:
                    y_transposes(part, b + 2, b)
                out_projection(part, b)

            y_transposes("lead", 0, 0)
            front_transposes("front", 0, 0)
            front_split("front", 0)
            pe.wait_ge(wlo_done, NW)
            for item in ("Q0", "K0", "Q1", "K1"):
                heads_projection("front", item, 0)
            values_projection("front", 0, 0)
            values_projection("front", 0, 1)
            y_transposes("front", 1, 0)
            for item in ("Q1", "K1", "V0", "V1", "Q0", "K0"):
                pe.wait_ge(*emptied("front", item, 0))
            pe.wait_ge(gate_loaded, 16)
            step("first", 0, True, False, True)
            with pe.Fori(1, B - 2) as b:
                step("mid", b, True, True, True)
            step("late", B - 2, True, True, False)
            pe.wait_ge(*emptied("late", "V1", B - 2))
            step("last", B - 1, False, True, False)


            def hidden_chunk(b, j, first):
                if not (first and j < 2):
                    pe.wait_ge(h_done, CB * b + j - 1)
                bank = gu_bank[j % 2]
                for g in range(2):
                    ins = triple(bank[:, g * S:(g + 1) * S], range(CB),
                                 lambda k, a: wslice((sw_h, sw_l)[a], g, k, j * P, (j + 1) * P),
                                 lambda k, a: (xb_h, xb_l)[a][:, k, :])
                ins.then_inc(gu_full, 1)

            def down_chunk(b, j, first):
                pe.wait_ge(hl_done, CB * b + j + 1)
                if j == 0 and not first:
                    pe.wait_ge(dn_free, b)
                for tt in range(TT):
                    for m, (a, c) in enumerate(((0, 0), (0, 1), (1, 0))):
                        ins = pe.matmul(dn_bank[tt], (hh, hl)[a][:, j, tt * P:(tt + 1) * P],
                                        wslice((sw_h, sw_l)[c], 2, j, 0, C), start=j == 0 and m == 0,
                                        stop=j == CB - 1 and m == 2)
                if j == CB - 1:
                    ins.then_inc(dn_full, 1)

            def shared(b):
                pe.wait_ge(xb_l_done, b + 1)
                hidden_chunk(b, 0, False)
                down_chunk(b - 1, CB - 1, False)
                for j in range(1, CB):
                    hidden_chunk(b, j, False)
                    down_chunk(b, j - 1, False)

            pe.wait_ge(xb_l_done, 1)
            pe.wait_ge(tanh_done, 8 * B)
            hidden_chunk(0, 0, True)
            hidden_chunk(0, 1, True)
            down_chunk(0, 0, True)
            gate_transposes("tail", B - 1, B)
            hidden_chunk(0, 2, True)
            gate_logits("tail", B)
            down_chunk(0, 1, True)
            hidden_chunk(0, 3, True)
            down_chunk(0, 2, True)

            pe.wait_ge(*emptied("tail", "GT", B))
            pe.wait_ge(chosen_ready, 1)
            rhs = chosen[:, :, :].rearrange("p t e -> p (t e)")
            pe.matmul(route_bank[:, 0:P], before[:, :], rhs, start=True, stop=True)
            pe.matmul(route_bank[:, P:2 * P], ones[:, :], rhs, start=True, stop=True).then_inc(prefix_full, 1)
            with pe.Fori(1, 4) as b:
                shared(b)
            pe.wait_ge(onehot_ready, 2 * CB)
            for c in range(2 * NT):
                ins = pe.matmul(ids_bank[:, 0:NTILES], oh_lo[:, c, :], oh_hi[:, c, 0:NTILES], start=c == 0,
                                stop=c == 2 * NT - 1)
            ins.then_inc(ids_full, 1)
            with pe.Fori(4, B) as b:
                shared(b)
            down_chunk(B - 1, CB - 1, False)

            def gather_T(t, k, turn):
                pe.wait_ge(xg_loaded[k], 16 * (turn + 1))
                for c in range(CB):
                    ins = pe.transpose(xT_bank[:, c * P:(c + 1) * P], xg[:, k, c * P:(c + 1) * P], ident[:, :])
                ins.then_inc(xT_full, 1)

            def expert_hidden(t, e):
                pe.wait_ge(xT_ready, t + 1)
                w = at(wgu_sb, e)
                for k in range(CB):
                    ins = pe.matmul(egu_bank, xgT[:, k * P:(k + 1) * P], w[:, k * 2 * I:(k + 1) * 2 * I],
                                    start=k == 0, stop=k == CB - 1)
                ins.then_inc(egu_full, 1)

            def hidden_T(t):
                pe.wait_ge(eh_ready, t + 1)
                for c in range(I // P):
                    ins = pe.transpose(hT_bank[:, c * P:(c + 1) * P], eh[:, c * P:(c + 1) * P], ident[:, :])
                ins.then_inc(hT_full, 1)

            def expert_down(t, e):
                pe.wait_ge(hT_ready, t + 1)
                if not (isinstance(t, int) and t == 0):
                    pe.wait_ge(yo_ready, t)
                w = at(wd_sb, e)
                for k in range(I // P):
                    ins = pe.matmul(ey_bank, ehT[:, k * P:(k + 1) * P], w[:, k * C:(k + 1) * C],
                                    start=k == 0, stop=k == I // P - 1)
                ins.then_inc(ey_full, 1)

            expert_reg = [pe.alloc_register(f"expert{k}") for k in range(3)]

            def load_expert(t, k):
                pe.reg_load(expert_reg[k], tile_expert[0:1, bass.ds(t, 1)])

            def expert_in(k):
                return pe.snap(expert_reg[k], min_val=0, max_val=E - 1)

            def three_tiles(i, start=False, end=False):
                for k in range(3):
                    t = 3 * i + k
                    expert_hidden(t, expert_in(k))
                    if not (end and k == 2):
                        load_expert(t + 1, (k + 1) % 3)
                        gather_T(t + 1, (k + 1) % 3, i + (k + 1) // 3)
                    if not (start and k == 0):
                        if start and k == 1:
                            pe.wait_ge(wd_loaded, 16 * E)
                        expert_down(t - 1, expert_in((k + 2) % 3))
                    hidden_T(t)

            pe.wait_ge(experts_ready, 1)
            pe.wait_ge(wgu_loaded, 16 * E)
            pe.wait_ge(dn_free, B)
            load_expert(0, 0)
            gather_T(0, 0, 0)
            three_tiles(0, start=True)
            with pe.Fori(1, NTILES // 3 - 1) as i:
                three_tiles(i)
            three_tiles(NTILES // 3 - 1, end=True)
            expert_down(NTILES - 1, expert_in(2))


def kernel(**inputs):
    import concourse.bacc as _bacc
    from concourse.bass_utils import run_bass_kernel_spmd as _run

    a = {k: np.asarray(v_) for k, v_ in inputs.items()}

    def by_rows(w):
        return w.reshape(-1, P, w.shape[-1]).transpose(1, 0, 2).reshape(P, -1)

    def channels(w):
        return w.reshape(CB, P, -1).transpose(1, 0, 2).reshape(P, -1)

    attn = [a[f"L1_attn_w_{n}"].T for n in "qkvo"]
    wgu = np.concatenate([a["L1_ffn_wg"], a["L1_ffn_wu"]], axis=2)
    arrays = {
        "x": a["x"].reshape(B, C, S),
        "params": np.concatenate([channels(a["L0_conv_cfc_w"]), channels(a["L0_conv_bn_w"]),
                                  channels(a["L0_conv_bn_b"])], axis=1),
        "wqkvo": np.stack([by_rows(w) for w in attn], axis=1),
        "gate": channels(a["L1_ffn_gate_w"].T).reshape(P, CB, E),
        "ws": np.stack([by_rows(a[f"L1_ffn_s{n}"]) for n in "gud"], axis=1),
        "wgu": np.stack([by_rows(w) for w in wgu], axis=1),
        "wd": np.stack([by_rows(w) for w in a["L1_ffn_wd"]], axis=1),
    }
    nc = _bacc.Bacc("TRN2", target_bir_lowering=False, num_devices=1)
    ins, args = {}, []
    for name, array in arrays.items():
        array = np.ascontiguousarray(array)
        ins[f"in_{name}"] = array
        args.append(nc.dram_tensor(f"in_{name}", array.shape, mybir.dt.from_np(array.dtype), kind="ExternalInput").ap())
    args.append(nc.dram_tensor("out_tokens", (B * S, C), fp32, kind="ExternalOutput").ap())
    layer_kernel(nc, *args)
    r = _run(nc, [ins], core_ids=[0])
    tokens = r.results[0]["out_tokens"]
    return np.ascontiguousarray(tokens.reshape(B, S, C).transpose(0, 2, 1)).reshape(B, C, 16, 16)
```

```python
from contextlib import ExitStack

import numpy as np
import concourse.bass as bass
from concourse import mybir

B, C, S = 8, 512, 256
NH, D = 16, 32
E, I = 8, 256
IS = 512
P = 128
CB = C // P
TT = S // P
NT = B * TT
GN_CH = C // 32
UK = 3
ACT_STATS = 3
UP = CB * UK
MED_N = C * UK
CNT = 17
ROUNDS = (7, 9)
RANGE = 128.0
NPAIR = NH // 2
HC = P // D
NTILES = (2 * B * S + E * (P - 1)) // P
TILE_COLS = NTILES + NTILES % 2
PAIRS = 4
BIG = 1e9
SOFTCAP = 30.0
EPS = 1e-5

fp32 = mybir.dt.float32
fp32r = mybir.dt.float32r
bf16 = mybir.dt.bfloat16
i32 = mybir.dt.int32
u32 = mybir.dt.uint32
ALU = mybir.AluOpType
ACT = mybir.ActivationFunctionType
AX = mybir.AxisListType

RING = 3
STEP = ["XN0", "XN1", "X2T0", "X2T1", "GT", "Q0", "K0", "Q1", "K1", "V0", "V1", "YT0", "YT1", "OP0", "OP1"]
GATE_ITEMS = ["X2T0", "X2T1", "GT"]
PARTS = {
    "lead": (1, ["YT0", "YT1"]),
    "front": (1, ["XN0", "XN1", "Q0", "K0", "Q1", "K1", "YT0", "YT1", "V0", "V1"]),
    "first": (1, [i for i in STEP if i not in GATE_ITEMS]),
    "mid": (B - 3, STEP),
    "late": (1, [i for i in STEP if i[:2] != "YT"]),
    "last": (1, GATE_ITEMS + ["OP0", "OP1"]),
    "tail": (1, GATE_ITEMS),
}


def ring(part, item, b):
    n = 0
    for name, (steps, items) in PARTS.items():
        if name == part:
            break
        n += steps * len(items)
    n += items.index(item)
    return n % RING, n // RING + ((b - 1) * (len(items) // RING) if part == "mid" else 0)


class Steps:

    def __init__(self):
        self.n = 0
        self.base = 0

    def up(self):
        self.n += 1
        return self.value()

    def value(self):
        return self.n + self.base

    def enter(self, turn, per):
        self.start, self.per = self.n, per
        self.base = turn * per

    def leave(self, turns):
        assert self.n - self.start == self.per, (self.n - self.start, self.per)
        self.n += (turns - 1) * self.per
        self.base = 0



def layer_kernel(nc, x, params, wqkvo, gate, ws, wgu, wd, out):
    ctx = ExitStack()
    with ctx:
        def sb(name, shape, dt=fp32, scope=ctx):
            return scope.enter_context(nc.sbuf_tensor(name, shape, dt))

        x2_rows = nc.dram_tensor("x2_rows", [B * S, C], fp32, kind="Internal").ap()
        x2_cols = nc.dram_tensor("x2_cols", [B * P, CB * S], fp32, kind="Internal").ap()

        ident = sb("ident", [P, P])
        ones = sb("ones", [P, P])
        before = sb("before", [P, P])
        iota_f = sb("iota_f", [P, P])
        token_f = sb("token_f", [P, 2 * NT])
        maxes = sb("maxes", [P, NT, 8])
        topi = sb("topi", [P, NT, 8])
        w12 = sb("w12", [P, 2, NT])
        ids = sb("ids", [P, NTILES], u32)
        dest = sb("dest", [P, NTILES], u32)
        slot_w = sb("slot_w", [P, NTILES])
        tile_expert = sb("tile_expert", [1, NTILES], u32)

        PROBS, SMALL, BATCH = 4 * 2 * 384, 1840, CB * S
        MAIN = PROBS + SMALL
        T_AT = MAIN + 10 * BATCH
        SW_AT = T_AT + B * BATCH
        W_AT = SW_AT + 3 * 2 * CB * C

        def area(name, start):
            scope = ExitStack()
            if start:
                sb(f"below_{name}", [P, start], fp32, scope)
            return scope

        scope = area("T", T_AT)
        T = sb("T", [P, B, BATCH], fp32, scope)
        sw = sb("sw", [P, 3, 2, CB * C], fp32r, scope)
        sw_h, sw_l = sw[:, :, 0, :], sw[:, :, 1, :]
        w_h = sb("w_h", [P, 4, CB * C], fp32r, scope)
        w_l = sb("w_l", [P, 4, CB * C], fp32r, scope)
        scope.close()

        scope = area("small", 0)
        probs = sb("probs", [P, 4, 2 * 384], fp32, scope)
        rden = sb("rden", [P, S], fp32, scope)
        att = sb("att", [P, S], fp32, scope)
        gate_sb = sb("gate_sb", [P, CB, D], fp32, scope)
        fold = sb("fold", [P, E], fp32, scope)
        lg = sb("lg", [P, TT * E], fp32, scope)
        top8 = sb("top8", [P, TT, 8], fp32, scope)
        idx8 = sb("idx8", [P, TT, 8], u32, scope)
        mean_var = sb("mean_var", [P, TT, 2], fp32, scope)
        bn6 = sb("bn6", [P, TT, 6], fp32, scope)
        var_eps = sb("var_eps", [P, TT], fp32, scope)
        rstd = sb("rstd", [P, TT], fp32, scope)
        powers = sb("powers", [P, TT], fp32, scope)
        prm = sb("prm", [P, CB * UK + 2 * CB], fp32, scope)
        coefA = sb("coefA", [P, B * CB], fp32, scope)
        coefB = sb("coefB", [P, B * CB], fp32, scope)
        col = sb("col", [B * UP, 24], fp32, scope)
        row = sb("row", [1, 8, B * UP], fp32, scope)
        g_avg = sb("g_avg", [P, P], fp32, scope)
        g_med = sb("g_med", [B * UP, B * UP], fp32, scope)
        scope.close()

        scope = area("attention", MAIN)
        qT = sb("qT", [P, CB, S], fp32, scope)
        kT = sb("kT", [P, CB, S], fp32, scope)
        xt_h = sb("xt_h", [P, CB, S], fp32r, scope)
        xt_l = sb("xt_l", [P, CB, S], fp32r, scope)
        front = sb("front", [P, CB * S], fp32, scope)
        x2T = sb("x2T", [P, CB * S], fp32, scope)
        x2 = sb("x2", [P, TT * C], fp32, scope)
        att_h = sb("att_h", [P, CB, S], fp32r, scope)
        att_l = sb("att_l", [P, CB, S], fp32r, scope)
        v = sb("v", [P, TT, C], fp32, scope)
        scope.close()

        qf = qT[:, :, :].rearrange("p c s -> p (c s)")
        kf = kT[:, :, :].rearrange("p c s -> p (c s)")
        vf = v[:, :, :].rearrange("p t c -> p (t c)")
        n32 = B * CB
        bst = qf[:, 0:6 * n32].rearrange("p (n k) -> p n k", k=6)
        chmax = qf[:, 6 * n32:7 * n32]
        small = kf[:, 0:16 * n32].rearrange("p (k n) -> p k n", n=n32)
        var2 = kf[:, 16 * n32:18 * n32]
        root = kf[:, 18 * n32:20 * n32]
        root2 = kf[:, 20 * n32:22 * n32]
        inv2 = kf[:, 22 * n32:24 * n32]
        u = vf[:, 0:B * UP]
        uw = vf[:, B * UP:4 * B * UP].rearrange("p (k n) -> p k n", k=3)
        uT = vf[0:B * UP, 4 * B * UP:4 * B * UP + P]
        junk = vf[0:B * UP, 4 * B * UP + P:4 * B * UP + 4 * P].rearrange("p (k n) -> p k n", k=3)
        counted = vf[0:B * UP, 4 * B * UP + 4 * P:4 * B * UP + 4 * P + 2].bitcast(bf16)[:, 0:3]
        sum_batch = vf[0:B * UP, 4 * B * UP + 4 * P + 2:4 * B * UP + 4 * P + 2 + B * UP // 2].bitcast(bf16)
        iota_i = qf[:, 512:512 + P].bitcast(i32)
        token_i = qf[:, 768:768 + 2 * NT].bitcast(i32)
        stage = probs[:, :, :].rearrange("p a n -> p (a n)").rearrange("p (k n) -> p k n", n=1024)

        scope = area("hidden", 0)
        hh = sb("hh", [P, CB, S], fp32r, scope)
        hl = sb("hl", [P, CB, S], fp32r, scope)
        sg = sb("sg", [P, 2, S], fp32, scope)
        hf = sb("hf", [P, 2, S], fp32, scope)
        xg = sb("xg", [P, 3, C], fp32, scope)
        scope.close()

        scope = area("tokens", MAIN)
        xb = sb("xb", [P, 2, 2, CB * S], fp32r, scope)
        xc = sb("xc", [P, CB * S], fp32, scope)
        picked = sb("picked", [P, 2, NT, E], fp32, scope)
        chosen = sb("chosen", [P, NT, E], fp32, scope)
        r4 = sb("r4", [P, 4, NT, E], fp32, scope)
        masked = sb("masked", [P, 2 * NT, E], fp32, scope)
        cmp = sb("cmp", [P, E, NT], fp32, scope)
        cmp8 = sb("cmp8", [P, 2, E, E], fp32, scope)
        s8 = sb("s8", [P, 4, E], fp32, scope)
        te = sb("te", [1, NTILES, E], fp32, scope)
        te_f = sb("te_f", [1, NTILES], fp32, scope)
        ex = sb("ex", [P, 4, NT], fp32, scope)
        slot_f = sb("slot_f", [P, 3, 2 * NT], fp32, scope)
        slot_i = sb("slot_i", [P, 3, 2 * NT], i32, scope)
        w12_h = sb("w12_h", [P, 2, NT], fp32r, scope)
        w12_l = sb("w12_l", [P, 2, NT], fp32r, scope)
        oh_row = sb("oh_row", [P, 2, PAIRS, P], fp32r, scope)
        oh_tile = sb("oh_tile", [P, 2, PAIRS, 3, TILE_COLS], fp32r, scope)
        spare_row = sb("spare_row", [P, 1], fp32, scope)
        unused = sb("unused", [P, NTILES], fp32, scope)
        scope.close()

        partial = rden

        def xb_part(parity, part):
            return xb[:, 1 - parity, part, :]

        scope = area("experts", MAIN)
        wgu_h = sb("wgu_h", [P, E, CB * 2 * I], fp32r, scope)
        scope.close()
        scope = area("down", SW_AT)
        wd_sb = sb("wd_sb", [P, E, (I // P) * C], fp32, scope)
        xgT_h = sb("xgT_h", [P, C], fp32r, scope)
        xgT_l = sb("xgT_l", [P, C], fp32r, scope)
        es = sb("es", [P, I], fp32, scope)
        eh = sb("eh", [P, I], fp32, scope)
        ehT = sb("ehT", [P, I], fp32, scope)
        yo = sb("yo", [P, 3, C], fp32, scope)
        scope.close()
        scope = area("gate_up", W_AT)
        wgu_l = sb("wgu_l", [P, E, CB * 2 * I], fp32r, scope)
        scope.close()

        scores = ctx.enter_context(nc.psum_tensor("scores", [P, 4, 512], fp32))
        PS = [scores[:, i, :] for i in range(4)]
        PS += [ctx.enter_context(nc.psum_tensor(f"PS{i}", [P, 512], fp32))[:, :] for i in range(4, 8)]
        score_bank, od_bank, ring_bank = PS[0:4], PS[4], PS[5:8]
        gu_bank, dn_bank = PS[0:2], PS[2:4]
        route_bank, ids_bank = PS[4], PS[5]
        egu_bank, ey_bank, xT_bank, hT_bank = PS[0], PS[2], PS[6], PS[7]

        def sem(name):
            return ctx.enter_context(nc.semaphore(name))

        wait_carrier = sem("wait_carrier")
        x_loaded = [sem(f"x_loaded{b}") for b in range(B)]
        prm_loaded, gate_loaded = sem("prm_loaded"), sem("gate_loaded")
        stage_loaded = [sem(f"stage_loaded{k}") for k in range(3)]
        whi_done, wlo_done = sem("whi_done"), sem("wlo_done")
        fills_done, consts_done = sem("fills_done"), sem("consts_done")
        dve_step, pool_step, act_step = sem("dve_step"), sem("pool_step"), sem("act_step")
        chmean_ready, grpmean_ready, chvar_ready, grpvar_ready = (
            sem("chmean_ready"), sem("grpmean_ready"), sem("chvar_ready"), sem("grpvar_ready"))
        act_sums = sem("act_sums")
        partial_full, partial_ready = sem("partial_full"), sem("partial_ready")
        var_ready, root_ready = sem("var_ready"), sem("root_ready")
        u_ready, uT_full = sem("u_ready"), sem("uT_full")
        counts_ready, counts_summed = sem("counts_ready"), sem("counts_summed")
        med_in, med_out = sem("med_in"), sem("med_out")
        z_ready, ez_ready = sem("z_ready"), sem("ez_ready")
        y_ready, t_ready = sem("y_ready"), sem("t_ready")
        var1_ready, rstd1_ready, var2_ready, rstd2_ready = (
            sem("var1_ready"), sem("rstd1_ready"), sem("var2_ready"), sem("rstd2_ready"))
        xn_ready, xt_h_done, x2_ready = sem("xn_ready"), sem("xt_h_done"), sem("x2_ready")
        ring_full = [sem(f"ring_full{k}") for k in range(RING)]
        ring_free = [sem(f"ring_free{k}") for k in range(RING)]
        scores_full, tanh_done, exp_done, mask_done = (
            sem("scores_full"), sem("tanh_done"), sem("exp_done"), sem("mask_done"))
        pv_done, att_ready, att_h_done, att_l_done = (
            sem("pv_done"), sem("att_ready"), sem("att_h_done"), sem("att_l_done"))
        x2_stored, x2T_stored = sem("x2_stored"), sem("x2T_stored")
        attention_over = sem("attention_over")
        wgu_loaded, wd_loaded = [sem(f"wgu_loaded{e}") for e in range(E)], sem("wd_loaded")
        wgu_h_done, wgu_l_pool, wgu_l_dve = sem("wgu_h_done"), sem("wgu_l_pool"), sem("wgu_l_dve")
        xc_loaded, xb_h_done, xb_l_done = sem("xc_loaded"), sem("xb_h_done"), sem("xb_l_done")
        gu_full, silu_done, h_done, hh_done, hl_done = (
            sem("gu_full"), sem("silu_done"), sem("h_done"), sem("hh_done"), sem("hl_done"))
        dn_full, dn_free = sem("dn_full"), sem("dn_free")
        chosen_ready, prefix_full, gap_exp = (
            sem("chosen_ready"), sem("prefix_full"), sem("gap_exp"))
        onehot_ready, onehot_used, ids_ready, experts_ready = (
            sem("onehot_ready"), sem("onehot_used"), sem("ids_ready"), sem("experts_ready"))
        xg_loaded = [sem(f"xg_loaded{k}") for k in range(3)]
        xT_h_done, xT_full, xT_ready, egu_full, esilu_done, eh_ready = (
            sem("xT_h_done"), sem("xT_full"), sem("xT_ready"), sem("egu_full"), sem("esilu_done"), sem("eh_ready"))
        hT_full, hT_ready, ey_full, yo_ready = (
            sem("hT_full"), sem("hT_ready"), sem("ey_full"), sem("yo_ready"))
        y_added = sem("y_added")
        residual_stored = [sem(f"residual_stored{b}") for b in range(B)]

        def at(t, b):
            return t[:, bass.ds(b, 1), :].rearrange("p a n -> p (a n)")

        def stand_alone(eng):
            eng.sem_inc(wait_carrier, 1)

        SPLITS = [(e, k) for e in (3, 4, 5, 6, 7, 2, 1, 0) for k in range(2)]
        HALF = CB * I
        DVE_SPLITS = (11, 12, 14, 15)

        def half_of(t, m):
            e, k = SPLITS[m]
            return t[:, e, k * HALF:(k + 1) * HALF]

        def tile_at(b, tt):
            return at(T, b)[:, tt * C:(tt + 1) * C]

        def filled(part, item, s):
            k, used = ring(part, item, s)
            return ring_full[k], used + 1

        def emptied(part, item, s):
            k, used = ring(part, item, s)
            return ring_free[k], used + 1

        NFILLS = 17
        NCONSTS = 8
        NW = 14

        def chunk_of(k, attn, shared):
            t, j = (attn, k) if k < 8 else (shared, k - 8)
            return t[:, j // 2, 1024 * (j % 2):1024 * (j % 2 + 1)]

        block = ctx.enter_context(nc.Block())

        @block.sync
        def _(sp):
            for b in range(B):
                sp.dma_start(at(T, b).rearrange("p (k s) -> p k s", k=CB),
                             x[b].rearrange("(k p) s -> p k s", p=P)).then_inc(x_loaded[b], 16)
            for k in range(NW):
                if k >= 3:
                    sp.wait_ge(wlo_done, k - 2)
                sp.dma_start(stage[:, k % 3, :], chunk_of(k, wqkvo, ws)).then_inc(stage_loaded[k % 3], 16)

            def store_x2(b):
                sp.wait_ge(x2_ready, b + 1)
                sp.dma_start(x2_rows[bass.ds(b * S, S), :].rearrange("(t p) c -> p t c", p=P),
                             x2[:, :].rearrange("p (t c) -> p t c", t=TT)).then_inc(x2_stored, 16)

            def store_x2T(part, b, s):
                sp.wait_ge(*emptied(part, "X2T0", s))
                stand_alone(sp)
                sp.wait_ge(*emptied(part, "X2T1", s))
                sp.dma_start(x2_cols[bass.ds(b * P, P), :], x2T[:, :]).then_inc(x2T_stored, 16)

            store_x2(0)
            with sp.Fori(1, B - 2) as b:
                store_x2T("mid", b - 1, b)
                store_x2(b)
            store_x2T("late", B - 3, B - 2)

            def load_tokens(b):
                if b:
                    sp.wait_ge(xc_loaded, 16 * b)
                    sp.wait_ge(xb_l_done, b)
                sp.wait_ge(x2T_stored, 16 * (b + 1))
                sp.dma_start(xc[:, :], x2_cols[b * P:(b + 1) * P, :]).then_inc(xc_loaded, 16)

            sp.wait_ge(*filled("late", "XN1", B - 2))
            load_tokens(0)
            store_x2(B - 2)
            store_x2T("last", B - 2, B - 1)
            load_tokens(1)
            store_x2(B - 1)
            store_x2T("tail", B - 1, B)

            sp.wait_ge(*filled("last", "OP1", B - 1))
            sp.wait_ge(x2T_stored, 16 * B)

            def load_gate_up(e):
                sp.dma_start(wgu_l[:, e, :].bitcast(fp32), at(wgu, e)).then_inc(wgu_loaded[e], 16)

            load_gate_up(3)

            def store_residual(b):
                sp.wait_ge(dn_free, b + 1)
                sp.dma_start(out[b * S:(b + 1) * S, :].rearrange("(t p) c -> p t c", p=P),
                             at(T, b).rearrange("p (t c) -> p t c", t=TT)).then_inc(residual_stored[b], 16)

            for b in range(1, B):
                if b > 1:
                    load_tokens(b)
                load_gate_up(SPLITS[2 * b][0])
                if b == 3:
                    sp.wait_ge(dn_free, 1)
                    sp.dma_start(out[B * S:B * S + P, :], at(T, 0)[:, 0:C]).then_inc(residual_stored[0], 16)
                if b >= 3:
                    store_residual(b - 3)
            store_residual(B - 3)
            store_residual(B - 2)
            sp.wait_ge(gu_full, CB * B)
            for e in range(E):
                sp.dma_start(at(wd_sb, e), at(wd, e)).then_inc(wd_loaded, 16)
            store_residual(B - 1)

        @block.gpsimd
        def _(pool):
            pool.wait_ge(fills_done, NFILLS)
            for t, base, pattern, mult, fill, op in (
                (ident[:, :], 0, [[-1, P]], 1, 1.0, ALU.not_equal),
                (before[:, :], -1, [[1, P]], -1, 0.0, ALU.is_ge),
                (g_avg[:, :].rearrange("p (a c) -> p a c", c=GN_CH), 0, [[-GN_CH, 8], [0, GN_CH]], 1, 0.0, ALU.is_ge),
                (g_med[:, :].rearrange("p (a c) -> p a c", c=UP), 0, [[-UP, B], [0, UP]], 1, 0.0, ALU.is_ge),
            ):
                pool.affine_select(out=t, in_=t, compare_op=op, fill=fill, base=base, pattern=pattern,
                                   channel_multiplier=mult).then_inc(consts_done, 1)
            pool.wait_ge(consts_done, 4)
            for t, base, pattern in (
                (g_avg[:, :].rearrange("p (a c) -> p a c", c=GN_CH), GN_CH - 1, [[GN_CH, 8], [0, GN_CH]]),
                (g_med[:, :].rearrange("p (a c) -> p a c", c=UP), UP - 1, [[UP, B], [0, UP]]),
            ):
                pool.affine_select(out=t, in_=t, compare_op=ALU.is_ge, fill=0.0, base=base, pattern=pattern,
                                   channel_multiplier=-1).then_inc(consts_done, 1)
            pool.iota(iota_i, pattern=[[1, P]], base=0, channel_multiplier=0).then_inc(consts_done, 1)
            pool.iota(token_i.rearrange("p (a t) -> p a t", a=2), pattern=[[0, 2], [P, NT]], base=0,
                      channel_multiplier=1).then_inc(consts_done, 1)

            for k in range(NW):
                pool.wait_ge(whi_done, k + 1)
                pool.tensor_tensor(chunk_of(k, w_l, sw_l), stage[:, k % 3, :],
                                   chunk_of(k, w_h, sw_h).bitcast(fp32), ALU.subtract).then_inc(wlo_done, 1)

            def rstd_of(var_ready, rstd_ready, b):
                pool.wait_ge(var_ready, b + 1)
                pool.tensor_tensor(rstd[:, :], var_eps[:, :], powers[:, 0:TT], ALU.pow).then_inc(rstd_ready, 1)

            def mask(b, p):
                pool.wait_ge(exp_done, 8 * b + p + 1)
                stand_alone(pool)
                for a in range(2):
                    t = probs[:, p % 4, :].rearrange("p (h q) -> p h q", h=2)[:, :, 256 * a:256 * a + P]
                    ins = pool.affine_select(out=t, in_=t, compare_op=ALU.is_ge, fill=0.0, base=0,
                                             pattern=[[0, 2], [1, P]], channel_multiplier=-1)
                ins.then_inc(mask_done, 1)

            def att_low(b, c):
                pool.wait_ge(att_h_done, 4 * b + c + 1)
                pool.tensor_tensor(att_l[:, c, :], att[:, :], att_h[:, c, :].bitcast(fp32),
                                   ALU.subtract).then_inc(att_l_done, 1)

            def hidden_low(b, j):
                pool.wait_ge(hh_done, CB * b + j + 1)
                pool.tensor_tensor(hl[:, j, :], hf[:, j % 2, :], hh[:, j, :].bitcast(fp32),
                                   ALU.subtract).then_inc(hl_done, 1)

            def step(b, has_next):
                for p in range(5):
                    mask(b, p)
                att_low(b, 0)
                mask(b, 5)
                mask(b, 6)
                att_low(b, 1)
                mask(b, 7)
                att_low(b, 2)
                att_low(b, 3)
                if has_next:
                    rstd_of(var1_ready, rstd1_ready, b + 2)
                if isinstance(b, int) and b == B - 1:
                    hidden_low(0, 0)
                    hidden_low(0, 1)
                rstd_of(var2_ready, rstd2_ready, b)

            rstd_of(var1_ready, rstd1_ready, 0)
            rstd_of(var1_ready, rstd1_ready, 1)
            step(0, True)
            with pool.Fori(1, B - 2) as b:
                step(b, True)
            step(B - 2, False)
            step(B - 1, False)

            def weight_low(m):
                pool.wait_ge(wgu_h_done, m + 1)
                t = half_of(wgu_l, m)
                pool.tensor_tensor(t, t.bitcast(fp32), half_of(wgu_h, m).bitcast(fp32),
                                   ALU.subtract).then_inc(wgu_l_pool, 1)

            def low_with_weights(b, splits, gathers=()):
                for j in range(CB):
                    hidden_low(b, j)
                    if j < len(splits):
                        weight_low(splits[j])
                    if j < len(gathers):
                        gather(gathers[j])

            hidden_low(0, 2)
            hidden_low(0, 3)
            with pool.Fori(1, 4) as b:
                for j in range(CB):
                    hidden_low(b, j)
            def gather(t):
                if t >= 3:
                    pool.wait_ge(xT_full, t - 2)
                pool.indirect_dma_start(xg[:, t % 3, :], None, x2_rows[:, :],
                                        bass.IndirectOffsetOnAxis(ids[:, t:t + 1], 0)).then_inc(xg_loaded[t % 3], 16)

            def scatter_add(t):
                if t == 0:
                    for b in range(B):
                        pool.wait_ge(residual_stored[b], 16 if b else 32)
                else:
                    pool.wait_ge(y_added, 16 * t)
                pool.wait_ge(yo_ready, t + 1)
                pool.indirect_dma_start(out[:, :], bass.IndirectOffsetOnAxis(dest[:, t:t + 1], 0), yo[:, t % 3, :],
                                        None, compute_op=ALU.add).then_inc(y_added, 16)

            low_with_weights(4, (0, 1, 2, 3))
            low_with_weights(5, (4, 5, 6, 7))
            pool.wait_ge(ids_ready, 2)
            low_with_weights(6, (), (0, 1, 2))
            low_with_weights(7, (8, 9, 10))
            weight_low(13)
            for t in range(3, NTILES):
                gather(t)
                if t >= 5:
                    scatter_add(t - 5)
            for t in range(NTILES - 5, NTILES):
                scatter_add(t)
            pool.wait_ge(y_added, 16 * NTILES)

        @block.scalar
        def _(act):
            act.dma_start(prm[:, :], params).then_inc(prm_loaded, 16)
            act.wait_ge(fills_done, NFILLS)
            act.dma_start(gate_sb[:, :, 0:E], gate).then_inc(gate_loaded, 16)
            cols = [(b, k, CB * b + k) for b in range(ACT_STATS) for k in range(CB)]
            na = CB * ACT_STATS
            unread = [t[:, S * k:S * (k + 1)] for t in (front, x2T, x2) for k in range(CB)]
            for b, k, c in cols:
                act.wait_ge(x_loaded[b], 16)
                ins = act.activation(unread[c], at(T, b)[:, k * S:(k + 1) * S], ACT.Copy,
                                     accum_out=small[:, 12, c:c + 1])
            ins.then_inc(act_sums, 1)
            act.wait_ge(act_sums, 1)
            act.activation(small[:, 13, 0:na], small[:, 12, 0:na], ACT.Copy, scale=-1.0 / S).then_inc(act_sums, 1)
            act.wait_ge(act_sums, 2)
            for b, k, c in cols:
                ins = act.activation(unread[c], at(T, b)[:, k * S:(k + 1) * S], ACT.Square,
                                     bias=small[:, 13, c:c + 1], accum_out=small[:, 5, c:c + 1])
            ins.then_inc(act_sums, 1)

            for k in range(NW):
                act.wait_ge(stage_loaded[k % 3], 16 * (k // 3 + 1))
                act.activation(chunk_of(k, w_h, sw_h), stage[:, k % 3, :], ACT.Copy).then_inc(whi_done, 1)
                if k == 2:
                    act.wait_ge(var_ready, 1)
                    act.activation(root, var2, ACT.Sqrt).then_inc(root_ready, 1)
            act.wait_ge(z_ready, 1)
            act.activation(small[:, 15, :], small[:, 14, :], ACT.Exp, scale=-1.0).then_inc(ez_ready, 1)

            def tokens(part, b, s):
                for tt in range(TT):
                    act.wait_ge(*filled(part, f"YT{tt}", s))
                    k, _ = ring(part, f"YT{tt}", s)
                    act.activation(tile_at(b, tt), ring_bank[k], ACT.Copy).then_inc(ring_free[k], 1)

            def xt_high(part, s):
                for h in range(2):
                    act.wait_ge(*filled(part, f"XN{h}", s))
                    k, _ = ring(part, f"XN{h}", s)
                    act.activation(xt_h[:, 2 * h:2 * h + 2, :].rearrange("p c s -> p (c s)"), ring_bank[k],
                                   ACT.Copy).then_inc(xt_h_done, 1)

            def values(part, s):
                for tt in range(TT):
                    act.wait_ge(*filled(part, f"V{tt}", s))
                    k, _ = ring(part, f"V{tt}", s)
                    act.activation(v[:, tt, :], ring_bank[k], ACT.Copy).then_inc(ring_free[k], 1)

            def soft(b, p, first=False):
                act.wait_ge(scores_full, 8 * b + p + 1)
                if not (first and p < 4):
                    act.wait_ge(pv_done, 4 * b + p // 2 - 1)
                act.activation(probs[:, p % 4, :].rearrange("p (h q) -> p h q", h=2),
                               scores[:, 2 * (p % 2):2 * (p % 2) + 2, 0:384], ACT.Tanh,
                               scale=1.0 / (np.sqrt(D) * SOFTCAP)).then_inc(tanh_done, 1)
                act.wait_ge(tanh_done, 8 * b + p + 1)
                act.activation(probs[:, p % 4, :], probs[:, p % 4, :], ACT.Exp, scale=SOFTCAP).then_inc(exp_done, 1)

            def att_high(b, c):
                act.wait_ge(att_ready, 4 * b + c + 1)
                act.activation(att_h[:, c, :], att[:, :], ACT.Copy).then_inc(att_h_done, 1)

            def x2_transposed(part, s):
                for h in range(2):
                    act.wait_ge(*filled(part, f"X2T{h}", s))
                    k, _ = ring(part, f"X2T{h}", s)
                    act.activation(x2T[:, 512 * h:512 * (h + 1)], ring_bank[k], ACT.Copy).then_inc(ring_free[k], 1)

            def step(part, b, has_front, has_back, has_next):
                first = isinstance(b, int) and b == 0
                if part == "last":
                    split_high(0, 0)
                soft(b, 0, first)
                soft(b, 1, first)
                if has_front:
                    xt_high(part, b)
                soft(b, 2, first)
                soft(b, 3, first)
                if has_back:
                    x2_transposed(part, b)
                soft(b, 4, first)
                att_high(b, 0)
                soft(b, 5, first)
                att_high(b, 1)
                soft(b, 6, first)
                soft(b, 7, first)
                att_high(b, 2)
                att_high(b, 3)
                if has_front:
                    values(part, b)
                if has_next:
                    tokens(part, b + 2, b)
                if has_back:
                    act.wait_ge(x2T_stored, 16 * b)

            def split_high(b, parity):
                act.wait_ge(xc_loaded, 16 * (b + 1))
                act.activation(xb_part(parity, 0), xc[:, :], ACT.Copy).then_inc(xb_h_done, 1)

            tokens("lead", 0, 0)
            xt_high("front", 0)
            tokens("front", 1, 0)
            values("front", 0)
            act.wait_ge(wlo_done, NW)
            step("first", 0, True, False, True)
            with act.Fori(1, B - 2) as b:
                step("mid", b, True, True, True)
            step("late", B - 2, True, True, False)
            step("last", B - 1, False, True, False)

            def gated_shared(b, j):
                act.wait_ge(gu_full, CB * b + j + 1)
                act.activation(sg[:, j % 2, :], gu_bank[j % 2][:, 0:S], ACT.Silu).then_inc(silu_done, 1)
                act.wait_ge(h_done, CB * b + j + 1)
                act.activation(hh[:, j, :], hf[:, j % 2, :], ACT.Copy).then_inc(hh_done, 1)

            gated_shared(0, 0)
            gated_shared(0, 1)
            gated_shared(0, 2)
            x2_transposed("tail", B)
            split_high(1, 1)
            gated_shared(0, 3)

            def weight_high(m):
                act.wait_ge(wgu_loaded[SPLITS[m][0]], 16)
                act.activation(half_of(wgu_h, m), half_of(wgu_l, m).bitcast(fp32), ACT.Copy).then_inc(wgu_h_done, 1)

            for b in range(1, B):
                for j in range(CB):
                    gated_shared(b, j)
                    if j == 1 and b + 1 < B:
                        split_high(b + 1, (b + 1) % 2)
                    if b == 1 and j == 0:
                        act.wait_ge(attention_over, 1)
                        act.activation(ex[:, 1, :], ex[:, 0, :], ACT.Exp).then_inc(gap_exp, 1)
                    if b == 4 and j == 0:
                        act.wait_ge(ids_ready, 2)
                    if b == 5 and j == 0:
                        act.wait_ge(residual_stored[0], 32)
                        act.wait_ge(residual_stored[1], 16)
                    if b == 5 and j == 2:
                        act.wait_ge(residual_stored[2], 16)
                        act.wait_ge(residual_stored[3], 16)
                    if b in (4, 5):
                        weight_high(CB * (b - 4) + j)
                    if b == 6 and j >= 2:
                        if j == 2:
                            act.wait_ge(residual_stored[4], 16)
                            act.wait_ge(residual_stored[5], 16)
                        weight_high(8 + j - 2)
                    if b == 7:
                        if j == 0:
                            act.wait_ge(xb_l_done, B)
                            weight_high(10)
                        if j < 3:
                            weight_high(11 + j)
            weight_high(14)
            weight_high(15)

            def x_transposed(t):
                act.wait_ge(xT_full, t + 1)
                act.activation(xgT_h[:, :], xT_bank, ACT.Copy).then_inc(xT_h_done, 1)

            def gated(t):
                act.wait_ge(egu_full, t + 1)
                act.activation(es[:, :], egu_bank[:, 0:I], ACT.Silu).then_inc(esilu_done, 1)

            act.wait_ge(dn_full, B)
            x_transposed(0)
            with act.Fori(0, NTILES - 1) as t:
                gated(t)
                x_transposed(t + 1)
            gated(NTILES - 1)

        @block.vector
        def _(dve):
            n = Steps()

            def fill(t, value):
                dve.memset(t, value).then_inc(fills_done, 1)

            fill(ident[:, :], 0.0)
            fill(before[:, :], 1.0)
            fill(g_avg[:, :], 1.0 / GN_CH)
            fill(g_med[:, :], 1.0)
            fill(ones[:, :], 1.0)
            fill(powers[:, :], -0.5)
            fill(gate_sb[:, :, :], 0.0)
            below, lo, lo_part = col[:, 0:1], col[:, 1:2], col[:, 2:3]
            thr, base, width, fourths = col[:, 3:6], col[:, 6:9], col[:, 11:14], col[:, 14:17]
            cnt, flags = col[:, CNT:CNT + 3], col[:, 20:23]
            for j in range(3):
                fill(thr[:, j:j + 1], -RANGE / 2 + (j + 1) * RANGE / 4)
                fill(base[:, j:j + 1], -RANGE / 2 + (j + 1) * RANGE / 16)
                fill(fourths[:, j:j + 1], ((j + 1) / 4 - 1) * RANGE / 4)
            fill(width, RANGE / 4)
            dve.wait_ge(fills_done, NFILLS)

            dve.wait_ge(consts_done, NCONSTS)
            dve.tensor_copy(sum_batch, g_med[:, :]).then_inc(dve_step, 1)
            dve.tensor_copy(iota_f[:, :], iota_i).then_inc(dve_step, 1)
            dve.tensor_copy(token_f[:, :], token_i).then_inc(dve_step, 1)
            dve.tensor_reduce(fold[:, :], ident[:, :].rearrange("p (k e) -> p e k", e=D)[:, 0:E, :], AX.X,
                              ALU.add).then_inc(dve_step, 1)
            n.n = 4

            for b in range(B):
                dve.wait_ge(x_loaded[b], 16)
                xb = at(T, b).rearrange("p (k s) -> p k s", k=CB)
                if b >= ACT_STATS:
                    for k in range(CB):
                        dve.bn_stats(bst[:, CB * b + k, :], xb[:, k, :])
                ins = dve.reduce_max(chmax[:, CB * b:CB * (b + 1)], xb, AX.X)
            ins.then_inc(dve_step, 1)
            dve.wait_ge(dve_step, n.up())

            def step_of(ins):
                ins.then_inc(dve_step, 1)
                return n.up()

            def K(k):
                return small[:, k, :]

            na = CB * ACT_STATS
            kb = [small[:, k, na:n32] for k in range(6)]
            mean_of, m2_of = bst[:, na:n32, 1:5:3], bst[:, na:n32, 2:6:3]
            step_of(dve.tensor_tensor(kb[0], mean_of[:, :, 0], mean_of[:, :, 1], ALU.add))
            step_of(dve.tensor_tensor(kb[1], mean_of[:, :, 0], mean_of[:, :, 1], ALU.subtract))
            dve.wait_ge(dve_step, step_of(dve.tensor_tensor(kb[2], m2_of[:, :, 0], m2_of[:, :, 1], ALU.add)))
            dve.wait_ge(act_sums, 2)
            step_of(dve.tensor_scalar(small[:, 3, 0:na], small[:, 13, 0:na], -1.0, None, ALU.mult))
            dve.tensor_scalar(kb[3], kb[0], 0.5, None, ALU.mult).then_inc(chmean_ready, 1)
            dve.wait_ge(dve_step, step_of(dve.tensor_tensor(kb[4], kb[1], kb[1], ALU.mult)))
            dve.wait_ge(dve_step, step_of(dve.scalar_tensor_tensor(
                kb[5], kb[4], S / 4.0, kb[2], ALU.mult, ALU.add)))
            dve.wait_ge(act_sums, 3)
            dve.wait_ge(grpmean_ready, 1)
            grp_mean = K(6)
            dve.wait_ge(dve_step, step_of(dve.tensor_copy(grp_mean, PS[0][:, 0:n32])))
            dve.wait_ge(dve_step, step_of(dve.tensor_tensor(K(7), K(3), grp_mean, ALU.subtract)))
            dve.wait_ge(dve_step, step_of(dve.tensor_tensor(K(8), K(7), K(7), ALU.mult)))
            dve.scalar_tensor_tensor(K(9), K(5), 1.0 / S, K(8), ALU.mult, ALU.add).then_inc(chvar_ready, 1)
            step_of(dve.tensor_scalar(var2[:, n32:2 * n32], K(5), 1.0 / (S - 1), 1e-30, ALU.mult, ALU.max))
            dve.wait_ge(grpvar_ready, 1)
            dve.tensor_scalar(var2[:, 0:n32], PS[1][:, 0:n32], EPS, None, ALU.add).then_inc(var_ready, 1)
            step_of(dve.tensor_tensor(K(10), chmax, grp_mean, ALU.subtract))
            dve.wait_ge(root_ready, 1)
            dve.wait_ge(dve_step, step_of(dve.reciprocal(inv2, root)))
            dve.wait_ge(dve_step, step_of(dve.tensor_tensor(root2, var2, inv2, ALU.mult)))
            dve.wait_ge(dve_step, step_of(dve.tensor_tensor(root2, root2, root, ALU.add)))
            dve.wait_ge(dve_step, step_of(dve.reciprocal(inv2[:, 0:n32], root2[:, 0:n32])))
            r = inv2[:, n32:2 * n32]
            dve.wait_ge(dve_step, step_of(dve.tensor_scalar(r, inv2[:, 0:n32], 2.0, None, ALU.mult)))
            u3 = u.rearrange("p (n k) -> p n k", k=UK)
            dve.tensor_tensor(u3[:, :, 0], K(7), r, ALU.mult)
            dve.tensor_tensor(u3[:, :, 1], K(10), r, ALU.mult)
            dve.scalar_tensor_tensor(u3[:, :, 2], root2[:, n32:2 * n32], 0.5, r, ALU.mult, ALU.mult).then_inc(u_ready, 1)

            dve.wait_ge(uT_full, 1)
            dve.wait_ge(dve_step, step_of(dve.tensor_copy(uT, PS[2][0:B * UP, 0:P])))
            def counts():
                for j in range(3):
                    ins = dve.tensor_scalar(junk[:, j, :], uT, thr[:, j:j + 1], 0.0, ALU.is_le, ALU.add,
                                            accum_out=counted[:, j:j + 1])
                    if j < 2:
                        step_of(ins)
                ins.then_inc(counts_ready, 1)

            def new_thresholds(i):
                dve.wait_ge(counts_summed, i + 1)
                dve.wait_ge(dve_step, step_of(dve.tensor_scalar(
                    flags, PS[3][0:B * UP, 0:3], MED_N / 2 - 0.5, 0.0, ALU.is_lt, ALU.add, accum_out=below)))
                dve.wait_ge(dve_step, step_of(dve.scalar_tensor_tensor(
                    thr, width, below, base, ALU.mult, ALU.add)))

            def new_base():
                dve.wait_ge(dve_step, step_of(dve.tensor_scalar(col[:, 11:17], col[:, 11:17], 0.25, None, ALU.mult)))
                dve.wait_ge(dve_step, step_of(dve.tensor_scalar(base, fourths, thr[:, 0:1], None, ALU.add)))

            def narrow(i):
                new_thresholds(i)
                counts()
                new_base()

            def find_lo(dst):
                dve.wait_ge(dve_step, step_of(dve.tensor_tensor(dst, thr[:, 0:1], width[:, 0:1], ALU.subtract)))

            counts()
            first_rounds, rounds = ROUNDS[0], ROUNDS[0] + ROUNDS[1]
            with dve.Fori(0, (first_rounds - 1) // 3) as i:
                n.enter(i, 18)
                for k in range(3):
                    narrow(3 * i + k)
                n.leave((first_rounds - 1) // 3)
            new_thresholds(first_rounds - 1)
            new_base()
            find_lo(lo_part)
            step_of(dve.tensor_scalar(uT, uT, lo_part, None, ALU.subtract))
            dve.wait_ge(dve_step, step_of(dve.tensor_scalar(col[:, 3:9], col[:, 3:9], lo_part, None, ALU.subtract)))
            counts()
            with dve.Fori(0, (rounds - 1 - first_rounds) // 4) as i:
                n.enter(i, 24)
                for k in range(4):
                    narrow(first_rounds + 4 * i + k)
                n.leave((rounds - 1 - first_rounds) // 4)
            new_thresholds(rounds - 1)
            new_base()
            find_lo(lo)

            def least(dst, bound):
                dve.wait_ge(dve_step, step_of(dve.tensor_scalar(junk[:, 0, :], uT, bound, BIG, ALU.is_le, ALU.mult)))
                dve.wait_ge(dve_step, step_of(dve.tensor_tensor(junk[:, 1, :], junk[:, 0, :], uT, ALU.add)))
                return dve.tensor_reduce(dst, junk[:, 1, :], AX.X, ALU.min)

            def of_batch(k):
                return row[0:1, k, :].rearrange("p (b n) -> p b n", b=B)

            least(cnt[:, 0:1], lo).then_inc(med_in, 1)
            dve.wait_ge(med_out, 1)
            dve.wait_ge(dve_step, step_of(dve.tensor_reduce(
                row[0:1, 1, 0:B], PS[4][0:1, 0:B * UP].rearrange("p (b n) -> p b n", b=B), AX.X, ALU.min)))
            dve.tensor_copy(of_batch(2), row[0:1, 1, 0:B].unsqueeze(2).to_broadcast([1, B, UP])).then_inc(med_in, 1)
            dve.wait_ge(med_out, 2)
            dve.wait_ge(dve_step, step_of(dve.tensor_copy(thr[:, 0:1], PS[4][0:B * UP, 128:129])))
            dve.tensor_scalar(junk[:, 2, :], uT, thr[:, 0:1], 0.0, ALU.is_le, ALU.add,
                              accum_out=cnt[:, 1:2]).then_inc(med_in, 1)
            least(cnt[:, 2:3], thr[:, 0:1]).then_inc(med_in, 1)
            dve.wait_ge(med_out, 3)
            step_of(dve.tensor_reduce(row[0:1, 3, 0:B], PS[5][0:1, 0:B * UP].rearrange("p (b n) -> p b n", b=B),
                                      AX.X, ALU.add))
            dve.wait_ge(dve_step, step_of(dve.tensor_reduce(
                row[0:1, 4, 0:B], PS[5][0:1, 128:128 + B * UP].rearrange("p (b n) -> p b n", b=B), AX.X, ALU.min)))
            dve.wait_ge(dve_step, step_of(dve.tensor_scalar(
                row[0:1, 5, 0:B], row[0:1, 3, 0:B], MED_N / 2 + 0.5, BIG, ALU.is_lt, ALU.mult)))
            dve.wait_ge(dve_step, step_of(dve.tensor_tensor(
                row[0:1, 5, 0:B], row[0:1, 5, 0:B], row[0:1, 1, 0:B], ALU.add)))
            dve.wait_ge(dve_step, step_of(dve.tensor_tensor(
                row[0:1, 6, 0:B], row[0:1, 5, 0:B], row[0:1, 4, 0:B], ALU.min)))
            dve.wait_ge(dve_step, step_of(dve.tensor_tensor(
                row[0:1, 6, 0:B], row[0:1, 6, 0:B], row[0:1, 1, 0:B], ALU.add)))
            dve.scalar_tensor_tensor(row[0:1, 7, 0:B], row[0:1, 6, 0:B], 0.5,
                                     PS[4][0:1, 256:256 + B * UP].rearrange("p (b n) -> p b n", b=B)[:, :, 0],
                                     ALU.mult, ALU.add).then_inc(med_in, 1)

            dve.wait_ge(med_out, 4)
            dve.wait_ge(prm_loaded, 16)
            by_b = "p (b n) -> p b n"
            dve.wait_ge(dve_step, step_of(dve.tensor_tensor(
                uw[:, 0, :].rearrange(by_b, b=B), u.rearrange(by_b, b=B),
                PS[6][:, 0:B].unsqueeze(2).to_broadcast([P, B, UP]), ALU.subtract)))
            dve.wait_ge(dve_step, step_of(dve.tensor_tensor(uw[:, 1, :], uw[:, 0, :], uw[:, 0, :], ALU.mult)))
            dve.wait_ge(dve_step, step_of(dve.tensor_tensor(uw[:, 2, :], uw[:, 1, :], uw[:, 0, :], ALU.mult)))
            dve.wait_ge(dve_step, step_of(dve.tensor_tensor(
                uw[:, 0, :].rearrange(by_b, b=B), uw[:, 2, :].rearrange(by_b, b=B),
                prm[:, 0:UP].unsqueeze(1).to_broadcast([P, B, UP]), ALU.mult)))
            dve.wait_ge(dve_step, step_of(dve.tensor_reduce(
                K(11), uw[:, 0, :].rearrange("p (n k) -> p n k", k=UK), AX.X, ALU.add)))
            bn_scale = float(1.0 / np.sqrt(np.float32(1.0) + np.float32(EPS)))
            dve.wait_ge(dve_step, step_of(dve.scalar_tensor_tensor(
                K(12).rearrange(by_b, b=B), K(11).rearrange(by_b, b=B), bn_scale,
                prm[:, UP:UP + CB].unsqueeze(1).to_broadcast([P, B, CB]), ALU.mult, ALU.mult)))
            dve.tensor_tensor(K(14).rearrange(by_b, b=B), K(12).rearrange(by_b, b=B),
                              prm[:, UP + CB:UP + 2 * CB].unsqueeze(1).to_broadcast([P, B, CB]),
                              ALU.add).then_inc(z_ready, 1)
            dve.wait_ge(ez_ready, 1)
            dve.wait_ge(dve_step, step_of(dve.tensor_scalar(K(0), K(15), 1.0, None, ALU.add)))
            dve.wait_ge(dve_step, step_of(dve.reciprocal(K(1), K(0))))
            dve.wait_ge(dve_step, step_of(dve.tensor_tensor(K(2), K(1), r, ALU.mult)))
            step_of(dve.tensor_scalar(coefA[:, :], K(2), 1.0, None, ALU.add))
            dve.wait_ge(dve_step, step_of(dve.scalar_tensor_tensor(
                coefB[:, :], grp_mean, -1.0, K(2), ALU.mult, ALU.mult)))
            dve.wait_ge(dve_step, n.value())

            def affine(b):
                xb = at(T, b).rearrange("p (k s) -> p k s", k=CB)
                ab, bb = coefA[:, bass.ds(b * CB, CB)], coefB[:, bass.ds(b * CB, CB)]
                for k in range(CB):
                    ins = dve.tensor_scalar(front[:, k * S:(k + 1) * S], xb[:, k, :], ab[:, k:k + 1], bb[:, k:k + 1],
                                            ALU.mult, ALU.add)
                ins.then_inc(y_ready, 1)

            def layernorm(dst, b, var_ready, rstd_ready):
                stand_alone(dve)
                for tt in range(TT):
                    step_of(dve.bn_stats(bn6[:, tt, :], tile_at(b, tt)))
                dve.wait_ge(dve_step, n.value())
                stand_alone(dve)
                for tt in range(TT):
                    step_of(dve.bn_aggr(mean_var[:, tt, :], bn6[:, tt, :]))
                dve.wait_ge(dve_step, n.value())
                dve.tensor_scalar(var_eps[:, :], mean_var[:, :, 1], EPS, None, ALU.add).then_inc(var_ready, 1)
                dve.wait_ge(rstd_ready, b + 1)
                for tt in range(TT):
                    ins = dve.tensor_scalar(dst[:, tt * C:(tt + 1) * C], tile_at(b, tt), mean_var[:, tt, 0:1],
                                            rstd[:, tt:tt + 1], ALU.subtract, ALU.mult)
                return ins

            def first_norm(part, b, s):
                for tt in range(TT):
                    dve.wait_ge(*emptied(part, f"YT{tt}", s))
                layernorm(front, b, var1_ready, rstd1_ready).then_inc(xn_ready, 1)

            def xt_low(part, b, s):
                for h in range(2):
                    dve.wait_ge(xt_h_done, 2 * b + h + 1)
                    k, _ = ring(part, f"XN{h}", s)
                    dve.tensor_tensor(xt_l[:, 2 * h:2 * h + 2, :].rearrange("p c s -> p (c s)"), ring_bank[k],
                                      xt_h[:, 2 * h:2 * h + 2, :].rearrange("p c s -> p (c s)").bitcast(fp32),
                                      ALU.subtract).then_inc(ring_free[k], 1)

            def project_out(part, item, s):
                dve.wait_ge(*filled(part, item, s))
                k, _ = ring(part, item, s)
                h = int(item[1])
                dst = (qT if item[0] == "Q" else kT)[:, 2 * h:2 * h + 2, :].rearrange("p c s -> p (c s)")
                dve.tensor_copy(dst, ring_bank[k]).then_inc(ring_free[k], 1)

            def normalise(b, c, first=False):
                dve.wait_ge(pv_done, 4 * b + c + 1)
                dve.wait_ge(dve_step, step_of(dve.reciprocal(rden[:, :], od_bank[:, S:2 * S])))
                if not first:
                    dve.wait_ge(att_l_done, 4 * b + c)
                dve.tensor_tensor(att[:, :], od_bank[:, 0:S], rden[:, :], ALU.mult).then_inc(att_ready, 1)

            def partial_out(part, b, s):
                dve.wait_ge(partial_full, b + 1)
                stand_alone(dve)
                dve.wait_ge(att_ready, 4 * s if part == "tail" else 4 * s + 1)
                k, _ = ring(part, "GT", s)
                dve.tensor_copy(partial[:, :], ring_bank[k][:, 0:S]).then_inc(partial_ready, 1)

            def gate_top(part, b, s):
                dve.wait_ge(*filled(part, "GT", s))
                k, _ = ring(part, "GT", s)
                dve.tensor_copy(lg[:, :], ring_bank[k][:, S:S + TT * E]).then_inc(ring_free[k], 1)
                dve.wait_ge(*emptied(part, "GT", s))
                stand_alone(dve)
                for tt in range(TT):
                    step_of(dve.max(top8[:, tt, :], lg[:, tt * E:(tt + 1) * E]))
                dve.wait_ge(dve_step, n.value())
                stand_alone(dve)
                for tt in range(TT):
                    step_of(dve.max_index(idx8[:, tt, :], top8[:, tt, :], lg[:, tt * E:(tt + 1) * E]))
                dve.wait_ge(dve_step, n.value())
                step_of(dve.tensor_copy(maxes[:, bass.ds(b * TT, TT), :], top8[:, :, :]))
                dve.wait_ge(dve_step, step_of(dve.tensor_copy(topi[:, bass.ds(b * TT, TT), :], idx8[:, :, :])))

            def second(part, b, s, first=False):
                for tt in range(TT):
                    dve.wait_ge(*filled(part, f"OP{tt}", s))
                    k, _ = ring(part, f"OP{tt}", s)
                    dve.tensor_tensor(tile_at(b, tt), ring_bank[k], tile_at(b, tt),
                                      ALU.add).then_inc(ring_free[k], 1)
                for tt in range(TT):
                    dve.wait_ge(*emptied(part, f"OP{tt}", s))
                if not first:
                    dve.wait_ge(x2_stored, 16 * b)
                layernorm(x2, b, var2_ready, rstd2_ready).then_inc(x2_ready, 1)

            def hidden_shared(b, j, first=False):
                dve.wait_ge(silu_done, CB * b + j + 1)
                if not (first and j < 2):
                    dve.wait_ge(hl_done, CB * b + j - 1)
                dve.tensor_tensor(hf[:, j % 2, :], gu_bank[j % 2][:, S:2 * S], sg[:, j % 2, :],
                                  ALU.mult).then_inc(h_done, 1)

            def split_low(b, parity):
                dve.wait_ge(xb_h_done, b + 1)
                dve.tensor_tensor(xb_part(parity, 1), xc[:, :], xb_part(parity, 0).bitcast(fp32),
                                  ALU.subtract).then_inc(xb_l_done, 1)

            def step(part, b, has_front, has_back, has_next):
                first = isinstance(b, int) and b == 0
                if has_front:
                    xt_low(part, b + 1, b)
                normalise(b, 0, first)
                if has_back:
                    partial_out(part, b - 1, b)
                if has_front:
                    project_out(part, "Q0", b)
                if has_back:
                    gate_top(part, b - 1, b)
                normalise(b, 1)
                if has_front:
                    project_out(part, "K0", b)
                if not (has_front or has_next):
                    split_low(0, 0)
                if has_next:
                    affine(b + 2)
                normalise(b, 2)
                if has_front:
                    project_out(part, "Q1", b)
                normalise(b, 3)
                if not (has_front or has_next):
                    hidden_shared(0, 0, True)
                    hidden_shared(0, 1, True)
                if has_front:
                    project_out(part, "K1", b)
                if has_next:
                    first_norm(part, b + 2, b)
                second(part, b, b, first)

            affine(0)
            first_norm("lead", 0, 0)
            xt_low("front", 0, 0)
            affine(1)
            for item in ("Q0", "K0", "Q1", "K1"):
                project_out("front", item, 0)
            first_norm("front", 1, 0)
            step("first", 0, True, False, True)
            with dve.Fori(1, B - 2) as b:
                n.enter(b - 1, 18)
                step("mid", b, True, True, True)
                n.leave(B - 3)
            step("late", B - 2, True, True, False)
            step("last", B - 1, False, True, False)

            def add_shared(b):
                dve.wait_ge(dn_full, b + 1)
                for tt in range(TT):
                    ins = dve.tensor_tensor(tile_at(b, tt), dn_bank[tt], tile_at(b, tt), ALU.add)
                ins.then_inc(dn_free, 1)

            hidden_shared(0, 2)
            split_low(1, 1)
            hidden_shared(0, 3)
            partial_out("tail", B - 1, B)
            gate_top("tail", B - 1, B)
            dve.wait_ge(x2_stored, 16 * B)
            dve.wait_ge(x2T_stored, 16 * B)
            dve.tensor_tensor(ex[:, 0, :], maxes[:, :, 1], maxes[:, :, 0], ALU.subtract).then_inc(attention_over, 1)

            for j in range(2):
                step_of(dve.tensor_tensor(
                    picked[:, j, :, :], iota_f[:, 0:E].unsqueeze(1).to_broadcast([P, NT, E]),
                    topi[:, :, j:j + 1].to_broadcast([P, NT, E]), ALU.is_equal))
            dve.wait_ge(dve_step, n.value())
            dve.tensor_tensor(chosen[:, :, :], picked[:, 0, :, :], picked[:, 1, :, :],
                              ALU.add).then_inc(chosen_ready, 1)
            R = [r4[:, k, :, :] for k in range(4)]
            prefix = route_bank[:, 0:P].rearrange("p (t e) -> p t e", e=E)
            total, running = R[3], R[1]

            def pair_weights():
                dve.wait_ge(gap_exp, 1)
                dve.wait_ge(dve_step, step_of(dve.tensor_scalar(ex[:, 2, :], ex[:, 1, :], 1.0, None, ALU.add)))
                dve.wait_ge(dve_step, step_of(dve.reciprocal(w12[:, 0, :], ex[:, 2, :])))
                dve.wait_ge(dve_step, step_of(dve.tensor_tensor(w12[:, 1, :], w12[:, 0, :], ex[:, 1, :], ALU.mult)))
                dve.wait_ge(dve_step, step_of(dve.tensor_copy(w12_h[:, :, :], w12[:, :, :])))
                step_of(dve.tensor_tensor(w12_l[:, :, :], w12[:, :, :], w12_h[:, :, :].bitcast(fp32), ALU.subtract))

            def running_sums():
                dve.wait_ge(prefix_full, 1)
                step_of(dve.tensor_copy(total, route_bank[:, P:2 * P].rearrange("p (t e) -> p t e", e=E)))
                dve.wait_ge(dve_step, n.value())
                src = total
                for k, d in enumerate((1, 2, 4, 8)):
                    dst = R[k % 2]
                    step_of(dve.tensor_copy(dst[:, 0:d, :], src[:, 0:d, :]))
                    step_of(dve.tensor_tensor(dst[:, d:NT, :], src[:, d:NT, :], src[:, 0:NT - d, :], ALU.add))
                    dve.wait_ge(dve_step, n.value())
                    src = dst

            def expert_starts():
                dve.wait_ge(dve_step, step_of(dve.tensor_tensor(R[0], running, total, ALU.subtract)))
                dve.wait_ge(dve_step, step_of(dve.tensor_tensor(R[2], prefix, R[0], ALU.add)))
                dve.wait_ge(dve_step, step_of(dve.tensor_scalar(s8[:, 0, :], running[:, NT - 1, :], 1.0 / P, None, ALU.mult)))
                dve.wait_ge(dve_step, step_of(dve.tensor_tensor(
                    cmp[:, :, :], s8[:, 0, :].unsqueeze(2).to_broadcast([P, E, NT]),
                    iota_f[:, 0:NT].unsqueeze(1).to_broadcast([P, E, NT]), ALU.is_gt)))
                step_of(dve.tensor_reduce(s8[:, 1, :], cmp[:, :, :], AX.X, ALU.add))
                dve.wait_ge(dve_step, step_of(dve.tensor_tensor(
                    cmp8[:, 0, :, :], iota_f[:, 0:E].unsqueeze(1).to_broadcast([P, E, E]),
                    iota_f[:, 0:E].unsqueeze(2).to_broadcast([P, E, E]), ALU.is_lt)))
                dve.wait_ge(dve_step, step_of(dve.tensor_tensor(
                    cmp8[:, 1, :, :], cmp8[:, 0, :, :], s8[:, 1, :].unsqueeze(1).to_broadcast([P, E, E]), ALU.mult)))
                dve.wait_ge(dve_step, step_of(dve.tensor_reduce(s8[:, 2, :], cmp8[:, 1, :, :], AX.X, ALU.add)))
                dve.wait_ge(dve_step, step_of(dve.tensor_scalar(s8[:, 3, :], s8[:, 2, :], float(P), None, ALU.mult)))

            def pair_slots():
                dve.wait_ge(dve_step, step_of(dve.tensor_tensor(
                    R[0], R[2], s8[:, 3, :].unsqueeze(1).to_broadcast([P, NT, E]), ALU.add)))
                for j in range(2):
                    step_of(dve.tensor_tensor(masked[:, j * NT:(j + 1) * NT, :], picked[:, j, :, :], R[0], ALU.mult))
                dve.wait_ge(dve_step, n.value())
                dve.wait_ge(dve_step, step_of(dve.tensor_reduce(slot_f[:, 0, :], masked[:, :, :], AX.X, ALU.add)))
                dve.wait_ge(dve_step, step_of(dve.tensor_copy(slot_i[:, 0, :], slot_f[:, 0, :])))
                step_of(dve.tensor_scalar(slot_i[:, 1, :], slot_i[:, 0, :], 7, None, ALU.logical_shift_right))
                dve.wait_ge(dve_step, step_of(dve.tensor_scalar(slot_i[:, 2, :], slot_i[:, 0, :], P - 1, None,
                                                                ALU.bitwise_and)))
                dve.wait_ge(dve_step, step_of(dve.tensor_copy(slot_f[:, 1:3, :], slot_i[:, 1:3, :])))

            def tile_experts():
                dve.wait_ge(dve_step, step_of(dve.tensor_tensor(
                    te[:, :, :], iota_f[0:1, 0:NTILES].unsqueeze(2).to_broadcast([1, NTILES, E]),
                    s8[0:1, 2, :].unsqueeze(1).to_broadcast([1, NTILES, E]), ALU.is_ge)))
                dve.wait_ge(dve_step, step_of(dve.tensor_reduce(te_f[:, :], te[:, :, :], AX.X, ALU.add)))
                dve.tensor_scalar(tile_expert[:, :], te_f[:, :], -1.0, None, ALU.add).then_inc(experts_ready, 1)

            def one_hots(g):
                if g >= 2:
                    dve.wait_ge(onehot_used, g - 1)
                for k in range(PAIRS):
                    c = PAIRS * g + k
                    j, t = c // NT, c % NT
                    row_of, tile_of = slot_f[:, 2, c:c + 1], slot_f[:, 1, c:c + 1]
                    dve.tensor_scalar(oh_row[:, g % 2, k, :], iota_f[:, :], row_of, None, ALU.is_equal)
                    for m, value in enumerate((token_f[:, c:c + 1], w12_h[:, j, t:t + 1].bitcast(fp32),
                                               w12_l[:, j, t:t + 1].bitcast(fp32))):
                        ins = dve.tensor_scalar(oh_tile[:, g % 2, k, m, :], iota_f[:, 0:TILE_COLS], tile_of, value,
                                                ALU.is_equal, ALU.mult)
                ins.then_inc(onehot_ready, 1)

            def slots_out():
                by_tile = ids_bank[:, 0:3 * TILE_COLS].rearrange("p (m t) -> p m t", m=3)[:, :, 0:NTILES]
                step_of(dve.tensor_scalar(spare_row[:, :], token_f[:, 0:1], float(B * S), None, ALU.add))
                dve.wait_ge(onehot_used, 2 * NT // PAIRS)
                dve.wait_ge(dve_step, step_of(dve.tensor_copy(slot_w[:, :], by_tile[:, 1, :])))
                dve.wait_ge(dve_step, step_of(dve.tensor_tensor(slot_w[:, :], by_tile[:, 2, :], slot_w[:, :], ALU.add)))
                dve.wait_ge(dve_step, step_of(dve.tensor_scalar(
                    unused[:, :], slot_w[:, :], 0.0, spare_row[:, 0:1], ALU.is_equal, ALU.mult)))
                dve.tensor_tensor(dest[:, :], by_tile[:, 0, :], unused[:, :], ALU.max).then_inc(ids_ready, 1)
                dve.tensor_copy(ids[:, :], by_tile[:, 0, :]).then_inc(ids_ready, 1)

            hidden_shared(1, 0)
            add_shared(0)
            pair_weights()
            hidden_shared(1, 1)
            running_sums()
            hidden_shared(1, 2)
            split_low(2, 0)
            expert_starts()
            hidden_shared(1, 3)
            pair_slots()
            one_hots(0)
            for b, groups in ((2, (1, 2, 3, 4)), (3, (5, 6, 7))):
                for j in range(CB):
                    hidden_shared(b, j)
                    if j == 0:
                        add_shared(b - 1)
                    if j == 2:
                        split_low(b + 1, (b + 1) % 2)
                    if j < len(groups):
                        one_hots(groups[j])
            tile_experts()
            slots_out()

            def shared(b, parity, has_next=True):
                hidden_shared(b, 0)
                add_shared(b - 1)
                hidden_shared(b, 1)
                if not has_next:
                    weight_low(DVE_SPLITS[0])
                hidden_shared(b, 2)
                if has_next:
                    split_low(b + 1, 1 - parity)
                else:
                    weight_low(DVE_SPLITS[1])
                hidden_shared(b, 3)

            def weight_low(m):
                dve.wait_ge(wgu_h_done, m + 1)
                t = half_of(wgu_l, m)
                dve.tensor_tensor(t, t.bitcast(fp32), half_of(wgu_h, m).bitcast(fp32),
                                  ALU.subtract).then_inc(wgu_l_dve, 1)

            for b in range(4, B):
                shared(b, b % 2, b + 1 < B)
            for m in DVE_SPLITS[2:]:
                weight_low(m)

            def hidden(t):
                dve.wait_ge(esilu_done, t + 1)
                dve.tensor_tensor(eh[:, :], egu_bank[:, I:2 * I], es[:, :], ALU.mult).then_inc(eh_ready, 1)

            def hidden_T(t):
                dve.wait_ge(hT_full, t + 1)
                dve.tensor_copy(ehT[:, :], hT_bank[:, 0:I]).then_inc(hT_ready, 1)

            def x_low(t):
                dve.wait_ge(xT_h_done, t + 1)
                dve.tensor_tensor(xgT_l[:, :], xT_bank, xgT_h[:, :].bitcast(fp32), ALU.subtract).then_inc(xT_ready, 1)

            def expert_out(t, k, uses):
                dve.wait_ge(ey_full, t + 1)
                if not (isinstance(uses, int) and uses == 0):
                    dve.wait_ge(y_added, 16 * (t - 2))
                dve.tensor_scalar(yo[:, k, :], ey_bank, slot_w[:, bass.ds(t, 1)], None, ALU.mult).then_inc(yo_ready, 1)

            def three_tiles(i, start=False, end=False):
                for k in range(3):
                    hidden(3 * i + k)
                    if not (end and k == 2):
                        x_low(3 * i + k + 1)
                    if k == 0 and not start:
                        expert_out(3 * i - 1, 2, i - 1)
                    elif k:
                        expert_out(3 * i + k - 1, k - 1, i)
                    hidden_T(3 * i + k)

            x_low(0)
            add_shared(B - 1)
            three_tiles(0, start=True)
            three_tiles(1)
            with dve.Fori(2, NTILES // 3 - 1) as i:
                three_tiles(i)
            three_tiles(NTILES // 3 - 1, end=True)
            expert_out(NTILES - 1, 2, NTILES // 3 - 1)

        @block.tensor
        def _(pe):
            def triple(out, parts, lhs, rhs):
                products = [(k, a, b) for k in parts for a, b in ((0, 0), (0, 1), (1, 0))]
                for m, (k, a, b) in enumerate(products):
                    ins = pe.matmul(out, lhs(k, a), rhs(k, b), start=m == 0, stop=m == len(products) - 1)
                return ins

            pe.wait_ge(chmean_ready, 1)
            pe.wait_ge(consts_done, NCONSTS)
            pe.matmul(PS[0][:, 0:n32], g_avg[:, :], small[:, 3, :], start=True, stop=True).then_inc(grpmean_ready, 1)
            pe.wait_ge(chvar_ready, 1)
            pe.matmul(PS[1][:, 0:n32], g_avg[:, :], small[:, 9, :], start=True, stop=True).then_inc(grpvar_ready, 1)
            pe.wait_ge(u_ready, 1)
            pe.transpose(PS[2][0:B * UP, 0:P], u, ident[:, :]).then_inc(uT_full, 1)
            UPS = B * UP
            with pe.Fori(0, ROUNDS[0] + ROUNDS[1]) as i:
                pe.wait_ge(counts_ready, i + 1)
                pe.matmul(PS[3][0:UPS, 0:3], sum_batch, counted, start=True, stop=True).then_inc(counts_summed, 1)
            pe.wait_ge(med_in, 1)
            pe.transpose(PS[4][0:1, 256:256 + UPS], col[:, 2:3], ident[0:UPS, 0:UPS])
            pe.transpose(PS[4][0:1, 0:UPS], col[:, CNT:CNT + 1], ident[0:UPS, 0:UPS]).then_inc(med_out, 1)
            pe.wait_ge(med_in, 2)
            pe.matmul(PS[4][0:UPS, 128:129], row[0:1, 2, :], ones[0:1, 0:1], start=True, stop=True).then_inc(med_out, 1)
            pe.wait_ge(med_in, 4)
            pe.transpose(PS[5][0:1, 0:UPS], col[:, CNT + 1:CNT + 2], ident[0:UPS, 0:UPS])
            pe.transpose(PS[5][0:1, 128:128 + UPS], col[:, CNT + 2:CNT + 3], ident[0:UPS, 0:UPS]).then_inc(med_out, 1)
            pe.wait_ge(med_in, 5)
            pe.matmul(PS[6][:, 0:B], ones[0:1, :], row[0:1, 7, 0:B], start=True, stop=True).then_inc(med_out, 1)

            def begin(part, item, s):
                k, used = ring(part, item, s)
                if not (isinstance(used, int) and used == 0):
                    pe.wait_ge(ring_free[k], used)
                return ring_bank[k], ring_full[k]

            def y_transposes(part, b, s):
                pe.wait_ge(y_ready, b + 1)
                for tt in range(TT):
                    bank, full = begin(part, f"YT{tt}", s)
                    for k in range(CB):
                        ins = pe.transpose(bank[:, k * P:(k + 1) * P], front[:, k * S + tt * P:k * S + (tt + 1) * P],
                                           ident[:, :])
                    ins.then_inc(full, 1)

            def transposes(part, name, src, s):
                for h in range(2):
                    bank, full = begin(part, f"{name}{h}", s)
                    for k in range(2):
                        for tt in range(TT):
                            at_c = tt * C + (2 * h + k) * P
                            ins = pe.transpose(bank[:, k * S + tt * P:k * S + (tt + 1) * P], src[:, at_c:at_c + P],
                                               ident[:, :])
                    ins.then_inc(full, 1)

            def wslice(t, j, k, lo_, hi_):
                return t[:, j, k * C + lo_:k * C + hi_]

            def heads_projection(part, item, s):
                j = "QK".index(item[0])
                bank, full = begin(part, item, s)
                for m in range(2):
                    lo_ = (2 * int(item[1]) + m) * P
                    ins = triple(bank[:, m * S:(m + 1) * S], range(CB),
                                 lambda k, a: wslice((w_h, w_l)[a], j, k, lo_, lo_ + P),
                                 lambda k, a: (xt_h, xt_l)[a][:, k, :])
                ins.then_inc(full, 1)

            def values_projection(part, s, tt):
                bank, full = begin(part, f"V{tt}", s)
                triple(bank, range(CB), lambda k, a: (xt_h, xt_l)[a][:, k, tt * P:(tt + 1) * P],
                       lambda k, a: wslice((w_h, w_l)[a], 2, k, 0, C)).then_inc(full, 1)

            def head_scores(b, p, first):
                if not (first and p < 2):
                    pe.wait_ge(tanh_done, 8 * b + p - 1)
                for tt in range(TT):
                    for h in (2 * p, 2 * p + 1):
                        bank, c, r = score_bank[2 * (p % 2) + h % 2], h // HC, D * (h % HC)
                        ins = pe.matmul(bank[:, tt * S:S + tt * P], kT[r:r + D, c, tt * P:(tt + 1) * P],
                                        qT[r:r + D, c, tt * P:S], start=True, stop=True)
                ins.then_inc(scores_full, 1)

            def head_values(b, c, first):
                pe.wait_ge(mask_done, 8 * b + 2 * c + 2)
                if not (first and c == 0):
                    pe.wait_ge(att_ready, 4 * b + c)
                for off, lhs in ((0, lambda h, tt: v[:, tt, h * D:(h + 1) * D]), (S, lambda h, tt: ones[:, 0:D])):
                    for tt in range(TT):
                        for j in range(HC):
                            h = HC * c + j
                            pr = probs[:, (h // 2) % 4, 384 * (h % 2):384 * (h % 2 + 1)]
                            ins = pe.matmul(od_bank[j * D:(j + 1) * D, off + tt * P:off + S], lhs(h, tt),
                                            pr[:, 0:S] if tt == 0 else pr[:, S:S + P], start=tt == 0, stop=tt == TT - 1,
                                            skip_group_check=True)
                ins.then_inc(pv_done, 1)

            def out_projection(part, b):
                pe.wait_ge(att_l_done, 4 * b + 4)
                for tt in range(TT):
                    bank, full = begin(part, f"OP{tt}", b)
                    triple(bank, range(CB), lambda k, a: (att_h, att_l)[a][:, k, tt * P:(tt + 1) * P],
                           lambda k, a: wslice((w_h, w_l)[a], 3, k, 0, C)).then_inc(full, 1)

            def gate_transposes(part, b, s):
                pe.wait_ge(x2_ready, b + 1)
                transposes(part, "X2T", x2, s)

            def gate_partial(part, s):
                begin(part, "GT", s)
                pe.wait_ge(*emptied(part, "X2T0", s))
                pe.wait_ge(*emptied(part, "X2T1", s))
                k, _ = ring(part, "GT", s)
                for c in range(CB):
                    ins = pe.matmul(ring_bank[k][c * D:(c + 1) * D, 0:S], gate_sb[:, c, :], x2T[:, c * S:(c + 1) * S],
                                    start=True, stop=True, skip_group_check=True)
                ins.then_inc(partial_full, 1)

            def gate_logits(part, b, s):
                pe.wait_ge(partial_ready, b + 1)
                k, _ = ring(part, "GT", s)
                for tt in range(TT):
                    ins = pe.matmul(ring_bank[k][:, S + tt * E:S + (tt + 1) * E], partial[:, tt * P:(tt + 1) * P],
                                    fold[:, :], start=True, stop=True)
                ins.then_inc(ring_full[k], 1)

            def front_transposes(part, b, s):
                pe.wait_ge(xn_ready, b + 1)
                transposes(part, "XN", front, s)

            def front_split(part, s):
                pe.wait_ge(*emptied(part, "XN0", s))
                pe.wait_ge(*emptied(part, "XN1", s))

            def hidden_chunk(b, j, first, parity):
                if not (first and j < 2):
                    pe.wait_ge(h_done, CB * b + j - 1)
                bank = gu_bank[j % 2]
                for g in range(2):
                    ins = triple(bank[:, g * S:(g + 1) * S], range(CB),
                                 lambda k, a: wslice((sw_h, sw_l)[a], g, k, j * P, (j + 1) * P),
                                 lambda k, a: xb_part(parity, a)[:, k * S:(k + 1) * S])
                ins.then_inc(gu_full, 1)

            def step(part, b, has_front, has_back, has_next):
                first = isinstance(b, int) and b == 0
                head_scores(b, 0, first)
                head_scores(b, 1, first)
                if has_front:
                    front_transposes(part, b + 1, b)
                head_scores(b, 2, first)
                head_scores(b, 3, first)
                if first:
                    pe.wait_ge(*emptied("front", "V0", 0))
                    pe.wait_ge(*emptied("front", "V1", 0))
                head_values(b, 0, first)
                if has_back:
                    gate_transposes(part, b - 1, b)
                head_scores(b, 4, first)
                if has_back:
                    gate_partial(part, b)
                if has_front:
                    front_split(part, b)
                    heads_projection(part, "Q0", b)
                if has_back and has_front:
                    gate_logits(part, b - 1, b)
                head_scores(b, 5, first)
                if has_back and not has_front:
                    gate_logits(part, b - 1, b)
                head_values(b, 1, first)
                if has_front:
                    heads_projection(part, "K0", b)
                head_scores(b, 6, first)
                head_scores(b, 7, first)
                head_values(b, 2, first)
                if has_front:
                    heads_projection(part, "Q1", b)
                if part == "last":
                    pe.wait_ge(tanh_done, 8 * b + 7)
                    pe.wait_ge(xb_l_done, 1)
                    hidden_chunk(0, 0, True, 0)
                head_values(b, 3, first)
                if part == "last":
                    hidden_chunk(0, 1, True, 0)
                if has_front:
                    heads_projection(part, "K1", b)
                    values_projection(part, b, 0)
                    values_projection(part, b, 1)
                if has_next:
                    y_transposes(part, b + 2, b)
                out_projection(part, b)

            y_transposes("lead", 0, 0)
            front_transposes("front", 0, 0)
            front_split("front", 0)
            pe.wait_ge(wlo_done, NW)
            for item in ("Q0", "K0", "Q1", "K1"):
                heads_projection("front", item, 0)
            y_transposes("front", 1, 0)
            values_projection("front", 0, 0)
            values_projection("front", 0, 1)
            for item in ("Q0", "K0", "Q1", "K1"):
                pe.wait_ge(*emptied("front", item, 0))
            pe.wait_ge(gate_loaded, 16)
            step("first", 0, True, False, True)
            with pe.Fori(1, B - 2) as b:
                step("mid", b, True, True, True)
            step("late", B - 2, True, True, False)
            pe.wait_ge(*emptied("late", "V1", B - 2))
            step("last", B - 1, False, True, False)


            def down_chunk(b, j, first):
                pe.wait_ge(hl_done, CB * b + j + 1)
                if j == 0 and not first:
                    pe.wait_ge(dn_free, b)
                for tt in range(TT):
                    for m, (a, c) in enumerate(((0, 0), (0, 1), (1, 0))):
                        ins = pe.matmul(dn_bank[tt], (hh, hl)[a][:, j, tt * P:(tt + 1) * P],
                                        wslice((sw_h, sw_l)[c], 2, j, 0, C), start=j == 0 and m == 0,
                                        stop=j == CB - 1 and m == 2)
                if j == CB - 1:
                    ins.then_inc(dn_full, 1)

            def shared(b, parity, groups=()):
                pe.wait_ge(xb_l_done, b + 1)
                for j in range(CB):
                    hidden_chunk(b, j, False, parity)
                    if j == 0:
                        down_chunk(b - 1, CB - 1, False)
                    else:
                        down_chunk(b, j - 1, False)
                    if isinstance(b, int) and b == 1 and j == 0:
                        prefixes()
                    if j < len(groups):
                        place(groups[j])

            def gather_T(t, k, turn):
                pe.wait_ge(xg_loaded[k], 16 * (turn + 1))
                for c in range(CB):
                    ins = pe.transpose(xT_bank[:, c * P:(c + 1) * P], xg[:, k, c * P:(c + 1) * P], ident[:, :])
                ins.then_inc(xT_full, 1)

            def place(g):
                pe.wait_ge(onehot_ready, g + 1)
                for k in range(PAIRS):
                    ins = pe.matmul(ids_bank[:, 0:3 * TILE_COLS], oh_row[:, g % 2, k, :],
                                    oh_tile[:, g % 2, k, :, :], start=g == 0 and k == 0,
                                    stop=g == 2 * NT // PAIRS - 1 and k == PAIRS - 1)
                ins.then_inc(onehot_used, 1)

            pe.wait_ge(tanh_done, 8 * B)
            down_chunk(0, 0, True)
            hidden_chunk(0, 2, True, 0)
            down_chunk(0, 1, True)
            gate_transposes("tail", B - 1, B)
            hidden_chunk(0, 3, True, 0)
            gate_partial("tail", B)
            down_chunk(0, 2, True)
            gate_logits("tail", B - 1, B)

            def prefixes():
                pe.wait_ge(*emptied("tail", "GT", B))
                pe.wait_ge(chosen_ready, 1)
                rhs = chosen[:, :, :].rearrange("p t e -> p (t e)")
                pe.matmul(route_bank[:, 0:P], before[:, :], rhs, start=True, stop=True)
                pe.matmul(route_bank[:, P:2 * P], ones[:, :], rhs, start=True, stop=True).then_inc(prefix_full, 1)

            shared(1, 1)
            shared(2, 0, (0, 1, 2, 3))
            shared(3, 1, (4, 5, 6, 7))
            with pe.Fori(2, B // 2) as i:
                shared(2 * i, 0)
                shared(2 * i + 1, 1)
            gather_T(0, 0, 0)
            down_chunk(B - 1, CB - 1, False)

            def expert_hidden(t, e):
                pe.wait_ge(xT_ready, t + 1)
                w = at(wgu_h, e), at(wgu_l, e)
                triple(egu_bank, range(CB), lambda k, a: (xgT_h, xgT_l)[a][:, k * P:(k + 1) * P],
                       lambda k, a: w[a][:, k * 2 * I:(k + 1) * 2 * I]).then_inc(egu_full, 1)

            def hidden_T(t):
                pe.wait_ge(eh_ready, t + 1)
                for c in range(I // P):
                    ins = pe.transpose(hT_bank[:, c * P:(c + 1) * P], eh[:, c * P:(c + 1) * P], ident[:, :])
                ins.then_inc(hT_full, 1)

            def expert_down(t, e):
                pe.wait_ge(hT_ready, t + 1)
                if not (isinstance(t, int) and t == 0):
                    pe.wait_ge(yo_ready, t)
                w = at(wd_sb, e)
                for k in range(I // P):
                    ins = pe.matmul(ey_bank, ehT[:, k * P:(k + 1) * P], w[:, k * C:(k + 1) * C],
                                    start=k == 0, stop=k == I // P - 1)
                ins.then_inc(ey_full, 1)

            expert_reg = [pe.alloc_register(f"expert{k}") for k in range(3)]

            def load_expert(t, k):
                pe.reg_load(expert_reg[k], tile_expert[0:1, bass.ds(t, 1)])

            def expert_in(k):
                return pe.snap(expert_reg[k], min_val=0, max_val=E - 1)

            def three_tiles(i, start=False, end=False):
                for k in range(3):
                    t = 3 * i + k
                    expert_hidden(t, expert_in(k))
                    if not (end and k == 2):
                        load_expert(t + 1, (k + 1) % 3)
                        gather_T(t + 1, (k + 1) % 3, i + (k + 1) // 3)
                    if not (start and k == 0):
                        if start and k == 1:
                            pe.wait_ge(wd_loaded, 16 * E)
                            pe.wait_ge(dn_free, B)
                        expert_down(t - 1, expert_in((k + 2) % 3))
                    hidden_T(t)

            pe.wait_ge(experts_ready, 1)
            pe.wait_ge(wgu_l_pool, 2 * E - len(DVE_SPLITS))
            pe.wait_ge(wgu_l_dve, len(DVE_SPLITS))
            load_expert(0, 0)
            three_tiles(0, start=True)
            with pe.Fori(1, NTILES // 3 - 1) as i:
                three_tiles(i)
            three_tiles(NTILES // 3 - 1, end=True)
            expert_down(NTILES - 1, expert_in(2))


def kernel(**inputs):
    import concourse.bacc as _bacc
    from concourse.bass_utils import run_bass_kernel_spmd as _run

    a = {k: np.asarray(v_) for k, v_ in inputs.items()}

    def by_rows(w):
        return w.reshape(-1, P, w.shape[-1]).transpose(1, 0, 2).reshape(P, -1)

    def channels(w):
        return w.reshape(CB, P, -1).transpose(1, 0, 2).reshape(P, -1)

    attn = [a[f"L1_attn_w_{n}"].T for n in "qkvo"]
    wgu = np.concatenate([a["L1_ffn_wg"], a["L1_ffn_wu"]], axis=2)
    arrays = {
        "x": a["x"].reshape(B, C, S),
        "params": np.concatenate([channels(a["L0_conv_cfc_w"]), channels(a["L0_conv_bn_w"]),
                                  channels(a["L0_conv_bn_b"])], axis=1),
        "wqkvo": np.stack([by_rows(w) for w in attn], axis=1),
        "gate": channels(a["L1_ffn_gate_w"].T).reshape(P, CB, E),
        "ws": np.stack([by_rows(a[f"L1_ffn_s{n}"]) for n in "gud"], axis=1),
        "wgu": np.stack([by_rows(w) for w in wgu], axis=1),
        "wd": np.stack([by_rows(w) for w in a["L1_ffn_wd"]], axis=1),
    }
    nc = _bacc.Bacc("TRN2", target_bir_lowering=False, num_devices=1)
    ins, args = {}, []
    for name, array in arrays.items():
        array = np.ascontiguousarray(array)
        ins[f"in_{name}"] = array
        args.append(nc.dram_tensor(f"in_{name}", array.shape, mybir.dt.from_np(array.dtype), kind="ExternalInput").ap())
    args.append(nc.dram_tensor("out_tokens", (B * S + P, C), fp32, kind="ExternalOutput").ap())
    layer_kernel(nc, *args)
    r = _run(nc, [ins], core_ids=[0])
    tokens = r.results[0]["out_tokens"][:B * S]
    return np.ascontiguousarray(tokens.reshape(B, S, C).transpose(0, 2, 1)).reshape(B, C, 16, 16)
```
